# Optimizing a Trainium2 kernel written in Bass

```python
import numpy as np
import jax
import jax.numpy as jnp

def _softmax(x, axis=-1):
    return jax.nn.softmax(x, axis=axis)

def _gelu(x):
    return jax.nn.gelu(x, approximate=True)

def _silu(x):
    return jax.nn.silu(x)

def _sigmoid(x):
    return jax.nn.sigmoid(x)

def _layernorm(x, axis=-1, eps=1e-05):
    m = jnp.mean(x, axis=axis, keepdims=True)
    v = jnp.var(x, axis=axis, keepdims=True)
    return (x - m) / jnp.sqrt(v + eps)

def _scatter_add(tgt, idx, src, axis=0):
    return tgt.at[idx].add(src)

def _segment_sum(src, seg, n):
    return jax.ops.segment_sum(src, seg, n)
kernel_name = 'mk_seq_postln_d2_jaxref_r8_db498f'

def setup_inputs(seed: int=0):
    np.random.seed(seed)
    _w = jnp.asarray

    def _L0_attn_setup():
        import jax, jax.numpy as jnp
        import numpy as np
        import math
        HIDDEN = 256
        NUM_HEADS = 16
        HEAD_SIZE = HIDDEN // NUM_HEADS
        BATCH = 2
        SEQ = 256
        key = jax.random.key(seed)
        k_x, k_wq, k_bq, k_wo, k_bo = jax.random.split(key, 5)
        scale_in = 1.0 / math.sqrt(HIDDEN)
        return {'x': jax.random.normal(k_x, (BATCH, SEQ, HIDDEN), dtype=jnp.float32), 'Wqkv': jax.random.normal(k_wq, (HIDDEN, 3 * HIDDEN), dtype=jnp.float32) * scale_in, 'bqkv': jax.random.normal(k_bq, (3 * HIDDEN,), dtype=jnp.float32) * 0.01, 'Wo': jax.random.normal(k_wo, (HIDDEN, HIDDEN), dtype=jnp.float32) * scale_in, 'bo': jax.random.normal(k_bo, (HIDDEN,), dtype=jnp.float32) * 0.01}
    _L0_attn_in = _L0_attn_setup()

    def _L0_ffn_setup():
        import jax, jax.numpy as jnp
        import numpy as np

        def _sparsify_2to4(h):
            B, S, I = h.shape
            g = h.reshape(B, S, I // 4, 4)
            a = jnp.abs(g)
            _, idx = jax.lax.top_k(a, 2)
            pos = jnp.arange(4)
            mask = (pos == idx[..., 0:1]) | (pos == idx[..., 1:2])
            return (g * mask.astype(g.dtype)).reshape(B, S, I)
        key = jax.random.key(seed)
        k1, k2, k3, k4 = jax.random.split(key, 4)
        B, S, H, I = (4, 256, 256, 1024)
        x = jax.random.normal(k1, (B, S, H), dtype=jnp.float32)
        w_gate = jax.random.normal(k2, (H, I), dtype=jnp.float32) / np.sqrt(H)
        w_up = jax.random.normal(k3, (H, I), dtype=jnp.float32) / np.sqrt(H)
        w_down = jax.random.normal(k4, (I, H), dtype=jnp.float32) / np.sqrt(I)
        return {'x': x, 'w_gate': w_gate, 'w_up': w_up, 'w_down': w_down}
    _L0_ffn_in = _L0_ffn_setup()

    def _L1_attn_setup():
        import jax, jax.numpy as jnp
        import numpy as np
        D_MODEL = 256
        D_INNER = 2 * D_MODEL
        D_STATE = 16
        D_CONV = 4
        DT_RANK = D_MODEL // 16
        BATCH, SEQLEN = (2, 128)

        def _mamba_forward(hidden_states, in_proj_w, conv_w, conv_b, x_proj_w, dt_proj_w, dt_proj_b, A_log, D, out_proj_w):
            B, L, _ = hidden_states.shape
            xz = jnp.einsum('bld,ed->ble', hidden_states, in_proj_w)
            x, z = jnp.split(xz, 2, axis=-1)
            x_pad = jnp.pad(x, ((0, 0), (D_CONV - 1, 0), (0, 0)))
            windows = jnp.stack([x_pad[:, k:k + L, :] for k in range(D_CONV)], axis=-1)
            x_conv = jnp.einsum('bldk,dk->bld', windows, conv_w) + conv_b
            x_act = jax.nn.silu(x_conv)
            x_dbl = jnp.einsum('bld,ed->ble', x_act, x_proj_w)
            dt, Bc, Cc = jnp.split(x_dbl, [DT_RANK, DT_RANK + D_STATE], axis=-1)
            dt = jax.nn.softplus(jnp.einsum('blr,dr->bld', dt, dt_proj_w) + dt_proj_b)
            A = -jnp.exp(A_log)

            def step(h, inp):
                x_t, dt_t, B_t, C_t = inp
                dA = jnp.exp(dt_t[:, :, None] * A[None])
                dBx = dt_t[:, :, None] * B_t[:, None, :] * x_t[:, :, None]
                h = h * dA + dBx
                y = jnp.einsum('bdn,bn->bd', h, C_t)
                return (h, y)
            xs = (x_act.transpose(1, 0, 2), dt.transpose(1, 0, 2), Bc.transpose(1, 0, 2), Cc.transpose(1, 0, 2))
            h0 = jnp.zeros((B, D_INNER, D_STATE), x_act.dtype)
            _, ys = jax.lax.scan(step, h0, xs)
            y = ys.transpose(1, 0, 2) + x_act * D
            y = y * jax.nn.silu(z)
            return jnp.einsum('bld,md->blm', y, out_proj_w)
        key = jax.random.key(seed)
        ks = jax.random.split(key, 10)
        s = 0.02
        inp = {'hidden_states': jax.random.normal(ks[0], (BATCH, SEQLEN, D_MODEL), jnp.float32), 'in_proj_w': jax.random.normal(ks[1], (2 * D_INNER, D_MODEL), jnp.float32) * s, 'conv_w': jax.random.normal(ks[2], (D_INNER, D_CONV), jnp.float32) * s, 'conv_b': jax.random.normal(ks[3], (D_INNER,), jnp.float32) * s, 'x_proj_w': jax.random.normal(ks[4], (DT_RANK + 2 * D_STATE, D_INNER), jnp.float32) * s, 'dt_proj_w': jax.random.normal(ks[5], (D_INNER, DT_RANK), jnp.float32) * s, 'dt_proj_b': jax.random.normal(ks[6], (D_INNER,), jnp.float32) * 0.1, 'A_log': jnp.log(jnp.tile(jnp.arange(1, D_STATE + 1, dtype=jnp.float32), (D_INNER, 1))), 'D': jnp.ones((D_INNER,), jnp.float32), 'out_proj_w': jax.random.normal(ks[7], (D_MODEL, D_INNER), jnp.float32) * s}
        return inp
    _L1_attn_in = _L1_attn_setup()

    def _L1_ffn_setup():
        import jax, jax.numpy as jnp
        import numpy as np
        H = 256
        I = 176
        E = 16
        K = 2
        SI = I * 2

        def _swiglu(gu, inter):
            g, u = (gu[..., :inter], gu[..., inter:])
            return jax.nn.silu(g) * u
        key = jax.random.key(seed)
        ks = jax.random.split(key, 6)
        s = 0.02
        hidden_states = jax.random.normal(ks[0], (1, 128, H), dtype=jnp.float32)
        gate_w = jax.random.normal(ks[1], (E, H), dtype=jnp.float32) * s
        w_gate_up = jax.random.normal(ks[2], (E, H, 2 * I), dtype=jnp.float32) * s
        w_down = jax.random.normal(ks[3], (E, I, H), dtype=jnp.float32) * s
        shared_gate_up = jax.random.normal(ks[4], (H, 2 * SI), dtype=jnp.float32) * s
        shared_down = jax.random.normal(ks[5], (SI, H), dtype=jnp.float32) * s
        return {'hidden_states': hidden_states, 'gate_w': gate_w, 'w_gate_up': w_gate_up, 'w_down': w_down, 'shared_gate_up': shared_gate_up, 'shared_down': shared_down}
    _L1_ffn_in = _L1_ffn_setup()
    _d = {'L0_attn_x': _L0_attn_in['x'], 'L0_attn_Wqkv': _L0_attn_in['Wqkv'], 'L0_attn_bqkv': _L0_attn_in['bqkv'], 'L0_attn_Wo': _L0_attn_in['Wo'], 'L0_attn_bo': _L0_attn_in['bo'], 'L0_ffn_w_gate': _L0_ffn_in['w_gate'], 'L0_ffn_w_up': _L0_ffn_in['w_up'], 'L0_ffn_w_down': _L0_ffn_in['w_down'], 'L1_attn_in_proj_w': _L1_attn_in['in_proj_w'], 'L1_attn_conv_w': _L1_attn_in['conv_w'], 'L1_attn_conv_b': _L1_attn_in['conv_b'], 'L1_attn_x_proj_w': _L1_attn_in['x_proj_w'], 'L1_attn_dt_proj_w': _L1_attn_in['dt_proj_w'], 'L1_attn_dt_proj_b': _L1_attn_in['dt_proj_b'], 'L1_attn_A_log': _L1_attn_in['A_log'], 'L1_attn_D': _L1_attn_in['D'], 'L1_attn_out_proj_w': _L1_attn_in['out_proj_w'], 'L1_ffn_gate_w': _L1_ffn_in['gate_w'], 'L1_ffn_w_gate_up': _L1_ffn_in['w_gate_up'], 'L1_ffn_w_down': _L1_ffn_in['w_down'], 'L1_ffn_shared_gate_up': _L1_ffn_in['shared_gate_up'], 'L1_ffn_shared_down': _L1_ffn_in['shared_down']}
    _x0 = _d['L0_attn_x']
    _d['L0_attn_x'] = jax.random.normal(jax.random.fold_in(jax.random.key(seed), 1), (1, 1024, 256), dtype=_x0.dtype)
    del _x0
    return _d

def reference(L0_attn_x, L0_attn_Wqkv, L0_attn_bqkv, L0_attn_Wo, L0_attn_bo, L0_ffn_w_gate, L0_ffn_w_up, L0_ffn_w_down, L1_attn_in_proj_w, L1_attn_conv_w, L1_attn_conv_b, L1_attn_x_proj_w, L1_attn_dt_proj_w, L1_attn_dt_proj_b, L1_attn_A_log, L1_attn_D, L1_attn_out_proj_w, L1_ffn_gate_w, L1_ffn_w_gate_up, L1_ffn_w_down, L1_ffn_shared_gate_up, L1_ffn_shared_down):

    def _L0_attn_ref(x, Wqkv, bqkv, Wo, bo):
        import jax, jax.numpy as jnp
        import numpy as np
        import math
        HIDDEN = 256
        NUM_HEADS = 16
        HEAD_SIZE = HIDDEN // NUM_HEADS
        BATCH = 2
        SEQ = 256
        b, s, _ = x.shape
        kqv = x @ Wqkv + bqkv
        kqv = kqv.reshape(b, s, 3, NUM_HEADS, HEAD_SIZE)
        q = kqv[:, :, 0]
        k = kqv[:, :, 1]
        v = kqv[:, :, 2]
        scores = jnp.einsum('bsnh,btnh->bnst', k, q) / math.sqrt(HEAD_SIZE)
        ones = jnp.ones_like(scores)
        scores = jnp.triu(scores) + -10000.0 * jnp.tril(ones, k=-1)
        attn = jax.nn.softmax(scores, axis=2)
        out = jnp.einsum('bnkq,bknh->bqnh', attn, v)
        out = out.reshape(b, s, NUM_HEADS * HEAD_SIZE)
        return out @ Wo + bo

    def _L0_ffn_ref(x, w_gate, w_up, w_down):
        import jax, jax.numpy as jnp
        import numpy as np

        def _sparsify_2to4(h):
            B, S, I = h.shape
            g = h.reshape(B, S, I // 4, 4)
            a = jnp.abs(g)
            _, idx = jax.lax.top_k(a, 2)
            pos = jnp.arange(4)
            mask = (pos == idx[..., 0:1]) | (pos == idx[..., 1:2])
            return (g * mask.astype(g.dtype)).reshape(B, S, I)
        h = jax.nn.silu(jnp.einsum('bsh,hi->bsi', x, w_gate)) * jnp.einsum('bsh,hi->bsi', x, w_up)
        h_sparse = _sparsify_2to4(h)
        return jnp.einsum('bsi,ih->bsh', h_sparse, w_down)

    def _L1_attn_ref(hidden_states, in_proj_w, conv_w, conv_b, x_proj_w, dt_proj_w, dt_proj_b, A_log, D, out_proj_w):
        import jax, jax.numpy as jnp
        import numpy as np
        D_MODEL = 256
        D_INNER = 2 * D_MODEL
        D_STATE = 16
        D_CONV = 4
        DT_RANK = D_MODEL // 16
        BATCH, SEQLEN = (2, 128)

        def _mamba_forward(hidden_states, in_proj_w, conv_w, conv_b, x_proj_w, dt_proj_w, dt_proj_b, A_log, D, out_proj_w):
            B, L, _ = hidden_states.shape
            xz = jnp.einsum('bld,ed->ble', hidden_states, in_proj_w)
            x, z = jnp.split(xz, 2, axis=-1)
            x_pad = jnp.pad(x, ((0, 0), (D_CONV - 1, 0), (0, 0)))
            windows = jnp.stack([x_pad[:, k:k + L, :] for k in range(D_CONV)], axis=-1)
            x_conv = jnp.einsum('bldk,dk->bld', windows, conv_w) + conv_b
            x_act = jax.nn.silu(x_conv)
            x_dbl = jnp.einsum('bld,ed->ble', x_act, x_proj_w)
            dt, Bc, Cc = jnp.split(x_dbl, [DT_RANK, DT_RANK + D_STATE], axis=-1)
            dt = jax.nn.softplus(jnp.einsum('blr,dr->bld', dt, dt_proj_w) + dt_proj_b)
            A = -jnp.exp(A_log)

            def step(h, inp):
                x_t, dt_t, B_t, C_t = inp
                dA = jnp.exp(dt_t[:, :, None] * A[None])
                dBx = dt_t[:, :, None] * B_t[:, None, :] * x_t[:, :, None]
                h = h * dA + dBx
                y = jnp.einsum('bdn,bn->bd', h, C_t)
                return (h, y)
            xs = (x_act.transpose(1, 0, 2), dt.transpose(1, 0, 2), Bc.transpose(1, 0, 2), Cc.transpose(1, 0, 2))
            h0 = jnp.zeros((B, D_INNER, D_STATE), x_act.dtype)
            _, ys = jax.lax.scan(step, h0, xs)
            y = ys.transpose(1, 0, 2) + x_act * D
            y = y * jax.nn.silu(z)
            return jnp.einsum('bld,md->blm', y, out_proj_w)
        return _mamba_forward(hidden_states, in_proj_w, conv_w, conv_b, x_proj_w, dt_proj_w, dt_proj_b, A_log, D, out_proj_w)

    def _L1_ffn_ref(hidden_states, gate_w, w_gate_up, w_down, shared_gate_up, shared_down):
        import jax, jax.numpy as jnp
        import numpy as np
        H = 256
        I = 176
        E = 16
        K = 2
        SI = I * 2

        def _swiglu(gu, inter):
            g, u = (gu[..., :inter], gu[..., inter:])
            return jax.nn.silu(g) * u
        orig_shape = hidden_states.shape
        x = hidden_states.reshape(-1, H)
        logits = jnp.einsum('th,eh->te', x, gate_w)
        scores = jax.nn.softmax(logits, axis=-1)
        topk_w, topk_idx = jax.lax.top_k(scores, K)
        combine = jnp.sum(jax.nn.one_hot(topk_idx, E, dtype=x.dtype) * topk_w[..., None], axis=1)
        gu = jnp.einsum('th,ehj->etj', x, w_gate_up)
        h = _swiglu(gu, I)
        y = jnp.einsum('eti,eih,te->th', h, w_down, combine)
        gu_s = x @ shared_gate_up
        y = y + _swiglu(gu_s, SI) @ shared_down
        return y.reshape(orig_shape)
    x = L0_attn_x
    x = _layernorm(x + _L0_attn_ref(x, L0_attn_Wqkv, L0_attn_bqkv, L0_attn_Wo, L0_attn_bo), axis=-1)
    x = _layernorm(x + _L0_ffn_ref(x, L0_ffn_w_gate, L0_ffn_w_up, L0_ffn_w_down), axis=-1)
    x = _layernorm(x + _L1_attn_ref(x, L1_attn_in_proj_w, L1_attn_conv_w, L1_attn_conv_b, L1_attn_x_proj_w, L1_attn_dt_proj_w, L1_attn_dt_proj_b, L1_attn_A_log, L1_attn_D, L1_attn_out_proj_w), axis=-1)
    x = _layernorm(x + _L1_ffn_ref(x, L1_ffn_gate_w, L1_ffn_w_gate_up, L1_ffn_w_down, L1_ffn_shared_gate_up, L1_ffn_shared_down), axis=-1)
    return x

_drawn_inputs = setup_inputs


def setup_inputs(seed=0):
    import zlib

    import numpy as np

    out = dict(_drawn_inputs(seed))
    spreads = {'L1_attn_D': (1.0, 0.6)}
    factors = {'L0_attn_bqkv': 2.813,
     'L0_attn_bo': 3.203,
     'L1_attn_in_proj_w': 8.0,
     'L1_attn_conv_w': 8.0,
     'L1_attn_conv_b': 8.0,
     'L1_attn_x_proj_w': 8.0,
     'L1_attn_dt_proj_w': 8.0,
     'L1_attn_dt_proj_b': 8.0,
     'L1_attn_A_log': 8.0,
     'L1_attn_out_proj_w': 8.0,
     'L1_ffn_gate_w': 8.0,
     'L1_ffn_w_gate_up': 8.0,
     'L1_ffn_w_down': 8.0,
     'L1_ffn_shared_gate_up': 2.849,
     'L1_ffn_shared_down': 2.845}
    for name, (base, spread) in spreads.items():
        noise = np.random.default_rng([zlib.crc32(name.encode()), seed]).standard_normal(out[name].shape)
        drawn = base * np.exp(spread * noise) if base else spread * noise
        out[name] = jnp.asarray(drawn.astype(out[name].dtype))
    for name, factor in factors.items():
        out[name] = (out[name] * factor).astype(out[name].dtype)
    return out
```

```python
from contextlib import ExitStack

import numpy as np

import concourse.bass as bass
from concourse import mybir

F32 = mybir.dt.float32
BF16 = mybir.dt.bfloat16
U32 = mybir.dt.uint32
ALU = mybir.AluOpType
ACT = mybir.ActivationFunctionType
AX = mybir.AxisListType

P = 128
T = 1024
NT = T // P
TH = 512
NH = T // TH
TPH = TH // P
D = 256
KD = D // P
HEADS = 16
HD = D // HEADS
HPT = HEADS // KD
G = 4
NG = HEADS // G
VC = 32
SPLIT = 3
KROWS = 6 * HD
KX = KROWS + SPLIT
EPS = 1e-5
FF = 1024
FB = FF // P
GS = 4
DI = 512
KI = DI // P
NS = 16
RANK = 16
BC = 2 * NS
XD = 3 * BC + RANK
TAPS = 4
E = 16
EI = 176
EH = EI // 2
SHARED = 2
EX = E + SHARED
DMA = 16

QK_ORDER = [(0, 0), (0, 1), (2, 0), (2, 1), (1, 0), (1, 1), (3, 0), (3, 1)]
UNITS = [(j, tt, h) for j in range(G) for tt in range(NT) for h in range(tt // TPH + 1)]
UPR = len(UNITS) // NT
COLS = {"b_qk": (0, 4), "conv_w": (4, 20), "conv_b": (20, 24), "dt_b": (24, 28), "skip": (28, 32),
        "a_log": (32, 32 + KI * NS)}
NCOLS = 32 + KI * NS


def out_bank(tt):
    return 3 if tt < TPH else 2 + tt % 2


def build(nc, a, out, scratch):
    ctx = ExitStack()
    with ctx:
        def sb(name, shape, dt=F32):
            return ctx.enter_context(nc.sbuf_tensor(name, shape, dt))

        def sem(name):
            return ctx.enter_context(nc.semaphore(name))

        ps = ctx.enter_context(nc.psum_tensor("ps", [P, 8, TH], F32))
        psb = ps[:, :, :].rearrange("p b n -> p (b n)").bitcast(BF16).rearrange("p (b n) -> p b n", b=8)

        ident = sb("ident", [P, P])
        masks = sb("masks", [P, 2, P], BF16)
        identb, causal = masks[:, 0, :], masks[:, 1, :]
        cols = sb("cols", [P, NCOLS])
        x_tok = sb("x_tok", [P, NT, D])
        y_tok = sb("y_tok", [P, NT, D])
        x_feat = sb("x_feat", [P, KD, T])
        stats = sb("stats", [P, NT, 6])
        mv = sb("mv", [P, NT, 2])
        rstd = sb("rstd", [P, NT])
        minus_half = sb("minus_half", [P, NT])

        ARENA = 46500
        arena = sb("arena", [P, ARENA])
        at = [0]

        def take(words):
            lo = at[0]
            at[0] += words
            assert at[0] <= ARENA, at[0]
            return arena[:, lo:lo + words]

        def take_b(n):
            return take(n // 2).bitcast(BF16)

        w_g = take(KD * FF).rearrange("p (k b n) -> p k b n", k=KD, b=FB)
        w_u = take(KD * FF).rearrange("p (k b n) -> p k b n", k=KD, b=FB)
        w_d = take(FB * D).rearrange("p (b n) -> p b n", b=FB)
        w_o = take(KD * D).rearrange("p (k n) -> p k n", k=KD)
        o_feat = take(NG * T).rearrange("p (g t) -> p g t", g=NG)
        rden = take(2 * HEADS).rearrange("p (b h) -> p b h", b=2)
        o_tok = take(2 * D).rearrange("p (b d) -> p b d", b=2)
        o_nf = take(2 * D).rearrange("p (b k t) -> p b k t", b=2, k=KD)
        after_attention = at[0]
        w_qkv = take(KD * 3 * D).rearrange("p (k n) -> p k n", k=KD)
        bias_vo = take(2 * D).rearrange("p (b n) -> p b n", b=2)
        b_q4 = take(KD)
        nmax = take(NH * NT * G).rearrange("p (h t j) -> p h t j", h=NH, t=NT)
        nmax_r = take(NT * G).rearrange("p (t j) -> p t j", t=NT)
        nmax_p = take_b(NT * SPLIT * G).rearrange("p (t c j) -> p t c j", t=NT, c=SPLIT)
        nmax_f = take_b(T)
        v_aug = take(NT * HEADS * VC).rearrange("p (s h c) -> p s h c", s=NT, h=HEADS)
        q_st = take_b(HEADS * T).rearrange("p (h t) -> p h t", h=HEADS)
        k_st = take_b(HEADS * T).rearrange("p (h t) -> p h t", h=HEADS)
        overlay = at[0]
        qk_full = take(8 * TH).rearrange("p (i t) -> p i t", i=8)
        qk_part = take_b(SPLIT * 4 * T).rearrange("p (c m t) -> p c m t", c=SPLIT, m=4)
        at[0] = overlay
        probs = take(8 * T).rearrange("p (b t) -> p b t", b=8)

        assert at[0] <= ARENA
        at[0] = after_attention
        ff_s = take(2 * TH).rearrange("p (b t) -> p b t", b=2)
        ff_h = take(2 * GS * TH).rearrange("p (b j t) -> p b j t", b=2, j=GS)
        ff_a = take(2 * GS * TH).rearrange("p (b j t) -> p b j t", b=2, j=GS)
        ff_c = take_b(6 * TH).rearrange("p (c t) -> p c t", c=6)
        ff_w = take_b(GS * TH).rearrange("p (j t) -> p j t", j=GS)
        ff_k = take(FB * T).rearrange("p (b t) -> p b t", b=FB)
        at[0] = ARENA - (KD * 2 * DI + KI * D + KI * XD + DI + BC * P // 2)
        assert at[0] >= after_attention + 20480
        mamba_top = at[0]
        w_in = take(KD * 2 * DI).rearrange("p (k n) -> p k n", k=KD)
        w_out = take(KI * D).rearrange("p (k n) -> p k n", k=KI)
        w_xp = take(KI * XD).rearrange("p (k n) -> p k n", k=KI)
        w_dt = take(DI)
        pick = take_b(BC * P).rearrange("p (r n) -> p r n", r=BC)
        at[0] = 0
        RING = 3
        w_gu = take(RING * KD * 2 * EI).rearrange("p (b k n) -> p b k n", b=RING, k=KD)
        w_dn = take(RING * 2 * D).rearrange("p (b k n) -> p b k n", b=RING, k=2)
        w_r = take(KD * E).rearrange("p (k e) -> p k e", k=KD)
        e_s = take(2 * EI).rearrange("p (b n) -> p b n", b=2)
        e_h = take(2 * EI).rearrange("p (b n) -> p b n", b=2)
        e_f = take(2 * 2 * P).rearrange("p (b c t) -> p b c t", b=2, c=2)
        combine = take(NT * EX).rearrange("p (t e) -> p t e", t=NT)
        r_p = take(NT * E).rearrange("p (t e) -> p t e", t=NT)
        r_q = take(NT * E).rearrange("p (t e) -> p t e", t=NT)
        r_m = take(NT * E).rearrange("p (t e) -> p t e", t=NT)
        r_max = take(NT)
        r_8 = take(NT * 8).rearrange("p (t e) -> p t e", t=NT)
        r_i = take(NT * 8).rearrange("p (t e) -> p t e", t=NT)
        r_if = take(NT * 8).rearrange("p (t e) -> p t e", t=NT)
        iota_e = take(E)
        zeros = arena[:, at[0]:at[0] + TH]
        bc3 = take_b(T)
        a_neg = take(KI * NS).rearrange("p (k n) -> p k n", k=KI)
        h_last = take(KI * NS).rearrange("p (k n) -> p k n", k=KI)
        xa = take(KI * T).rearrange("p (k t) -> p k t", k=KI)
        sz = take(KI * T).rearrange("p (k t) -> p k t", k=KI)
        dt_ = take(KI * T).rearrange("p (k t) -> p k t", k=KI)
        dtx = take(KI * T).rearrange("p (k t) -> p k t", k=KI)
        scan_at = at[0]
        assert scan_at + 8 * KI * TH + 2 * TH <= mamba_top, (scan_at + 8 * KI * TH + 2 * TH, mamba_top)
        b_sb = take(2 * TH).rearrange("p (b t) -> p b t", b=2)
        dA = take(2 * KI * TH).rearrange("p (b k t) -> p b k t", b=2, k=KI)
        dBx = take(2 * KI * TH).rearrange("p (b k t) -> p b k t", b=2, k=KI)
        hs = take(2 * KI * TH).rearrange("p (b k t) -> p b k t", b=2, k=KI)
        hc = take(2 * KI * TH).rearrange("p (b k t) -> p b k t", b=2, k=KI)
        at[0] = scan_at
        x_in = take(KI * (T + TAPS - 1) + 4)[:, 0:KI * (T + TAPS - 1)].rearrange("p (k t) -> p k t", k=KI)
        bc_p = take_b(2 * TH).rearrange("p (c t) -> p c t", c=2)
        bc_r = take(TH)
        dt_lo = take(T)
        sp_e = take(KI * TH).rearrange("p (k t) -> p k t", k=KI)
        sp_w = take(KI * TH).rearrange("p (k t) -> p k t", k=KI)
        sp_d = take(KI * TH).rearrange("p (k t) -> p k t", k=KI)
        assert at[0] <= mamba_top

        ld_x = sem("ld_x")
        ld_wqkv = sem("ld_wqkv")
        ld_small = sem("ld_small")
        ld_tok = sem("ld_tok")
        ld_wo = sem("ld_wo")
        parts_out = [sem(f"parts_out{i}") for i in range(4)]
        st_loaded = [sem(f"st_loaded{i}") for i in range(2)]
        nmax_loaded = [sem(f"nmax_loaded{i}") for i in range(NG)]
        stored = sem("stored")
        bias_ready = sem("bias_ready")
        qk_ready = sem("qk_ready")
        qk_taken = sem("qk_taken")
        qk_rest = sem("qk_rest")
        qk_mid = sem("qk_mid")
        parts_ready = sem("parts_ready")
        v_ready = sem("v_ready")
        v_taken = sem("v_taken")
        ones_ready = sem("ones_ready")
        max_ready = sem("max_ready")
        max_taken = sem("max_taken")
        nmax_parts = sem("nmax_parts")
        nmaxT_ready = sem("nmaxT_ready")
        nmax_feat = sem("nmax_feat")
        scores_ready = sem("scores_ready")
        probs_ready = sem("probs_ready")
        pv_done = sem("pv_done")
        o_taken = sem("o_taken")
        vec_own = sem("vec_own")
        ld_ffw = sem("ld_ffw")
        ld_mamba = sem("ld_mamba")
        ld_router = sem("ld_router")
        xb_ready = sem("xb_ready")
        oT_ready = sem("oT_ready")
        o_norm = sem("o_norm")
        oN_ready = sem("oN_ready")
        onf_ready = sem("onf_ready")
        wo_ready = sem("wo_ready")
        y_ready = sem("y_ready")
        stats_ready = sem("stats_ready")
        rstd_ready = sem("rstd_ready")
        norm_ready = sem("norm_ready")
        xT_ready = sem("xT_ready")
        feat_ready = sem("feat_ready")
        gu_ready = sem("gu_ready")
        silu_ready = sem("silu_ready")
        ffh_ready = sem("ffh_ready")
        abs_ready = sem("abs_ready")
        kept_ready = sem("kept_ready")
        down_ready = sem("down_ready")
        inx_ready = sem("inx_ready")
        xin_ready = sem("xin_ready")
        xacc_ready = sem("xacc_ready")
        conv_done = sem("conv_done")
        xa_ready = sem("xa_ready")
        z_ready = sem("z_ready")
        xd_ready = sem("xd_ready")
        bc_ready = sem("bc_ready")
        dt_ready = sem("dt_ready")
        sp_abs = sem("sp_abs")
        sp_exp = sem("sp_exp")
        sp_w_ready = sem("sp_w_ready")
        sp_ln = sem("sp_ln")
        sp_d_ready = sem("sp_d_ready")
        dt_done = sem("dt_done")
        u_done = sem("u_done")
        a_exp = sem("a_exp")
        a_ready = sem("a_ready")
        bcast_ready = sem("bcast_ready")
        b_copied = sem("b_copied")
        dA_ready = sem("dA_ready")
        dBx_ready = sem("dBx_ready")
        scanned = sem("scanned")
        cmul_done = sem("cmul_done")
        y_acc = sem("y_acc")
        y_half = sem("y_half")
        ym_ready = sem("ym_ready")
        mout_ready = sem("mout_ready")
        logit_ready = sem("logit_ready")
        r_sub = sem("r_sub")
        r_exp = sem("r_exp")
        combine_ready = sem("combine_ready")
        zero_ready = sem("zero_ready")
        zeroed = sem("zeroed")
        egu_ready = sem("egu_ready")
        es_ready = sem("es_ready")
        eh_ready = sem("eh_ready")
        eT_ready = sem("eT_ready")
        ef_ready = sem("ef_ready")
        edn_ready = sem("edn_ready")
        pool_own = sem("pool_own")
        act_own = sem("act_own")
        ld_expert = [sem(f"ld_expert{i}") for i in range(RING)]
        block = ctx.enter_context(nc.Block())

        rq = scratch.rearrange("m c p t -> m (c p) t")

        @block.sync
        def _(sp):
            for k in range(KD):
                sp.dma_start(w_qkv[:, k, :], a["w_qkv"][:, k, :]).then_inc(ld_wqkv, DMA)
                sp.dma_start(x_feat[:, k, :], a["x_feat"][:, k, :]).then_inc(ld_x, DMA)
            sp.dma_start(cols[:, :], a["cols"]).then_inc(ld_small, DMA)
            sp.dma_start(bias_vo[:, :, :], a["bias_vo"]).then_inc(ld_small, DMA)
            sp.dma_start(masks[:, :, :], a["masks"].bitcast(BF16)).then_inc(ld_small, DMA)
            sp.dma_start(ident[:, :], a["ident"]).then_inc(ld_small, DMA)
            for pair in range(KD):
                for m, st in ((pair, q_st), (KD + pair, k_st)):
                    order = 2 * pair + (m >= KD)
                    sp.wait_ge(parts_ready, 2 * (order + 1))
                    sp.dma_start(scratch[m].rearrange("c p t -> p c t"), qk_part[:, :, m, :]).then_inc(parts_out[m], DMA)
                for m, st in ((pair, q_st), (KD + pair, k_st)):
                    sp.wait_ge(parts_out[m], DMA)
                    heads = slice(pair * HPT, (pair + 1) * HPT)
                    runs = [(0, 0, 3), (3, 0, 2), (5, 0, 1)] if m < KD else \
                        [(0, 0, 1), (1, 0, 1), (2, 0, 1), (3, 1, 1), (4, 1, 1), (5, 2, 1)]
                    for slot, c, n in runs:
                        src = scratch[m, c:c + n].rearrange("c (r h) t -> (c r) (h t)", h=HPT)
                        sp.dma_start(st[slot * HD:(slot + n) * HD, heads, :], src.rearrange("r (h t) -> r h t", h=HPT)).then_inc(st_loaded[pair], DMA)
            sp.dma_start(x_tok[:, :, :], a["x_tok"]).then_inc(ld_tok, DMA)
            sp.dma_start(w_o[:, :, :], a["w_o"]).then_inc(ld_wo, DMA)
            for g in range(NG):
                sp.wait_ge(nmax_feat, g + 1)
                for c in range(SPLIT):
                    sp.dma_start(q_st[KROWS + c:KROWS + c + 1, G * g:G * g + G, :], nmax_f[c * G:(c + 1) * G, :]).then_inc(nmax_loaded[g], DMA)
            sp.dma_start(w_g[:, :, :, :], a["w_g"]).then_inc(ld_ffw, DMA)
            sp.dma_start(w_u[:, :, :, :], a["w_u"]).then_inc(ld_ffw, DMA)
            sp.dma_start(w_d[:, :, :], a["w_d"]).then_inc(ld_ffw, DMA)
            sp.wait_ge(pv_done, NG * NT)
            sp.dma_start(w_in[:, :, :], a["w_in"]).then_inc(ld_mamba, DMA)
            sp.dma_start(w_xp[:, :, :], a["w_xp"]).then_inc(ld_mamba, DMA)
            sp.dma_start(w_dt[3 * BC:XD, :], a["w_dt"]).then_inc(ld_mamba, DMA)
            sp.dma_start(pick[0:3 * BC, :, :], a["pick"].bitcast(BF16)).then_inc(ld_mamba, DMA)
            sp.dma_start(w_out[:, :, :], a["w_out"]).then_inc(ld_mamba, DMA)
            sp.wait_ge(down_ready, NT)
            sp.dma_start(w_r[:, :, :], a["w_r"]).then_inc(ld_router, DMA)
            sp.dma_start(iota_e[:, :], a["iota_e"]).then_inc(ld_router, DMA)
            for e in range(EX):
                if e >= RING:
                    sp.wait_ge(edn_ready, (e - RING + 1) * NT)
                sp.dma_start(w_gu[:, e % RING, :, :], a["w_gu"][e]).then_inc(ld_expert[e % RING], DMA)
                sp.dma_start(w_dn[0:EH, e % RING, :, :], a["w_dn"][e]).then_inc(ld_expert[e % RING], DMA)
            for h in range(NH):
                sp.wait_ge(norm_ready, 3 * NT + (h + 1) * TPH)
                sp.dma_start(out[:, h * TPH:(h + 1) * TPH, :], x_tok[:, h * TPH:(h + 1) * TPH, :]).then_inc(stored, DMA)
            sp.wait_ge(stored, NH * DMA)

        @block.gpsimd
        def _(pool):
            nc.gpsimd.memset(v_aug[:, :, :, HD:VC], 1.0).then_inc(ones_ready, 1)
            pool.wait_ge(ones_ready, 1)
            nc.gpsimd.memset(k_st[KROWS:KX, :, :], 1.0).then_inc(ones_ready, 1)
            pool.wait_ge(ones_ready, 2)
            nc.gpsimd.memset(minus_half[:, :], -0.5).then_inc(ones_ready, 1)

            pool.wait_ge(ld_tok, DMA)
            pool.wait_ge(ld_small, 4 * DMA)
            nc.gpsimd.tensor_tensor(x_tok[:, :, :], x_tok[:, :, :],
                                    bias_vo[:, 1, :].unsqueeze(1).broadcast_to([P, NT, D]), ALU.add).then_inc(xb_ready, 1)

            def inverse_deviation(layer, h):
                n = layer * NH + h + 1
                tts = slice(h * TPH, (h + 1) * TPH)
                pool.wait_ge(stats_ready, n)
                nc.gpsimd.tensor_tensor(rstd[:, tts], mv[:, tts, 1], minus_half[:, tts], ALU.pow).then_inc(rstd_ready, 1)

            for layer in range(2):
                for h in range(NH):
                    inverse_deviation(layer, h)
            pool.wait_ge(kept_ready, NH * FB)
            pool.wait_ge(down_ready, NT)
            nc.gpsimd.memset(x_in[:, :, 0:TAPS - 1], 0.0).then_inc(zero_ready, 1)
            nc.gpsimd.memset(combine[:, :, E:EX], 1.0).then_inc(zero_ready, 1)
            for i in range(NH * KI):
                h, k = divmod(i, KI)
                pool.wait_ge(dt_done, i + 1)
                nc.gpsimd.tensor_tensor(dtx[:, k, h * TH:(h + 1) * TH], dt_[:, k, h * TH:(h + 1) * TH],
                                        xa[:, k, h * TH:(h + 1) * TH], ALU.mult).then_inc(u_done, 1)
            pool.wait_ge(u_done, NH * KI)
            for i in range(NH * NS):
                h, n = divmod(i, NS)
                pool.wait_ge(b_copied, i + 1)
                if i >= 2:
                    pool.wait_ge(scanned, KI * (i - 1))
                nc.gpsimd.tensor_tensor(dBx[:, i % 2, :, :], dtx[:, :, h * TH:(h + 1) * TH],
                                        b_sb[:, i % 2, :].unsqueeze(1).broadcast_to([P, KI, TH]),
                                        ALU.mult).then_inc(dBx_ready, 1)
                if i == NS + 6:
                    inverse_deviation(2, 0)
            inverse_deviation(2, 1)
            pool.wait_ge(y_acc, NH * NS)
            nc.gpsimd.memset(zeros[0:1, :], 0.0).then_inc(zero_ready, 1)
            for h in range(NH):
                inverse_deviation(3, h)

        @block.tensor
        def _(pe):
            pe.wait_ge(ld_wqkv, KD * DMA)
            pe.wait_ge(ld_x, KD * DMA)
            for i, (m, h) in enumerate(QK_ORDER):
                for k in range(KD):
                    mm = nc.tensor.matmul(ps[:, i, :], w_qkv[:, k, m * P:(m + 1) * P],
                                          x_feat[:, k, h * TH:(h + 1) * TH], start=(k == 0), stop=(k == KD - 1))
                mm.then_inc(qk_ready, 1)
            for tt in range(NT):
                pe.wait_ge(qk_taken, tt + 1)
                for k in range(KD):
                    mm = nc.tensor.matmul(ps[:, tt, 0:D], x_feat[:, k, tt * P:(tt + 1) * P],
                                          w_qkv[:, k, 2 * D:3 * D], start=(k == 0), stop=(k == KD - 1))
                mm.then_inc(v_ready, 1)

            def bank_free(n):
                if n < 2:
                    pe.wait_ge(v_taken, n + 1)
                    return
                g, u = divmod(n - 2, len(UNITS) + 1)
                if u == len(UNITS):
                    pe.wait_ge(nmax_feat, g + 1)
                else:
                    pe.wait_ge(max_taken, g * len(UNITS) + u + 1)

            def max_unit(g, u):
                n = g * (len(UNITS) + 1) + u
                j, tt, h = UNITS[u]
                bank_free(n)
                head, bank = G * g + j, n % 2
                w = min(TH, (tt + 1) * P - h * TH)
                diagonal = h == tt // TPH
                mm = nc.tensor.matmul(ps[:, bank, 0:w], q_st[0:KROWS, head, tt * P:(tt + 1) * P],
                                      k_st[0:KROWS, head, h * TH:h * TH + w], start=True, stop=not diagonal)
                if diagonal:
                    mm = nc.tensor.matmul(ps[:, bank, w - P:w], causal, identb, start=False, stop=True)
                mm.then_inc(max_ready, 1)

            def max_transposes(g):
                n = (g + 1) * (len(UNITS) + 1) - 1
                bank_free(n)
                pe.wait_ge(nmax_parts, g + 1)
                for tt in range(NT):
                    mm = nc.tensor.transpose(psb[0:SPLIT * G, n % 2, tt * P:(tt + 1) * P],
                                             nmax_p[:, tt, :, :].rearrange("p c j -> p (c j)"), identb)
                mm.then_inc(nmaxT_ready, 1)

            def score(g, st, j):
                n = (g * NT + st) * G + j
                if n >= 2:
                    pe.wait_ge(probs_ready, n - 1)
                else:
                    pe.wait_ge(v_taken, 2 * n + 4)
                head, b = G * g + j, 2 + 2 * (n % 2)
                for h in range(st // TPH, NH):
                    lo = max(st * P, h * TH)
                    diagonal = h == st // TPH
                    mm = nc.tensor.matmul(ps[:, b + h, lo - h * TH:TH], k_st[0:KX, head, st * P:(st + 1) * P],
                                          q_st[0:KX, head, lo:(h + 1) * TH], start=True, stop=not diagonal)
                    if diagonal:
                        mm = nc.tensor.matmul(ps[:, b + h, lo - h * TH:lo - h * TH + P], identb, causal,
                                              start=False, stop=True)
                mm.then_inc(scores_ready, 1)

            def values(g, st):
                r = g * NT + st
                pe.wait_ge(probs_ready, G * (r + 1))
                if st == 0 and g:
                    pe.wait_ge(o_taken, g)
                elif st == 0:
                    pe.wait_ge(v_taken, NT)
                for h in range(st // TPH, NH):
                    lo = max(st * P, h * TH)
                    for j in range(G):
                        mm = nc.tensor.matmul(ps[VC * j:VC * (j + 1), 6 + h, lo - h * TH:TH],
                                              v_aug[:, st, G * g + j, :],
                                              probs[:, (G * r + j) % 8, lo:(h + 1) * TH],
                                              start=(st == 0), stop=(st == TPH * (h + 1) - 1))
                mm.then_inc(pv_done, 1)

            pe.wait_ge(ones_ready, 3)
            pe.wait_ge(ld_small, 4 * DMA)
            pe.wait_ge(st_loaded[0], 9 * DMA)
            for u in range(len(UNITS)):
                max_unit(0, u)
            max_transposes(0)
            for g in range(NG):
                if g + 1 == NG // 2:
                    pe.wait_ge(st_loaded[1], 9 * DMA)
                pe.wait_ge(nmax_loaded[g], SPLIT * DMA)
                for st in range(NT):
                    for j in range(G):
                        score(g, st, j)
                        if g + 1 < NG:
                            for u in range(st * UPR + j * UPR // G, st * UPR + (j + 1) * UPR // G):
                                max_unit(g + 1, u)
                    if st or g:
                        values(*divmod(g * NT + st - 1, NT))
                if g + 1 < NG:
                    max_transposes(g + 1)
            values(NG - 1, NT - 1)


            def o_transposes(tt):
                if tt >= 2:
                    pe.wait_ge(o_norm, tt - 1)
                for g in range(NG):
                    mm = nc.tensor.transpose(ps[:, tt % 2, g * P:(g + 1) * P], o_feat[:, g, tt * P:(tt + 1) * P], ident[:, :])
                mm.then_inc(oT_ready, 1)

            def o_back(tt):
                pe.wait_ge(o_norm, tt + 1)
                if tt >= 2:
                    pe.wait_ge(onf_ready, tt - 1)
                for k in range(KD):
                    mm = nc.tensor.transpose(ps[:, 2 + tt % 2, k * P:(k + 1) * P], o_tok[:, tt % 2, k * P:(k + 1) * P], ident[:, :])
                mm.then_inc(oN_ready, 1)

            def o_project(tt):
                pe.wait_ge(onf_ready, tt + 1)
                if tt >= 2:
                    pe.wait_ge(y_ready, tt - 1)
                for k in range(KD):
                    mm = nc.tensor.matmul(ps[:, 4 + tt % 2, 0:D], o_nf[:, tt % 2, k, :], w_o[:, k, :],
                                          start=(k == 0), stop=(k == KD - 1))
                mm.then_inc(wo_ready, 1)

            def to_features(layer, h):
                if layer or h:
                    pe.wait_ge(feat_ready, layer * NH + h)
                for tt in range(h * TPH, (h + 1) * TPH):
                    pe.wait_ge(norm_ready, layer * NT + tt + 1)
                    for k in range(KD):
                        c = (tt - h * TPH) * P
                        mm = nc.tensor.transpose(ps[:, 6 + k, c:c + P], x_tok[:, tt, k * P:(k + 1) * P], ident[:, :])
                mm.then_inc(xT_ready, 1)

            pe.wait_ge(ld_wo, DMA)
            pe.wait_ge(o_taken, NG)
            for i in range(NT + 2):
                if i < NT:
                    o_transposes(i)
                if 1 <= i <= NT:
                    o_back(i - 1)
                if i >= 2:
                    o_project(i - 2)

            def gate_up(h):
                pe.wait_ge(feat_ready, h + 1)
                for b in range(FB):
                    n = h * FB + b
                    if n >= 2:
                        pe.wait_ge(ffh_ready, n - 1)
                    for w, bank in ((w_g, 2 * (n % 2)), (w_u, 2 * (n % 2) + 1)):
                        for k in range(KD):
                            mm = nc.tensor.matmul(ps[:, bank, :], w[:, k, b, :], x_feat[:, k, h * TH:(h + 1) * TH],
                                                  start=(k == 0), stop=(k == KD - 1))
                    mm.then_inc(gu_ready, 1)

            pe.wait_ge(ld_ffw, 3 * DMA)
            for h in range(NH):
                to_features(0, h)
                gate_up(h)
            for tt in range(NT):
                pe.wait_ge(y_ready, NT + tt - 1)
                for b in range(FB):
                    if tt % TPH == 0:
                        pe.wait_ge(kept_ready, tt // TPH * FB + b + 1)
                    mm = nc.tensor.matmul(ps[:, 4 + tt % 2, 0:D], ff_k[:, b, tt * P:(tt + 1) * P], w_d[:, b, :],
                                          start=(b == 0), stop=(b == FB - 1))
                mm.then_inc(down_ready, 1)

            pe.wait_ge(ld_mamba, 5 * DMA)
            for h in range(NH):
                to_features(1, h)
                pe.wait_ge(feat_ready, NH + h + 1)
                for m in range(2 * KI):
                    n = h * 2 * KI + m
                    if n >= 4:
                        if m < KI:
                            pe.wait_ge(z_ready, (h - 1) * KI + m + 1)
                        else:
                            pe.wait_ge(xin_ready, h * KI + m - KI + 1)
                    for k in range(KD):
                        mm = nc.tensor.matmul(ps[:, m % 4, :], w_in[:, k, m * P:(m + 1) * P], x_feat[:, k, h * TH:(h + 1) * TH],
                                              start=(k == 0), stop=(k == KD - 1))
                    mm.then_inc(inx_ready, 1)
            for h in range(NH):
                for k in range(KI):
                    pe.wait_ge(xa_ready, h * KI + k + 1)
                    if k == 0:
                        pe.wait_ge(y_ready, 2 * NT)
                    mm = nc.tensor.matmul(ps[0:XD, 4 + h, :], w_xp[:, k, :], xa[:, k, h * TH:(h + 1) * TH],
                                          start=(k == 0), stop=(k == KI - 1))
                mm.then_inc(xd_ready, 1)
            for h in range(NH):
                pe.wait_ge(dt_ready, h + 1)
                for k in range(KI):
                    if h:
                        pe.wait_ge(sp_d_ready, (h - 1) * KI + k + 1)
                    else:
                        pe.wait_ge(z_ready, KI + k + 1)
                    nc.tensor.matmul(ps[:, k, :], w_dt[3 * BC:XD, k * P:(k + 1) * P], dt_lo[3 * BC:XD, h * TH:(h + 1) * TH],
                                     start=True, stop=True).then_inc(sp_abs, 1)

            def broadcast(i):
                h, n = divmod(i, NS)
                if i == 0:
                    pe.wait_ge(bc_ready, NH)
                    pe.wait_ge(sp_d_ready, NH * KI)
                else:
                    pe.wait_ge(b_copied, i)
                if i >= 2:
                    pe.wait_ge(cmul_done, i - 1)
                nc.tensor.matmul(ps[:, 0, :], pick[0:3 * BC, n, :], bc3[0:3 * BC, h * TH:(h + 1) * TH], start=True, stop=True)
                nc.tensor.matmul(ps[:, 1 + i % 2, :], pick[0:3 * BC, NS + n, :], bc3[0:3 * BC, h * TH:(h + 1) * TH],
                                 start=True, stop=True).then_inc(bcast_ready, 1)

            def accumulate(i):
                h, n = divmod(i, NS)
                pe.wait_ge(cmul_done, i + 1)
                if h and n == 0:
                    pe.wait_ge(y_half, h)
                for k in range(KI):
                    mm = nc.tensor.matmul(ps[:, 4 + k, :], ident[:, :], hc[:, i % 2, k, :], start=(n == 0), stop=(n == NS - 1))
                mm.then_inc(y_acc, 1)

            def mamba_out(tt):
                pe.wait_ge(ym_ready, (tt // TPH + 1) * KI)
                pe.wait_ge(y_ready, 2 * NT + (tt if tt < TPH else tt - 1))
                for k in range(KI):
                    mm = nc.tensor.matmul(ps[:, out_bank(tt), 0:D], dtx[:, k, tt * P:(tt + 1) * P], w_out[:, k, :],
                                          start=(k == 0), stop=(k == KI - 1))
                mm.then_inc(mout_ready, 1)

            for i in range(NH * NS):
                broadcast(i)
                if i:
                    accumulate(i - 1)
                if NS + 1 <= i <= NS + TPH:
                    mamba_out(i - NS - 1)
            accumulate(NH * NS - 1)
            for tt in range(TPH, NT):
                mamba_out(tt)

            for h in range(NH):
                to_features(2, h)
            pe.wait_ge(ld_router, 2 * DMA)
            pe.wait_ge(feat_ready, 3 * NH)
            for tt in range(NT):
                for k in range(KD):
                    mm = nc.tensor.matmul(ps[:, 5, tt * E:(tt + 1) * E], x_feat[:, k, tt * P:(tt + 1) * P], w_r[:, k, :],
                                          start=(k == 0), stop=(k == KD - 1))
            mm.then_inc(logit_ready, 1)
            pe.wait_ge(zero_ready, 3)
            pe.wait_ge(y_ready, 3 * NT)
            for b in range(NT // 2):
                nc.tensor.matmul(ps[:, b, :], zeros[0:1, 0:P], zeros[0:1, :], start=True, stop=False)

            def expert_up(n):
                e, tt = divmod(n, NT)
                if tt == 0:
                    pe.wait_ge(ld_expert[e % RING], 2 * DMA * (e // RING + 1))
                if n >= 2:
                    pe.wait_ge(eh_ready, n - 1)
                else:
                    pe.wait_ge(r_sub, 1)
                for k in range(KD):
                    mm = nc.tensor.matmul(ps[:, 4 + n % 2, 0:2 * EI], x_feat[:, k, tt * P:(tt + 1) * P], w_gu[:, e % RING, k, :],
                                          start=(k == 0), stop=(k == KD - 1))
                mm.then_inc(egu_ready, 1)

            def expert_transposes(n):
                pe.wait_ge(eh_ready, n + 1)
                if n >= 2:
                    pe.wait_ge(ef_ready, n - 1)
                for c in range(2):
                    mm = nc.tensor.transpose(ps[0:EH, 6 + n % 2, c * P:(c + 1) * P], e_h[:, n % 2, c * EH:(c + 1) * EH], ident[:, :])
                mm.then_inc(eT_ready, 1)

            def expert_down(n):
                e, tt = divmod(n, NT)
                pe.wait_ge(ef_ready, n + 1)
                for c in range(2):
                    mm = nc.tensor.matmul(ps[:, tt // 2, tt % 2 * D:(tt % 2 + 1) * D], e_f[0:EH, n % 2, c, :], w_dn[0:EH, e % RING, c, :],
                                          start=False, stop=(e == EX - 1 and c == 1 and tt % 2 == 1))
                mm.then_inc(edn_ready, 1)

            for n in range(EX * NT + 2):
                if n < EX * NT:
                    expert_up(n)
                if 1 <= n <= EX * NT:
                    expert_transposes(n - 1)
                if n >= 2:
                    expert_down(n - 2)

        @block.scalar
        def _(act):
            act.wait_ge(ld_small, 4 * DMA)
            act.wait_ge(bias_ready, 1)
            for i, (m, h) in enumerate(QK_ORDER):
                act.wait_ge(qk_ready, i + 1)
                bias = b_q4[:, m:m + 1] if m < KD else cols[:, m:m + 1]
                scale = HD ** -0.5 if m < KD else 1.0
                nc.scalar.activation(qk_full[:, i, :], ps[:, i, :], ACT.Identity, bias=bias, scale=scale)
                nc.scalar.activation(qk_part[:, 0, m, h * TH:(h + 1) * TH], ps[:, i, :], ACT.Identity,
                                     bias=bias, scale=scale).then_inc(qk_taken, 1)

            def evacuate(g):
                act.wait_ge(pv_done, NT * (g + 1))
                nc.scalar.activation(o_feat[:, g, :], ps[:, 6:8, :].rearrange("p b n -> p (b n)"),
                                     ACT.Copy).then_inc(o_taken, 1)

            for n in range(NG * NT * G):
                r, g = n // G, n // (G * NT)
                st = r % NT
                act.wait_ge(scores_ready, n + 1)
                if r >= 2:
                    act.wait_ge(pv_done, r - 1)
                elif n == 0:
                    act.wait_ge(parts_out[0], DMA)
                    act.wait_ge(parts_out[1], DMA)
                    act.wait_ge(parts_out[2], DMA)
                    act.wait_ge(parts_out[3], DMA)
                b = 2 + 2 * (n % 2)
                nc.scalar.activation(probs[:, n % 8, st * P:T],
                                     ps[:, b:b + 2, :].rearrange("p b n -> p (b n)")[:, st * P:T],
                                     ACT.Exp).then_inc(probs_ready, 1)
                if r % NT == 0 and n % G == G - 1 and g:
                    evacuate(g - 1)
            evacuate(NG - 1)


            for tt in range(NT):
                act.wait_ge(oN_ready, tt + 1)
                if tt >= 2:
                    act.wait_ge(wo_ready, tt - 1)
                nc.scalar.activation(o_nf[:, tt % 2, :, :], ps[:, 2 + tt % 2, 0:D].rearrange("p (k t) -> p k t", k=KD),
                                     ACT.Copy).then_inc(onf_ready, 1)

            def features(layer, h):
                act.wait_ge(xT_ready, layer * NH + h + 1)
                nc.scalar.activation(x_feat[:, :, h * TH:(h + 1) * TH], ps[:, 6:8, :], ACT.Copy).then_inc(feat_ready, 1)

            def magnitude(n):
                h, b = divmod(n, FB)
                q = n // GS % 2
                act.wait_ge(ffh_ready, n + 1)
                if n >= 2 * GS:
                    act.wait_ge(kept_ready, (n // GS - 1) * GS)
                nc.scalar.activation(ff_a[:, q, b % GS, :], ff_h[:, q, b % GS, :], ACT.Abs).then_inc(abs_ready, 1)

            for h in range(NH):
                features(0, h)
                for b in range(FB):
                    n = h * FB + b
                    act.wait_ge(gu_ready, n + 1)
                    if n >= 2:
                        act.wait_ge(ffh_ready, n - 1)
                    nc.scalar.activation(ff_s[:, n % 2, :], ps[:, 2 * (n % 2), :], ACT.Silu).then_inc(silu_ready, 1)
                    if n:
                        magnitude(n - 1)
            magnitude(NH * FB - 1)

            act.wait_ge(ld_small, 4 * DMA)
            features(1, 0)
            act.wait_ge(down_ready, NT)
            act.wait_ge(zero_ready, 1)
            cw = lambda k, tap: cols[:, COLS["conv_w"][0] + k * TAPS + tap:COLS["conv_w"][0] + k * TAPS + tap + 1]
            cc = lambda name, k: cols[:, COLS[name][0] + k:COLS[name][0] + k + 1]

            def act_x(h):
                t = slice(h * TH, (h + 1) * TH)
                for k in range(KI):
                    act.wait_ge(conv_done, h * KI + k + 1)
                    nc.scalar.activation(xa[:, k, t], xa[:, k, t], ACT.Silu).then_inc(xa_ready, 1)

            for h in range(NH):
                t = slice(h * TH, (h + 1) * TH)
                if h:
                    features(1, h)
                for k in range(KI):
                    act.wait_ge(inx_ready, h * 2 * KI + k + 1)
                    nc.scalar.activation(xa[:, k, t], ps[:, k, :], ACT.Identity, bias=cc("conv_b", k), scale=cw(k, TAPS - 1))
                    nc.scalar.activation(x_in[:, k, TAPS - 1 + h * TH:TAPS - 1 + (h + 1) * TH], ps[:, k, :],
                                         ACT.Copy).then_inc(xin_ready, 1)
                for k in range(KI):
                    act.wait_ge(inx_ready, h * 2 * KI + KI + k + 1)
                    nc.scalar.activation(sz[:, k, t], ps[:, k, :], ACT.Silu).then_inc(z_ready, 1)
                act_x(h)
            nc.scalar.activation(a_neg[:, :, :], cols[:, COLS["a_log"][0]:COLS["a_log"][1]].rearrange("p (k n) -> p k n", k=KI),
                                 ACT.Exp).then_inc(a_exp, 1)
            for i in range(NH * KI):
                h, k = divmod(i, KI)
                act.wait_ge(sp_abs, i + 1)
                if h:
                    act.wait_ge(dt_done, i - KI + 1)
                nc.scalar.activation(sp_e[:, k, :], ps[:, k, :], ACT.Abs, bias=cc("dt_b", k)).then_inc(act_own, 1)
                act.wait_ge(act_own, i + 1)
                nc.scalar.activation(sp_e[:, k, :], sp_e[:, k, :], ACT.Exp, scale=-1.0).then_inc(sp_exp, 1)
                act.wait_ge(sp_w_ready, i + 1)
                nc.scalar.activation(sp_w[:, k, :], sp_w[:, k, :], ACT.Ln).then_inc(sp_ln, 1)
            act.wait_ge(a_ready, 1)
            for i in range(NH * NS):
                h, n = divmod(i, NS)
                act.wait_ge(bcast_ready, i + 1)
                if i >= 2:
                    act.wait_ge(dBx_ready, i - 1)
                else:
                    act.wait_ge(u_done, NH * KI)
                nc.scalar.activation(b_sb[:, i % 2, :], ps[:, 0, :], ACT.Copy).then_inc(b_copied, 1)
                if i >= 2:
                    act.wait_ge(scanned, KI * (i - 1))
                for k in range(KI):
                    nc.scalar.activation(dA[:, i % 2, k, :], dt_[:, k, h * TH:(h + 1) * TH], ACT.Exp,
                                         scale=a_neg[:, k, n:n + 1]).then_inc(dA_ready, 1)
            for h in range(NH):
                features(2, h)
            act.wait_ge(r_sub, 1)
            nc.scalar.activation(r_p[:, :, :], r_p[:, :, :], ACT.Exp).then_inc(r_exp, 1)
            for n in range(EX * NT + 1):
                if n < EX * NT:
                    act.wait_ge(egu_ready, n + 1)
                    if n >= 2:
                        act.wait_ge(eh_ready, n - 1)
                    nc.scalar.activation(e_s[:, n % 2, :], ps[:, 4 + n % 2, 0:EI], ACT.Silu).then_inc(es_ready, 1)
                if n:
                    act.wait_ge(eT_ready, n)
                    if n >= 3:
                        act.wait_ge(edn_ready, n - 2)
                    nc.scalar.activation(e_f[0:EH, (n - 1) % 2, :, :], ps[0:EH, 6 + (n - 1) % 2, 0:2 * P].rearrange("p (c t) -> p c t", c=2),
                                         ACT.Copy).then_inc(ef_ready, 1)

        @block.vector
        def _(dve):
            done = [0]

            def link(ins):
                done[0] += 1
                ins.then_inc(vec_own, 1)
                dve.wait_ge(vec_own, done[0])

            dve.wait_ge(ld_small, 4 * DMA)
            nc.vector.tensor_scalar(b_q4[:, :], cols[:, 0:KD], HD ** -0.5, None, ALU.mult).then_inc(bias_ready, 1)
            for i, (m, h) in enumerate(QK_ORDER):
                t = slice(h * TH, (h + 1) * TH)
                dve.wait_ge(qk_taken, i + 1)
                link(nc.vector.tensor_tensor(qk_full[:, i, :], qk_full[:, i, :], qk_part[:, 0, m, t], ALU.subtract))
                link(nc.vector.tensor_copy(qk_part[:, 1, m, t], qk_full[:, i, :]))
                nc.vector.tensor_tensor(qk_part[:, 2, m, t], qk_full[:, i, :], qk_part[:, 1, m, t],
                                        ALU.subtract).then_inc(parts_ready, 1)
            for tt in range(NT):
                dve.wait_ge(v_ready, tt + 1)
                nc.vector.tensor_tensor(v_aug[:, tt, :, 0:HD], ps[:, tt, 0:D].rearrange("p (h d) -> p h d", h=HEADS),
                                        bias_vo[:, 0, :].rearrange("p (h d) -> p h d", h=HEADS),
                                        ALU.add).then_inc(v_taken, 1)
            for g in range(NG):
                for u, (j, tt, h) in enumerate(UNITS):
                    n = g * (len(UNITS) + 1) + u
                    w = min(TH, (tt + 1) * P - h * TH)
                    dve.wait_ge(max_ready, g * len(UNITS) + u + 1)
                    nc.vector.tensor_reduce(nmax[:, h, tt, j:j + 1], ps[:, n % 2, 0:w], AX.X, ALU.max,
                                            negate=True).then_inc(max_taken, 1)
                dve.wait_ge(max_taken, (g + 1) * len(UNITS))
                link(nc.vector.tensor_tensor(nmax[:, 0, TPH:, :], nmax[:, 0, TPH:, :], nmax[:, 1, TPH:, :], ALU.min))
                link(nc.vector.tensor_copy(nmax_p[:, :, 0, :], nmax[:, 0, :, :]))
                link(nc.vector.tensor_tensor(nmax_r[:, :, :], nmax[:, 0, :, :], nmax_p[:, :, 0, :], ALU.subtract))
                link(nc.vector.tensor_copy(nmax_p[:, :, 1, :], nmax_r[:, :, :]))
                nc.vector.tensor_tensor(nmax_p[:, :, 2, :], nmax_r[:, :, :], nmax_p[:, :, 1, :],
                                        ALU.subtract).then_inc(nmax_parts, 1)
                n = (g + 1) * (len(UNITS) + 1) - 1
                dve.wait_ge(nmaxT_ready, g + 1)
                if g:
                    dve.wait_ge(nmax_loaded[g - 1], SPLIT * DMA)
                nc.vector.tensor_copy(nmax_f[0:SPLIT * G, :], psb[0:SPLIT * G, n % 2, :]).then_inc(nmax_feat, 1)

            def add_residual(source, tt):
                nc.vector.tensor_tensor(y_tok[:, tt, :], source, x_tok[:, tt, :], ALU.add).then_inc(y_ready, 1)

            def statistics(layer, h):
                tts = range(h * TPH, (h + 1) * TPH)
                dve.wait_ge(y_ready, layer * NT + (h + 1) * TPH)
                for tt in tts:
                    last = nc.vector.bn_stats(stats[:, tt, :], y_tok[:, tt, :])
                link(last)
                for tt in tts:
                    last = nc.vector.bn_aggr(mv[:, tt, :], stats[:, tt, :])
                link(last)
                nc.vector.tensor_scalar(mv[:, h * TPH:(h + 1) * TPH, 1], mv[:, h * TPH:(h + 1) * TPH, 1], EPS, None,
                                        ALU.add).then_inc(stats_ready, 1)

            def normalise(layer, h):
                dve.wait_ge(rstd_ready, layer * NH + h + 1)
                for tt in range(h * TPH, (h + 1) * TPH):
                    nc.vector.tensor_scalar(x_tok[:, tt, :], y_tok[:, tt, :], mv[:, tt, 0:1], rstd[:, tt:tt + 1],
                                            ALU.subtract, ALU.mult).then_inc(norm_ready, 1)

            dve.wait_ge(xb_ready, 1)

            def divide(tt):
                heads = ps[:, tt % 2, :].rearrange("p (h c) -> p h c", h=HEADS)
                dve.wait_ge(oT_ready, tt + 1)
                link(nc.vector.reciprocal(rden[:, tt % 2, :], heads[:, :, HD]))
                if tt >= 2:
                    dve.wait_ge(oN_ready, tt - 1)
                nc.vector.tensor_tensor(o_tok[:, tt % 2, :].rearrange("p (h c) -> p h c", h=HEADS), heads[:, :, 0:HD],
                                        rden[:, tt % 2, :].unsqueeze(2).broadcast_to([P, HEADS, HD]), ALU.mult).then_inc(o_norm, 1)

            for i in range(NT + 2):
                if i < NT:
                    divide(i)
                if i >= 2:
                    tt = i - 2
                    dve.wait_ge(wo_ready, tt + 1)
                    add_residual(ps[:, 4 + tt % 2, 0:D], tt)
                    if tt == TPH - 1:
                        statistics(0, 0)
                        normalise(0, 0)
            statistics(0, 1)
            normalise(0, 1)

            def keep_two(q):
                hb, ab = ff_h[:, q % 2, :, :], ff_a[:, q % 2, :, :]
                dve.wait_ge(abs_ready, GS * (q + 1))
                nc.vector.tensor_tensor(ff_c[:, 0:3, :], ab[:, 0, :].unsqueeze(1).broadcast_to([P, 3, TH]), ab[:, 1:4, :], ALU.is_ge)
                nc.vector.tensor_tensor(ff_c[:, 3:5, :], ab[:, 1, :].unsqueeze(1).broadcast_to([P, 2, TH]), ab[:, 2:4, :], ALU.is_ge)
                link(nc.vector.tensor_tensor(ff_c[:, 5, :], ab[:, 2, :], ab[:, 3, :], ALU.is_ge))
                for j, (x, y) in enumerate(((0, 1), (3, 4), (1, 3), (2, 4))):
                    last = nc.vector.tensor_tensor(ff_w[:, j, :], ff_c[:, x, :], ff_c[:, y, :], ALU.add)
                link(last)
                nc.vector.tensor_tensor(ff_w[:, 0, :], ff_w[:, 0, :], ff_c[:, 2, :], ALU.add)
                nc.vector.tensor_tensor(ff_w[:, 1, :], ff_w[:, 1, :], ff_c[:, 0, :], ALU.subtract)
                nc.vector.tensor_tensor(ff_w[:, 2, :], ff_c[:, 5, :], ff_w[:, 2, :], ALU.subtract)
                link(nc.vector.tensor_tensor(ff_w[:, 3, :], ff_w[:, 3, :], ff_c[:, 5, :], ALU.add))
                h, gb = divmod(q, 2)
                for j, (bound, op) in enumerate(((1.5, ALU.is_ge), (0.5, ALU.is_ge), (-0.5, ALU.is_ge), (1.5, ALU.is_le))):
                    nc.vector.scalar_tensor_tensor(out=ff_k[:, gb * GS + j, h * TH:(h + 1) * TH], in0=ff_w[:, j, :], scalar=bound,
                                                   in1=hb[:, j, :], op0=op, op1=ALU.mult).then_inc(kept_ready, 1)

            for n in range(NH * FB):
                dve.wait_ge(silu_ready, n + 1)
                if n >= 2 * GS:
                    dve.wait_ge(kept_ready, (n // GS - 1) * GS)
                nc.vector.tensor_tensor(ff_h[:, n // GS % 2, n % GS, :], ff_s[:, n % 2, :], ps[:, 2 * (n % 2) + 1, :],
                                        ALU.mult).then_inc(ffh_ready, 1)
                if n % GS == GS - 2 and n > GS:
                    keep_two(n // GS - 1)
            keep_two(NH * FB // GS - 1)
            for h in range(NH):
                for tt in range(h * TPH, (h + 1) * TPH):
                    dve.wait_ge(down_ready, tt + 1)
                    add_residual(ps[:, 4 + tt % 2, 0:D], tt)
                statistics(1, h)
                normalise(1, h)

            cw = lambda k, tap: cols[:, COLS["conv_w"][0] + k * TAPS + tap:COLS["conv_w"][0] + k * TAPS + tap + 1]
            cc = lambda name, k: cols[:, COLS[name][0] + k:COLS[name][0] + k + 1]
            for h in range(NH):
                t = slice(h * TH, (h + 1) * TH)
                for k in range(KI):
                    dve.wait_ge(xin_ready, h * KI + k + 1)
                    for tap in range(TAPS - 1):
                        ins = nc.vector.scalar_tensor_tensor(out=xa[:, k, t], in0=x_in[:, k, h * TH + tap:h * TH + tap + TH],
                                                             scalar=cw(k, tap), in1=xa[:, k, t], op0=ALU.mult, op1=ALU.add)
                        if tap < TAPS - 2:
                            link(ins)
                    ins.then_inc(conv_done, 1)
            dve.wait_ge(a_exp, 1)
            nc.vector.tensor_scalar(a_neg[:, :, :], a_neg[:, :, :], -1.0, None, ALU.mult).then_inc(a_ready, 1)
            for h in range(NH):
                t = slice(h * TH, (h + 1) * TH)
                xd = ps[:, 4 + h, :]
                dve.wait_ge(xd_ready, h + 1)
                nc.vector.tensor_copy(dt_lo[3 * BC:XD, t], xd[3 * BC:XD, :]).then_inc(dt_ready, 1)
                link(nc.vector.tensor_copy(bc_p[0:3 * BC, 0, :], xd[0:3 * BC, :]))
                link(nc.vector.tensor_tensor(bc_r[0:3 * BC, :], xd[0:3 * BC, :], bc_p[0:3 * BC, 0, :], ALU.subtract))
                link(nc.vector.tensor_copy(bc_p[0:3 * BC, 1, :], bc_r[0:3 * BC, :]))
                link(nc.vector.tensor_tensor(bc3[0:3 * BC, t], bc_r[0:3 * BC, :], bc_p[0:3 * BC, 1, :], ALU.subtract))
                nc.vector.tensor_copy(bc3[0:BC, t], bc_p[0:BC, 0, :])
                last = nc.vector.tensor_copy(bc3[BC:2 * BC, t], bc_p[BC:2 * BC, 1, :])
                last.then_inc(bc_ready, 1)
                dve.wait_ge(bc_ready, h + 1)
            for i in range(NH * KI):
                h, k = divmod(i, KI)
                t = slice(h * TH, (h + 1) * TH)
                dve.wait_ge(sp_exp, i + 1)
                link(nc.vector.tensor_scalar(sp_d[:, k, :], sp_e[:, k, :], 1.0, None, ALU.add))
                nc.vector.tensor_copy(sp_w[:, k, :], sp_d[:, k, :]).then_inc(sp_w_ready, 1)
                link(nc.vector.scalar_tensor_tensor(out=sp_d[:, k, :], in0=sp_d[:, k, :], scalar=-1.0, in1=sp_e[:, k, :],
                                                    op0=ALU.add, op1=ALU.subtract))
                nc.vector.tensor_scalar(dt_[:, k, t], ps[:, k, :], cc("dt_b", k), 0.0, ALU.add, ALU.max).then_inc(sp_d_ready, 1)
                dve.wait_ge(sp_d_ready, i + 1)
                link(nc.vector.tensor_tensor(dt_[:, k, t], dt_[:, k, t], sp_d[:, k, :], ALU.subtract))
                dve.wait_ge(sp_ln, i + 1)
                nc.vector.tensor_tensor(dt_[:, k, t], dt_[:, k, t], sp_w[:, k, :], ALU.add).then_inc(dt_done, 1)
            for i in range(NH * NS):
                h, n = divmod(i, NS)
                dve.wait_ge(dBx_ready, i + 1)
                for k in range(KI):
                    dve.wait_ge(dA_ready, KI * i + k + 1)
                    nc.vector.tensor_tensor_scan(hs[:, i % 2, k, :], dA[:, i % 2, k, :], dBx[:, i % 2, k, :],
                                                 h_last[:, k, n:n + 1] if h else 0.0, ALU.mult, ALU.add).then_inc(scanned, 1)
                dve.wait_ge(scanned, KI * (i + 1))
                if h < NH - 1:
                    nc.vector.tensor_copy(h_last[:, :, n], hs[:, i % 2, :, TH - 1])
                if i >= 2:
                    dve.wait_ge(y_acc, i - 1)
                nc.vector.tensor_tensor(hc[:, i % 2, :, :], hs[:, i % 2, :, :],
                                        ps[:, 1 + i % 2, :].unsqueeze(1).broadcast_to([P, KI, TH]), ALU.mult).then_inc(cmul_done, 1)
                if n == NS - 1:
                    t = slice(h * TH, (h + 1) * TH)
                    dve.wait_ge(y_acc, i + 1)
                    for k in range(KI):
                        ins = nc.vector.scalar_tensor_tensor(out=dtx[:, k, t], in0=xa[:, k, t], scalar=cc("skip", k),
                                                             in1=ps[:, 4 + k, :], op0=ALU.mult, op1=ALU.add)
                    ins.then_inc(y_half, 1)
                    dve.wait_ge(y_half, h + 1)
                    for k in range(KI):
                        nc.vector.tensor_tensor(dtx[:, k, t], dtx[:, k, t], sz[:, k, t], ALU.mult).then_inc(ym_ready, 1)
                if i >= NS + 1 and i < NS + 1 + TPH:
                    tt = i - NS - 1
                    dve.wait_ge(mout_ready, tt + 1)
                    add_residual(ps[:, out_bank(tt), 0:D], tt)
                if i == NS + 5:
                    statistics(2, 0)
                if i == NS + 8:
                    normalise(2, 0)
            for tt in range(TPH, NT):
                dve.wait_ge(mout_ready, tt + 1)
                add_residual(ps[:, out_bank(tt), 0:D], tt)
            statistics(2, 1)
            normalise(2, 1)

            logits = ps[:, 5, 0:NT * E].rearrange("p (t e) -> p t e", t=NT)
            wide = lambda x: x.broadcast_to([P, NT, E])
            dve.wait_ge(logit_ready, 1)
            link(nc.vector.tensor_reduce(r_max[:, :], logits, AX.X, ALU.max))
            nc.vector.tensor_tensor(r_p[:, :, :], logits, wide(r_max[:, :].unsqueeze(2)), ALU.subtract).then_inc(r_sub, 1)
            dve.wait_ge(r_exp, 1)
            link(nc.vector.tensor_reduce(r_max[:, :], r_p[:, :, :], AX.X, ALU.add))
            link(nc.vector.reciprocal(r_max[:, :], r_max[:, :]))
            link(nc.vector.tensor_tensor(r_p[:, :, :], r_p[:, :, :], wide(r_max[:, :].unsqueeze(2)), ALU.mult))
            for tt in range(NT):
                last = nc.vector.max(r_8[:, tt, :], r_p[:, tt, :])
            link(last)
            for tt in range(NT):
                last = nc.vector.max_index(r_i[:, tt, :].bitcast(U32), r_8[:, tt, :], r_p[:, tt, :])
            link(last)
            link(nc.vector.tensor_copy(r_if[:, :, :], r_i[:, :, :].bitcast(U32)))
            dve.wait_ge(ld_router, 2 * DMA)
            experts = iota_e[:, :].unsqueeze(1).broadcast_to([P, NT, E])
            nc.vector.tensor_tensor(r_m[:, :, :], experts, wide(r_if[:, :, 0:1]), ALU.is_equal)
            link(nc.vector.tensor_tensor(r_q[:, :, :], experts, wide(r_if[:, :, 1:2]), ALU.is_equal))
            link(nc.vector.tensor_tensor(r_m[:, :, :], r_m[:, :, :], r_q[:, :, :], ALU.add))
            dve.wait_ge(zero_ready, 2)
            link(nc.vector.tensor_tensor(combine[:, :, 0:E], r_m[:, :, :], r_p[:, :, :], ALU.mult))
            for n in range(EX * NT):
                e, tt = divmod(n, NT)
                dve.wait_ge(es_ready, n + 1)
                if n >= 2:
                    dve.wait_ge(eT_ready, n - 1)
                nc.vector.scalar_tensor_tensor(out=e_h[:, n % 2, :], in0=e_s[:, n % 2, :], scalar=combine[:, tt, e:e + 1],
                                               in1=ps[:, 4 + n % 2, EI:2 * EI], op0=ALU.mult, op1=ALU.mult).then_inc(eh_ready, 1)
            for h in range(NH):
                for tt in range(h * TPH, (h + 1) * TPH):
                    dve.wait_ge(edn_ready, EX * NT)
                    add_residual(ps[:, tt // 2, tt % 2 * D:(tt % 2 + 1) * D], tt)
                statistics(3, h)
                normalise(3, h)


def host_arrays(v):
    bits = lambda w: (w.astype(np.float32).view(np.uint32) >> 16).astype(np.uint16)
    f = lambda x: np.asarray(x)
    c = np.ascontiguousarray
    tiles = lambda w: c(w.reshape(-1, P, w.shape[1]).transpose(1, 0, 2))
    x = f(v["L0_attn_x"])[0]
    order = np.arange(D).reshape(KD, HPT, HD).transpose(0, 2, 1).ravel()
    order = np.concatenate([order, D + order, 2 * D + np.arange(D)])
    wqkv, bqkv = f(v["L0_attn_Wqkv"])[:, order], f(v["L0_attn_bqkv"])[order]
    key, query = np.arange(P)[:, None], np.arange(P)[None, :]
    cols = np.zeros((P, NCOLS), np.float32)
    put = lambda n, w: cols.__setitem__((slice(None), slice(*COLS[n])), w)
    put("b_qk", bqkv[:2 * D].reshape(4, P).T)
    colt = lambda w: w.reshape(KI, P, -1).transpose(1, 0, 2).reshape(P, -1)
    put("conv_w", colt(f(v["L1_attn_conv_w"])))
    put("conv_b", colt(f(v["L1_attn_conv_b"])))
    put("dt_b", colt(f(v["L1_attn_dt_proj_b"])))
    put("skip", colt(f(v["L1_attn_D"])))
    put("a_log", colt(f(v["L1_attn_A_log"])))
    bias_vo = np.broadcast_to(np.stack([bqkv[2 * D:], f(v["L0_attn_bo"])])[None], (P, 2, D))
    ffc = np.arange(FF).reshape(2, P, GS).transpose(0, 2, 1).ravel()
    blocks = lambda w: c(w[:, ffc].reshape(KD, P, FB, P).transpose(1, 0, 2, 3))
    xp = f(v["L1_attn_x_proj_w"]).T
    xp = np.concatenate([xp[:, RANK:]] * 3 + [xp[:, :RANK]], 1)
    pick = np.zeros((3, BC, BC, P), np.float32)
    pick[:, np.arange(BC), np.arange(BC)] = 1.0
    sgu, sdn = f(v["L1_ffn_shared_gate_up"]), f(v["L1_ffn_shared_down"])
    half = lambda w, s: w[:, s * EI:(s + 1) * EI]
    w_gu = np.stack(list(f(v["L1_ffn_w_gate_up"])) +
                    [np.concatenate([half(sgu, s), half(sgu, SHARED + s)], 1) for s in range(SHARED)])
    w_dn = np.stack(list(f(v["L1_ffn_w_down"])) + [sdn[s * EI:(s + 1) * EI] for s in range(SHARED)])
    return {
        "w_g": blocks(f(v["L0_ffn_w_gate"])), "w_u": blocks(f(v["L0_ffn_w_up"])), "w_d": tiles(f(v["L0_ffn_w_down"])[ffc]),
        "w_in": tiles(c(f(v["L1_attn_in_proj_w"]).T)), "w_xp": tiles(xp), "w_dt": c(f(v["L1_attn_dt_proj_w"]).T),
        "pick": bits(pick.reshape(3 * BC, BC, P)), "w_out": tiles(c(f(v["L1_attn_out_proj_w"]).T)),
        "w_r": tiles(c(f(v["L1_ffn_gate_w"]).T)), "iota_e": np.broadcast_to(np.arange(E, dtype=np.float32), (P, E)).copy(),
        "w_gu": c(w_gu.reshape(EX, KD, P, 2 * EI).transpose(0, 2, 1, 3)),
        "w_dn": c(w_dn.reshape(EX, 2, EH, D).transpose(0, 2, 1, 3)),
        "x_feat": tiles(c(x.T)), "x_tok": tiles(x), "w_qkv": tiles(wqkv), "cols": cols,
        "bias_vo": c(bias_vo), "w_o": tiles(f(v["L0_attn_Wo"])),
        "masks": bits(np.stack([np.eye(P), np.where(query < key, -30000.0, 0.0)], 1)),
        "ident": np.eye(P, dtype=np.float32),
    }


def kernel(**inputs):
    import concourse.bacc as _bacc
    from concourse import mybir as _mybir
    from concourse.bass_utils import run_bass_kernel_spmd as _run

    nc = _bacc.Bacc("TRN2", target_bir_lowering=False, num_devices=1)
    arrays, args = {}, {}
    for name, array in host_arrays(inputs).items():
        arrays["in_" + name] = array
        args[name] = nc.dram_tensor("in_" + name, array.shape, _mybir.dt.from_np(array.dtype), kind="ExternalInput").ap()
    out = nc.dram_tensor("out", (1, T, D), _mybir.dt.float32, kind="ExternalOutput").ap()
    scratch = nc.dram_tensor("scratch", [2 * KD, SPLIT, P, T], _mybir.dt.bfloat16).ap()
    build(nc, args, out.rearrange("a (t p) d -> p (a t) d", p=P), scratch)
    r = _run(nc, [arrays], core_ids=[0])
    return r.results[0]["out"]
```

```python
from contextlib import ExitStack

import numpy as np

import concourse.bass as bass
from concourse import mybir

F32 = mybir.dt.float32
BF16 = mybir.dt.bfloat16
U32 = mybir.dt.uint32
I32 = mybir.dt.int32
ALU = mybir.AluOpType
ACT = mybir.ActivationFunctionType
AX = mybir.AxisListType

P = 128
T = 1024
NT = T // P
TH = 512
NH = T // TH
TPH = TH // P
D = 256
KD = D // P
HEADS = 16
HD = D // HEADS
HPT = HEADS // KD
G = 4
NG = HEADS // G
VC = 32
SPLIT = 3
KROWS = 6 * HD
KX = KROWS + SPLIT
EPS = 1e-5
FF = 1024
FB = FF // P
GS = 4
DI = 512
KI = DI // P
NS = 16
RANK = 16
BC = 2 * NS
XD = 3 * BC + RANK
TAPS = 4
E = 16
EI = 176
EH = EI // 2
SHARED = 2
TOP = 2
SLOTS = (TOP * T - E) // P + E
RING = 4
DMA = 16

QK_ORDER = [(0, 0), (2, 0), (1, 0), (3, 0), (0, 1), (2, 1), (1, 1), (3, 1)]
PHASES = [(h, g) for h in range(NH) for g in range(NG)]
RB = 3


def heads_of(w):
    n = {P: 4, 2 * P: 2}.get(w, 1)
    return [list(range(j, j + n)) for j in range(0, G, n)]


def max_jobs(phase):
    h, g = PHASES[phase]
    tiles = [(h * TPH + i, half, TH if half < h else (i + 1) * P) for i in range(TPH) for half in range(h + 1)]
    return [(phase, tt, half, w, js) for tt, half, w in tiles for js in heads_of(w)]


def score_jobs(phase):
    h, g = PHASES[phase]
    tiles = [(st, min(TH, (h + 1) * TH - st * P)) for st in range((h + 1) * TPH)]
    return [(phase, st, w, js) for st, w in tiles for js in heads_of(w)]


def first_round(phase):
    return sum((h + 1) * TPH for h, _ in PHASES[:phase])


MAX = []
for _phase in range(len(PHASES)):
    MAX += max_jobs(_phase)
_late = 4
for _phase in range(len(PHASES)):
    _last = max(i for i, m in enumerate(MAX) if m[0] == _phase and len(m) > 1)
    MAX.insert(min(_last + _late, len(MAX)) if _phase < len(PHASES) - 1 else len(MAX), (_phase,))
SCORES = [job for phase in range(len(PHASES)) for job in score_jobs(phase)]
columns = lambda job: job[-2] * len(job[-1]) if len(job) > 1 else 0


def max_jobs_before(score):
    done = sum(columns(m) for m in SCORES[:score])
    block = G * P
    target = min(16 * block + done * 3 // 2, done + 34 * block)
    n, seen = 0, 0
    while n < len(MAX) and (seen < target or len(MAX[n]) == 1):
        seen += columns(MAX[n])
        n += 1
    need = 1 + next(i for i, m in enumerate(MAX) if m == (SCORES[score][0],))
    return max(n, need)


COLS = {"b_qk": (0, 4), "conv_w": (4, 20), "conv_b": (20, 24), "dt_b": (24, 28), "skip": (28, 32),
        "a_log": (32, 32 + KI * NS)}
NCOLS = 32 + KI * NS


def out_bank(tt):
    return 3 if tt < TPH else 2 + tt % 2


def in_steps(engine, step, steps):
    peeled = 2 * RING
    turns = (SLOTS - peeled) // RING
    for n in range(peeled):
        step(n, n // RING, n % RING)
    with engine.Fori(0, turns) as j:
        for b in range(RING):
            step(j * RING + (peeled + b), j + peeled // RING, b)
    for n in range(peeled + turns * RING, steps):
        step(n, n // RING, n % RING)


def tile_of(rows, n):
    return rows[bass.ds(n, 1), :, :].rearrange("s p d -> p (s d)")


def has_tile(n):
    return not isinstance(n, int) or 0 <= n < SLOTS


def counts(n):
    return not isinstance(n, int) or n > 0


def build(nc, a, out, scratch, slots, results):
    ctx = ExitStack()
    with ctx:
        def sb(name, shape, dt=F32):
            return ctx.enter_context(nc.sbuf_tensor(name, shape, dt))

        def sem(name):
            return ctx.enter_context(nc.semaphore(name))

        ps = ctx.enter_context(nc.psum_tensor("ps", [P, 8, TH], F32))
        psb = ps[:, :, :].rearrange("p b n -> p (b n)").bitcast(BF16).rearrange("p (b n) -> p b n", b=8)

        ident = sb("ident", [P, P])
        masks = sb("masks", [P, 4, P], BF16)
        identb, causal, earlier, all_ones = (masks[:, i, :] for i in range(4))
        zero_row = sb("zero_row", [P, D])
        cols = sb("cols", [P, NCOLS])
        x_tok = sb("x_tok", [P, NT, D])
        y_tok = sb("y_tok", [P, NT, D])
        x_feat = sb("x_feat", [P, KD, T])
        stats = sb("stats", [P, NT, 6])
        mv = sb("mv", [P, NT, 2])
        rstd = sb("rstd", [P, NT])
        minus_half = sb("minus_half", [P, NT])

        ARENA = 46100
        arena = sb("arena", [P, ARENA])
        at = [0]

        def take(words):
            lo = at[0]
            at[0] += words
            assert at[0] <= ARENA, at[0]
            return arena[:, lo:lo + words]

        def take_b(n):
            return take(n // 2).bitcast(BF16)

        w_g = take(KD * FF).rearrange("p (k b n) -> p k b n", k=KD, b=FB)
        w_u = take(KD * FF).rearrange("p (k b n) -> p k b n", k=KD, b=FB)
        w_d = take(FB * D).rearrange("p (b n) -> p b n", b=FB)
        w_o = take(KD * D).rearrange("p (k n) -> p k n", k=KD)
        o_feat = take(NG * T).rearrange("p (g t) -> p g t", g=NG)
        rden = take(2 * HEADS).rearrange("p (b h) -> p b h", b=2)
        o_tok = take(2 * D).rearrange("p (b d) -> p b d", b=2)
        o_nf = take(2 * D).rearrange("p (b k t) -> p b k t", b=2, k=KD)
        after_attention = at[0]
        w_qkv = take(KD * 3 * D).rearrange("p (k n) -> p k n", k=KD)
        bias_vo = take(2 * D).rearrange("p (b n) -> p b n", b=2)
        b_q4 = take(KD)
        nmax = take(NH * NT * G).rearrange("p (h t j) -> p h t j", h=NH, t=NT)
        nmax_r = take(TPH * G).rearrange("p (t j) -> p t j", t=TPH)
        nmax_p = take_b(2 * TPH * SPLIT * G).rearrange("p (b t c j) -> p b t c j", b=2, t=TPH, c=SPLIT)
        nmax_f = take_b(2 * TH).rearrange("p (b t) -> p b t", b=2)
        v_aug = take(NT * HEADS * VC).rearrange("p (s h c) -> p s h c", s=NT, h=HEADS)
        q_st = take_b(NH * HEADS * TH).rearrange("p (a h t) -> p a h t", a=NH, h=HEADS)
        k_st = take_b(NH * HEADS * TH).rearrange("p (a h t) -> p a h t", a=NH, h=HEADS)
        overlay = at[0]
        qk_full = take(8 * TH).rearrange("p (i t) -> p i t", i=8)
        qk_part = take_b(SPLIT * 4 * T).rearrange("p (c m t) -> p c m t", c=SPLIT, m=4)
        at[0] = overlay
        probs = take(3 * G * TH).rearrange("p (b j t) -> p b j t", b=3, j=G)

        assert at[0] <= ARENA
        at[0] = after_attention
        ff_s = take(2 * TH).rearrange("p (b t) -> p b t", b=2)
        ff_h = take(2 * GS * TH).rearrange("p (b j t) -> p b j t", b=2, j=GS)
        ff_a = take(2 * GS * TH).rearrange("p (b j t) -> p b j t", b=2, j=GS)
        ff_c = take_b(6 * TH).rearrange("p (c t) -> p c t", c=6)
        ff_w = take_b(GS * TH).rearrange("p (j t) -> p j t", j=GS)
        ff_k = take(FB * T).rearrange("p (b t) -> p b t", b=FB)
        at[0] = ARENA - (KD * 2 * DI + KI * D + KI * XD + DI + BC * P // 2)
        assert at[0] >= after_attention + 20480
        mamba_top = at[0]
        w_in = take(KD * 2 * DI).rearrange("p (k n) -> p k n", k=KD)
        w_out = take(KI * D).rearrange("p (k n) -> p k n", k=KI)
        w_xp = take(KI * XD).rearrange("p (k n) -> p k n", k=KI)
        w_dt = take(DI)
        pick = take_b(BC * P).rearrange("p (r n) -> p r n", r=BC)
        at[0] = 0
        ws_gu = take(SHARED * KD * 2 * EI).rearrange("p (b k n) -> p b k n", b=SHARED, k=KD)
        ws_dn = take(SHARED * 2 * D).rearrange("p (b k n) -> p b k n", b=SHARED, k=2)
        w_r = take(KD * E).rearrange("p (k e) -> p k e", k=KD)
        e_s = take(2 * EI).rearrange("p (b n) -> p b n", b=2)
        e_h = take(2 * EI).rearrange("p (b n) -> p b n", b=2)
        e_f = take(2 * 2 * P).rearrange("p (b c t) -> p b c t", b=2, c=2)
        r_p = take(NT * E).rearrange("p (t e) -> p t e", t=NT)
        chosen = take(TOP * NT * E).rearrange("p (c t e) -> p c t e", c=TOP, t=NT)
        chosen_any = take_b(NT * E)
        r_q = take(TOP * NT * E).rearrange("p (c t e) -> p c t e", c=TOP, t=NT)
        r_max = take(NT)
        r_8 = take(NT * 8).rearrange("p (t e) -> p t e", t=NT)
        r_i = take(NT * 8).rearrange("p (t e) -> p t e", t=NT)
        r_if = take(NT * 8).rearrange("p (t e) -> p t e", t=NT)
        iota = take(E + NT + SLOTS)
        iota_e, fill_steps, iota_slot = iota[:, 0:E], iota[:, E:E + NT], iota[:, E + NT:]
        per_tile = take(E * NT)
        ones_r = take(E * NT)
        upto = take(E * NT)
        before = take(E * NT).rearrange("p (e t) -> p e t", e=E)
        place = take(NT * E).rearrange("p (t e) -> p t e", t=NT)
        count = take(E)
        tiles_of = take(E)
        end_tile = take(E)
        base = take(E)
        position_f = take(TOP * NT).rearrange("p (c t) -> p c t", c=TOP)
        position = take(TOP * NT).bitcast(U32).rearrange("p (c t) -> p c t", c=TOP)
        slot_f = take(SLOTS)
        slot_expert = take(SLOTS).bitcast(I32)
        bc3 = take_b(T)
        a_neg = take(KI * NS).rearrange("p (k n) -> p k n", k=KI)
        h_last = take(KI * NS).rearrange("p (k n) -> p k n", k=KI)
        dtx = take(KI * T).rearrange("p (k t) -> p k t", k=KI)
        slots_at = at[0]
        xa = take(KI * T).rearrange("p (k t) -> p k t", k=KI)
        sz = take(KI * T).rearrange("p (k t) -> p k t", k=KI)
        dt_ = take(KI * T).rearrange("p (k t) -> p k t", k=KI)
        scan_at = at[0]
        assert scan_at + 8 * KI * TH + 2 * TH <= mamba_top, (scan_at + 8 * KI * TH + 2 * TH, mamba_top)
        b_sb = take(2 * TH).rearrange("p (b t) -> p b t", b=2)
        dA = take(2 * KI * TH).rearrange("p (b k t) -> p b k t", b=2, k=KI)
        dBx = take(2 * KI * TH).rearrange("p (b k t) -> p b k t", b=2, k=KI)
        hs = take(2 * KI * TH).rearrange("p (b k t) -> p b k t", b=2, k=KI)
        hc = take(2 * KI * TH).rearrange("p (b k t) -> p b k t", b=2, k=KI)
        at[0] = scan_at
        x_in = take(KI * (T + TAPS - 1) + 4)[:, 0:KI * (T + TAPS - 1)].rearrange("p (k t) -> p k t", k=KI)
        bc_p = take_b(2 * TH).rearrange("p (c t) -> p c t", c=2)
        bc_r = take(TH)
        dt_lo = take(T)
        sp_e = take(KI * TH).rearrange("p (k t) -> p k t", k=KI)
        sp_w = take(KI * TH).rearrange("p (k t) -> p k t", k=KI)
        sp_d = take(KI * TH).rearrange("p (k t) -> p k t", k=KI)
        assert at[0] <= mamba_top
        at[0] = slots_at
        w_gu = take(E * KD * 2 * EI).rearrange("p (e k n) -> p e k n", e=E, k=KD)
        w_dn = take(E * 2 * D).rearrange("p (e k n) -> p e k n", e=E, k=2)
        slot_x = take(RING * D).rearrange("p (b d) -> p b d", b=RING)
        slot_y = take(RING * D).rearrange("p (b d) -> p b d", b=RING)
        slot_xf = take(2 * D).rearrange("p (b k t) -> p b k t", b=2, k=KD)
        picked_flat = take(TOP * NT * D)
        picked = picked_flat.rearrange("p (c t d) -> p c t d", c=TOP, t=NT)
        assert at[0] <= mamba_top

        ld_x = sem("ld_x")
        ld_wqkv = sem("ld_wqkv")
        ld_small = sem("ld_small")
        ld_tok = sem("ld_tok")
        ld_wo = sem("ld_wo")
        parts_out = [sem(f"parts_out{i}") for i in range(len(QK_ORDER))]
        st_loaded = [sem(f"st_loaded{i}") for i in range(NH * KD)]
        nmax_loaded = [sem(f"nmax_loaded{i}") for i in range(len(PHASES))]
        stored = sem("stored")
        bias_ready = sem("bias_ready")
        qk_ready = sem("qk_ready")
        qk_taken = sem("qk_taken")
        qk_rest = sem("qk_rest")
        qk_mid = sem("qk_mid")
        parts_ready = sem("parts_ready")
        v_ready = sem("v_ready")
        v_taken = sem("v_taken")
        ones_ready = sem("ones_ready")
        max_ready = sem("max_ready")
        max_taken = sem("max_taken")
        nmax_parts = sem("nmax_parts")
        nmaxT_ready = sem("nmaxT_ready")
        nmax_feat = sem("nmax_feat")
        scores_ready = sem("scores_ready")
        probs_ready = sem("probs_ready")
        pv_done = sem("pv_done")
        o_taken = sem("o_taken")
        vec_own = sem("vec_own")
        ld_ffw = sem("ld_ffw")
        ld_mamba = sem("ld_mamba")
        ld_router = sem("ld_router")
        xb_ready = sem("xb_ready")
        oT_ready = sem("oT_ready")
        o_norm = sem("o_norm")
        oN_ready = sem("oN_ready")
        onf_ready = sem("onf_ready")
        wo_ready = sem("wo_ready")
        y_ready = sem("y_ready")
        stats_ready = sem("stats_ready")
        rstd_ready = sem("rstd_ready")
        norm_ready = sem("norm_ready")
        xT_ready = sem("xT_ready")
        feat_ready = sem("feat_ready")
        gu_ready = sem("gu_ready")
        silu_ready = sem("silu_ready")
        ffh_ready = sem("ffh_ready")
        abs_ready = sem("abs_ready")
        kept_ready = sem("kept_ready")
        down_ready = sem("down_ready")
        inx_ready = sem("inx_ready")
        xin_ready = sem("xin_ready")
        xacc_ready = sem("xacc_ready")
        conv_done = sem("conv_done")
        xa_ready = sem("xa_ready")
        z_ready = sem("z_ready")
        xd_ready = sem("xd_ready")
        bc_ready = sem("bc_ready")
        dt_ready = sem("dt_ready")
        sp_abs = sem("sp_abs")
        sp_exp = sem("sp_exp")
        sp_w_ready = sem("sp_w_ready")
        sp_ln = sem("sp_ln")
        sp_d_ready = sem("sp_d_ready")
        dt_done = sem("dt_done")
        u_done = sem("u_done")
        a_exp = sem("a_exp")
        a_ready = sem("a_ready")
        b_ready = sem("b_ready")
        c_ready = sem("c_ready")
        b_copied = sem("b_copied")
        dA_ready = sem("dA_ready")
        dBx_ready = sem("dBx_ready")
        scanned = sem("scanned")
        cmul_done = sem("cmul_done")
        y_acc = sem("y_acc")
        y_half = sem("y_half")
        ym_ready = sem("ym_ready")
        mout_ready = sem("mout_ready")
        logit_ready = sem("logit_ready")
        r_sub = sem("r_sub")
        r_exp = sem("r_exp")
        choice_ready = sem("choice_ready")
        rank_ready = sem("rank_ready")
        position_ready = sem("position_ready")
        slot_expert_ready = sem("slot_expert_ready")
        slots_zeroed = sem("slots_zeroed")
        scattered = sem("scattered")
        shared_added = sem("shared_added")
        slot_xT_ready = sem("slot_xT_ready")
        slot_xf_ready = sem("slot_xf_ready")
        slot_gu_ready = sem("slot_gu_ready")
        slot_silu_ready = sem("slot_silu_ready")
        slot_h_ready = sem("slot_h_ready")
        slot_hT_ready = sem("slot_hT_ready")
        slot_hf_ready = sem("slot_hf_ready")
        slot_down_ready = sem("slot_down_ready")
        slot_y_ready = sem("slot_y_ready")
        slot_loaded = [sem(f"slot_loaded{i}") for i in range(RING)]
        slot_stored = [sem(f"slot_stored{i}") for i in range(RING)]
        picked_ready = [sem(f"picked_ready{i}") for i in range(NT)]
        zero_ready = sem("zero_ready")
        egu_ready = sem("egu_ready")
        es_ready = sem("es_ready")
        eh_ready = sem("eh_ready")
        eT_ready = sem("eT_ready")
        ef_ready = sem("ef_ready")
        edn_ready = sem("edn_ready")
        act_own = sem("act_own")
        ld_shared = sem("ld_shared")
        ld_experts = sem("ld_experts")
        block = ctx.enter_context(nc.Block())

        @block.sync
        def _(sp):
            for k in range(KD):
                sp.dma_start(w_qkv[:, k, :], a["w_qkv"][:, k, :]).then_inc(ld_wqkv, DMA)
                sp.dma_start(x_feat[:, k, :], a["x_feat"][:, k, :]).then_inc(ld_x, DMA)
            sp.dma_start(cols[:, :], a["cols"]).then_inc(ld_small, DMA)
            sp.dma_start(bias_vo[:, :, :], a["bias_vo"]).then_inc(ld_small, DMA)
            sp.dma_start(masks[:, :, :], a["masks"].bitcast(BF16)).then_inc(ld_small, DMA)
            sp.dma_start(ident[:, :], a["ident"]).then_inc(ld_small, DMA)
            for chunk in range(NH * KD):
                h, pair = divmod(chunk, KD)
                for qk in range(2):
                    i = 2 * chunk + qk
                    m = QK_ORDER[i][0]
                    sp.wait_ge(parts_ready, i + 1)
                    sp.dma_start(scratch[i].rearrange("c p t -> p c t"), qk_part[:, :, m, h * TH:(h + 1) * TH]).then_inc(parts_out[i], DMA)
                heads = slice(pair * HPT, (pair + 1) * HPT)
                for qk, st in ((0, q_st), (1, k_st)):
                    i = 2 * chunk + qk
                    sp.wait_ge(parts_out[i], DMA)
                    for slot, n in ((0, 3), (3, 2), (5, 1)):
                        if qk == 0:
                            src = scratch[i, 0:n].rearrange("c (r h) t -> (c r) (h t)", h=HPT)
                        else:
                            part = {0: 0, 3: 1, 5: 2}[slot]
                            src = scratch[i, part:part + 1].rearrange("c (r h) t -> c r (h t)", h=HPT).broadcast_to([n, HD, HPT * TH])
                        dst = st[slot * HD:(slot + n) * HD, h, heads, :]
                        sp.dma_start(dst, src).then_inc(st_loaded[chunk], DMA)
            sp.dma_start(x_tok[:, :, :], a["x_tok"]).then_inc(ld_tok, DMA)
            sp.dma_start(w_o[:, :, :], a["w_o"]).then_inc(ld_wo, DMA)
            for phase, (h, g) in enumerate(PHASES):
                sp.wait_ge(nmax_feat, phase + 1)
                for c in range(SPLIT):
                    sp.dma_start(q_st[KROWS + c:KROWS + c + 1, h, G * g:G * g + G, :],
                                 nmax_f[c * G:(c + 1) * G, phase % 2, :]).then_inc(nmax_loaded[phase], DMA)
            sp.dma_start(w_g[:, :, :, :], a["w_g"]).then_inc(ld_ffw, DMA)
            sp.dma_start(w_u[:, :, :, :], a["w_u"]).then_inc(ld_ffw, DMA)
            sp.dma_start(w_d[:, :, :], a["w_d"]).then_inc(ld_ffw, DMA)
            sp.wait_ge(ones_ready, 4)
            sp.dma_start(slots.rearrange("s p d -> p s d"),
                         zero_row[:, :].unsqueeze(1).broadcast_to([P, SLOTS, D])).then_inc(slots_zeroed, DMA)
            sp.wait_ge(pv_done, first_round(len(PHASES)))
            sp.dma_start(w_in[:, :, :], a["w_in"]).then_inc(ld_mamba, DMA)
            sp.dma_start(w_xp[:, :, :], a["w_xp"]).then_inc(ld_mamba, DMA)
            sp.dma_start(w_dt[3 * BC:XD, :], a["w_dt"]).then_inc(ld_mamba, DMA)
            sp.dma_start(pick[0:3 * BC, :, :], a["pick"].bitcast(BF16)).then_inc(ld_mamba, DMA)
            sp.dma_start(w_out[:, :, :], a["w_out"]).then_inc(ld_mamba, DMA)
            sp.wait_ge(down_ready, NT)
            sp.dma_start(w_r[:, :, :], a["w_r"]).then_inc(ld_router, DMA)
            sp.dma_start(iota[:, :], a["iota"]).then_inc(ld_router, DMA)
            sp.dma_start(ws_gu[:, :, :, :], a["ws_gu"]).then_inc(ld_shared, DMA)
            sp.dma_start(ws_dn[0:EH, :, :, :], a["ws_dn"]).then_inc(ld_shared, DMA)
            sp.wait_ge(y_acc, NH * NS)
            sp.wait_ge(ym_ready, NH * KI)
            for e in range(0, E, E // 4):
                es = slice(e, e + E // 4)
                sp.dma_start(w_gu[:, es, :, :], a["w_gu"][:, es]).then_inc(ld_experts, DMA)
                sp.dma_start(w_dn[0:EH, es, :, :], a["w_dn"][:, es]).then_inc(ld_experts, DMA)

            def exchange(n, turn, b):
                if has_tile(n):
                    if counts(n - RING + 1):
                        sp.wait_ge(slot_xT_ready, n - RING + 1)
                    sp.dma_start(slot_x[:, b, :], tile_of(slots, n)).then_inc(slot_loaded[b], DMA)
                if has_tile(n - 2 * RING):
                    sp.wait_ge(slot_y_ready, n - 2 * RING + 1)
                    sp.dma_start(tile_of(results, n - 2 * RING), slot_y[:, b, :]).then_inc(slot_stored[b], DMA)

            sp.wait_ge(slots_zeroed, DMA)
            sp.wait_ge(scattered, TOP * NT * DMA)
            in_steps(sp, exchange, SLOTS + 2 * RING)
            for h in range(NH):
                sp.wait_ge(norm_ready, 3 * NT + (h + 1) * TPH)
                sp.dma_start(out[:, h * TPH:(h + 1) * TPH, :], x_tok[:, h * TPH:(h + 1) * TPH, :]).then_inc(stored, DMA)
            sp.wait_ge(stored, NH * DMA)

        @block.gpsimd
        def _(pool):
            nc.gpsimd.memset(v_aug[:, :, :, HD:VC], 1.0).then_inc(ones_ready, 1)
            pool.wait_ge(ones_ready, 1)
            nc.gpsimd.memset(k_st[KROWS:KX, :, :, :], 1.0).then_inc(ones_ready, 1)
            pool.wait_ge(ones_ready, 2)
            nc.gpsimd.memset(minus_half[:, :], -0.5).then_inc(ones_ready, 1)
            nc.gpsimd.memset(zero_row[:, :], 0.0).then_inc(ones_ready, 1)

            pool.wait_ge(ld_tok, DMA)
            pool.wait_ge(ld_small, 4 * DMA)
            nc.gpsimd.tensor_tensor(x_tok[:, :, :], x_tok[:, :, :],
                                    bias_vo[:, 1, :].unsqueeze(1).broadcast_to([P, NT, D]), ALU.add).then_inc(xb_ready, 1)

            def inverse_deviation(layer, h):
                n = layer * NH + h + 1
                tts = slice(h * TPH, (h + 1) * TPH)
                pool.wait_ge(stats_ready, n)
                nc.gpsimd.tensor_tensor(rstd[:, tts], mv[:, tts, 1], minus_half[:, tts], ALU.pow).then_inc(rstd_ready, 1)

            for layer in range(2):
                for h in range(NH):
                    inverse_deviation(layer, h)
            pool.wait_ge(kept_ready, NH * FB)
            pool.wait_ge(down_ready, NT)
            nc.gpsimd.memset(x_in[:, :, 0:TAPS - 1], 0.0).then_inc(zero_ready, 1)
            nc.gpsimd.memset(ones_r, 1.0).then_inc(zero_ready, 1)
            for i in range(NH * KI):
                h, k = divmod(i, KI)
                pool.wait_ge(dt_done, i + 1)
                nc.gpsimd.tensor_tensor(dtx[:, k, h * TH:(h + 1) * TH], dt_[:, k, h * TH:(h + 1) * TH],
                                        xa[:, k, h * TH:(h + 1) * TH], ALU.mult).then_inc(u_done, 1)
            pool.wait_ge(u_done, NH * KI)
            for i in range(NH * NS):
                h, n = divmod(i, NS)
                pool.wait_ge(b_copied, i + 1)
                if i >= 2:
                    pool.wait_ge(scanned, KI * (i - 1))
                nc.gpsimd.tensor_tensor(dBx[:, i % 2, :, :], dtx[:, :, h * TH:(h + 1) * TH],
                                        b_sb[:, i % 2, :].unsqueeze(1).broadcast_to([P, KI, TH]),
                                        ALU.mult).then_inc(dBx_ready, 1)
                if i == NS + 6:
                    inverse_deviation(2, 0)
            inverse_deviation(2, 1)
            pool.wait_ge(slots_zeroed, DMA)
            pool.wait_ge(norm_ready, 3 * NT)
            pool.wait_ge(position_ready, 1)
            for tt in range(NT):
                for c in range(TOP):
                    to = bass.IndirectOffsetOnAxis(ap=position[:, c, tt:tt + 1], axis=0)
                    nc.gpsimd.indirect_dma_start(slots.rearrange("s p d -> (s p) d"), to, x_tok[:, tt, :], None).then_inc(scattered, DMA)
            for b in range(RING):
                pool.wait_ge(slot_stored[b], len(range(b, SLOTS, RING)) * DMA)
            for tt in range(NT):
                for c in range(TOP):
                    where = bass.IndirectOffsetOnAxis(ap=position[:, c, tt:tt + 1], axis=0)
                    nc.gpsimd.indirect_dma_start(picked[:, c, tt, :], None, results.rearrange("s p d -> (s p) d"), where).then_inc(picked_ready[tt], DMA)
            for h in range(NH):
                inverse_deviation(3, h)

        @block.tensor
        def _(pe):
            pe.wait_ge(ld_wqkv, KD * DMA)
            pe.wait_ge(ld_x, KD * DMA)
            for h in range(NH):
                for i in range(h * 2 * KD, (h + 1) * 2 * KD):
                    m = QK_ORDER[i][0]
                    for k in range(KD):
                        mm = nc.tensor.matmul(ps[:, i, :], w_qkv[:, k, m * P:(m + 1) * P],
                                              x_feat[:, k, h * TH:(h + 1) * TH], start=(k == 0), stop=(k == KD - 1))
                    mm.then_inc(qk_ready, 1)
                for tt in range(h * TPH, (h + 1) * TPH):
                    pe.wait_ge(qk_taken, tt + 1)
                    for k in range(KD):
                        mm = nc.tensor.matmul(ps[:, tt, 0:D], x_feat[:, k, tt * P:(tt + 1) * P],
                                              w_qkv[:, k, 2 * D:3 * D], start=(k == 0), stop=(k == KD - 1))
                    mm.then_inc(v_ready, 1)

            def max_entry(n):
                if n >= RB:
                    before = MAX[:n - RB + 1]
                    if len(before[-1]) == 1:
                        pe.wait_ge(nmax_feat, sum(len(m) == 1 for m in before))
                    else:
                        pe.wait_ge(max_taken, sum(len(m) > 1 for m in before))
                bank = n % RB
                if len(MAX[n]) == 1:
                    phase = MAX[n][0]
                    pe.wait_ge(nmax_parts, phase + 1)
                    for i in range(TPH):
                        mm = nc.tensor.transpose(psb[0:SPLIT * G, bank, i * P:(i + 1) * P],
                                                 nmax_p[:, phase % 2, i, :, :].rearrange("p c j -> p (c j)"), identb)
                    mm.then_inc(nmaxT_ready, 1)
                    return
                phase, tt, half, w, js = MAX[n]
                h, g = PHASES[phase]
                if n == 0 or MAX[n - 1][0] != phase:
                    pe.wait_ge(st_loaded[h * KD + g // 2], 6 * DMA)
                for a_, j in enumerate(js):
                    c = a_ * w
                    head = G * g + j
                    diagonal = half == h
                    mm = nc.tensor.matmul(ps[:, bank, c:c + w], q_st[0:KROWS, h, head, (tt % TPH) * P:(tt % TPH + 1) * P],
                                          k_st[0:KROWS, half, head, 0:w], start=True, stop=not diagonal)
                    if diagonal:
                        mm = nc.tensor.matmul(ps[:, bank, c + w - P:c + w], causal, identb, start=False, stop=True)
                mm.then_inc(max_ready, 1)

            def score(n):
                phase, st, w, js = SCORES[n]
                h, g = PHASES[phase]
                if n >= RB:
                    pe.wait_ge(probs_ready, n - RB + 1)
                if n == 0 or SCORES[n - 1][0] != phase:
                    pe.wait_ge(nmax_loaded[phase], SPLIT * DMA)
                for a_, j in enumerate(js):
                    c = a_ * w
                    head = G * g + j
                    diagonal = st // TPH == h
                    mm = nc.tensor.matmul(ps[:, RB + n % RB, c:c + w], k_st[0:KX, st // TPH, head, (st % TPH) * P:(st % TPH + 1) * P],
                                          q_st[0:KX, h, head, TH - w:TH], start=True, stop=not diagonal)
                    if diagonal:
                        mm = nc.tensor.matmul(ps[:, RB + n % RB, c:c + P], identb, causal, start=False, stop=True)
                mm.then_inc(scores_ready, 1)

            def values(phase, st):
                h, g = PHASES[phase]
                r = first_round(phase) + st
                pe.wait_ge(probs_ready, 1 + max(i for i, s in enumerate(SCORES) if s[:2] == (phase, st)))
                if st == 0 and phase >= 2:
                    pe.wait_ge(o_taken, phase - 1)
                w = min(TH, (h + 1) * TH - st * P)
                for j in range(G):
                    mm = nc.tensor.matmul(ps[VC * j:VC * (j + 1), 6 + phase % 2, TH - w:TH], v_aug[:, st, G * g + j, :],
                                          probs[:, r % 3, j, 0:w], start=(st == 0), stop=(st == (h + 1) * TPH - 1))
                mm.then_inc(pv_done, 1)

            pe.wait_ge(ones_ready, 3)
            pe.wait_ge(ld_small, 4 * DMA)
            pe.wait_ge(v_taken, NT)
            issued = 0
            for n, job in enumerate(SCORES):
                while issued < max_jobs_before(n):
                    max_entry(issued)
                    issued += 1
                score(n)
                if n and SCORES[n - 1][:2] != job[:2]:
                    values(*SCORES[n - 1][:2])
            values(*SCORES[-1][:2])

            def o_transposes(tt):
                if tt >= 2:
                    pe.wait_ge(o_norm, tt - 1)
                for g in range(NG):
                    mm = nc.tensor.transpose(ps[:, tt % 2, g * P:(g + 1) * P], o_feat[:, g, tt * P:(tt + 1) * P], ident[:, :])
                mm.then_inc(oT_ready, 1)

            def o_back(tt):
                pe.wait_ge(o_norm, tt + 1)
                if tt >= 2:
                    pe.wait_ge(onf_ready, tt - 1)
                for k in range(KD):
                    mm = nc.tensor.transpose(ps[:, 2 + tt % 2, k * P:(k + 1) * P], o_tok[:, tt % 2, k * P:(k + 1) * P], ident[:, :])
                mm.then_inc(oN_ready, 1)

            def o_project(tt):
                pe.wait_ge(onf_ready, tt + 1)
                if tt >= 2:
                    pe.wait_ge(y_ready, tt - 1)
                for k in range(KD):
                    mm = nc.tensor.matmul(ps[:, 4 + tt % 2, 0:D], o_nf[:, tt % 2, k, :], w_o[:, k, :],
                                          start=(k == 0), stop=(k == KD - 1))
                mm.then_inc(wo_ready, 1)

            def to_features(layer, h):
                if layer or h:
                    pe.wait_ge(feat_ready, layer * NH + h)
                for tt in range(h * TPH, (h + 1) * TPH):
                    pe.wait_ge(norm_ready, layer * NT + tt + 1)
                    for k in range(KD):
                        c = (tt - h * TPH) * P
                        mm = nc.tensor.transpose(ps[:, 6 + k, c:c + P], x_tok[:, tt, k * P:(k + 1) * P], ident[:, :])
                mm.then_inc(xT_ready, 1)

            pe.wait_ge(ld_wo, DMA)
            pe.wait_ge(o_taken, len(PHASES))
            for i in range(NT + 2):
                if i < NT:
                    o_transposes(i)
                if 1 <= i <= NT:
                    o_back(i - 1)
                if i >= 2:
                    o_project(i - 2)

            def gate_up(h):
                pe.wait_ge(feat_ready, h + 1)
                for b in range(FB):
                    n = h * FB + b
                    if n >= 2:
                        pe.wait_ge(ffh_ready, n - 1)
                    for w, bank in ((w_g, 2 * (n % 2)), (w_u, 2 * (n % 2) + 1)):
                        for k in range(KD):
                            mm = nc.tensor.matmul(ps[:, bank, :], w[:, k, b, :], x_feat[:, k, h * TH:(h + 1) * TH],
                                                  start=(k == 0), stop=(k == KD - 1))
                    mm.then_inc(gu_ready, 1)

            pe.wait_ge(ld_ffw, 3 * DMA)
            for h in range(NH):
                to_features(0, h)
                gate_up(h)
            for tt in range(NT):
                pe.wait_ge(y_ready, NT + tt - 1)
                for b in range(FB):
                    if tt % TPH == 0:
                        pe.wait_ge(kept_ready, tt // TPH * FB + b + 1)
                    mm = nc.tensor.matmul(ps[:, 4 + tt % 2, 0:D], ff_k[:, b, tt * P:(tt + 1) * P], w_d[:, b, :],
                                          start=(b == 0), stop=(b == FB - 1))
                mm.then_inc(down_ready, 1)

            pe.wait_ge(ld_mamba, 5 * DMA)
            for h in range(NH):
                to_features(1, h)
                pe.wait_ge(feat_ready, NH + h + 1)
                for m in range(2 * KI):
                    n = h * 2 * KI + m
                    if n >= 4:
                        if m < KI:
                            pe.wait_ge(z_ready, (h - 1) * KI + m + 1)
                        else:
                            pe.wait_ge(xin_ready, h * KI + m - KI + 1)
                    for k in range(KD):
                        mm = nc.tensor.matmul(ps[:, m % 4, :], w_in[:, k, m * P:(m + 1) * P], x_feat[:, k, h * TH:(h + 1) * TH],
                                              start=(k == 0), stop=(k == KD - 1))
                    mm.then_inc(inx_ready, 1)
            for h in range(NH):
                for k in range(KI):
                    pe.wait_ge(xa_ready, h * KI + k + 1)
                    if k == 0:
                        pe.wait_ge(y_ready, 2 * NT)
                    mm = nc.tensor.matmul(ps[0:XD, 4 + h, :], w_xp[:, k, :], xa[:, k, h * TH:(h + 1) * TH],
                                          start=(k == 0), stop=(k == KI - 1))
                mm.then_inc(xd_ready, 1)
            for h in range(NH):
                pe.wait_ge(dt_ready, h + 1)
                for k in range(KI):
                    if h:
                        pe.wait_ge(sp_d_ready, (h - 1) * KI + k + 1)
                    else:
                        pe.wait_ge(z_ready, KI + k + 1)
                    nc.tensor.matmul(ps[:, k, :], w_dt[3 * BC:XD, k * P:(k + 1) * P], dt_lo[3 * BC:XD, h * TH:(h + 1) * TH],
                                     start=True, stop=True).then_inc(sp_abs, 1)

            def broadcast_b(i):
                h, n = divmod(i, NS)
                if i:
                    pe.wait_ge(b_copied, i)
                nc.tensor.matmul(ps[:, 0, :], pick[0:3 * BC, n, :], bc3[0:3 * BC, h * TH:(h + 1) * TH],
                                 start=True, stop=True).then_inc(b_ready, 1)

            def broadcast_c(i):
                h, n = divmod(i, NS)
                if i >= 2:
                    pe.wait_ge(cmul_done, i - 1)
                nc.tensor.matmul(ps[:, 1 + i % 2, :], pick[0:3 * BC, NS + n, :], bc3[0:3 * BC, h * TH:(h + 1) * TH],
                                 start=True, stop=True).then_inc(c_ready, 1)

            def accumulate(i):
                h, n = divmod(i, NS)
                pe.wait_ge(cmul_done, i + 1)
                if h and n == 0:
                    pe.wait_ge(y_half, h)
                for k in range(KI):
                    mm = nc.tensor.matmul(ps[:, 4 + k, :], ident[:, :], hc[:, i % 2, k, :], start=(n == 0), stop=(n == NS - 1))
                mm.then_inc(y_acc, 1)

            def mamba_out(tt):
                pe.wait_ge(ym_ready, (tt // TPH + 1) * KI)
                pe.wait_ge(y_ready, 2 * NT + (tt if tt < TPH else tt - 1))
                for k in range(KI):
                    mm = nc.tensor.matmul(ps[:, out_bank(tt), 0:D], dtx[:, k, tt * P:(tt + 1) * P], w_out[:, k, :],
                                          start=(k == 0), stop=(k == KI - 1))
                mm.then_inc(mout_ready, 1)

            pe.wait_ge(bc_ready, NH)
            pe.wait_ge(sp_d_ready, NH * KI)
            broadcast_b(0)
            broadcast_c(0)
            broadcast_b(1)
            for i in range(NH * NS):
                if i + 2 < NH * NS:
                    broadcast_b(i + 2)
                if i + 1 < NH * NS:
                    broadcast_c(i + 1)
                if i:
                    accumulate(i - 1)
                if NS + 1 <= i <= NS + TPH:
                    mamba_out(i - NS - 1)
            accumulate(NH * NS - 1)
            for tt in range(TPH, NT):
                mamba_out(tt)

            for h in range(NH):
                to_features(2, h)
            pe.wait_ge(ld_router, 2 * DMA)
            pe.wait_ge(feat_ready, 3 * NH)
            for tt in range(NT):
                for k in range(KD):
                    mm = nc.tensor.matmul(ps[:, 6, tt * E:(tt + 1) * E], x_feat[:, k, tt * P:(tt + 1) * P], w_r[:, k, :],
                                          start=(k == 0), stop=(k == KD - 1))
            mm.then_inc(logit_ready, 1)

            def shared_up(n):
                tt, s = divmod(n, SHARED)
                if n >= 2:
                    pe.wait_ge(eh_ready, n - 1)
                for k in range(KD):
                    mm = nc.tensor.matmul(ps[:, n % 2, 0:2 * EI], x_feat[:, k, tt * P:(tt + 1) * P], ws_gu[:, s, k, :],
                                          start=(k == 0), stop=(k == KD - 1))
                mm.then_inc(egu_ready, 1)

            def shared_transposes(n):
                pe.wait_ge(eh_ready, n + 1)
                if n >= 2:
                    pe.wait_ge(ef_ready, n - 1)
                for c in range(2):
                    mm = nc.tensor.transpose(ps[0:EH, 2 + n % 2, c * P:(c + 1) * P], e_h[:, n % 2, c * EH:(c + 1) * EH], ident[:, :])
                mm.then_inc(eT_ready, 1)

            def shared_down(n):
                tt, s = divmod(n, SHARED)
                pe.wait_ge(ef_ready, n + 1)
                if s == 0 and tt >= 2:
                    pe.wait_ge(shared_added, tt - 1)
                for c in range(2):
                    mm = nc.tensor.matmul(ps[:, 4 + tt % 2, 0:D], e_f[0:EH, n % 2, c, :], ws_dn[0:EH, s, c, :],
                                          start=(s == 0 and c == 0), stop=(s == SHARED - 1 and c == 1))
                mm.then_inc(edn_ready, 1)

            pe.wait_ge(ld_shared, 2 * DMA)
            pe.wait_ge(y_ready, 3 * NT)
            for n in range(SHARED * NT + 2):
                if n < SHARED * NT:
                    shared_up(n)
                if 1 <= n <= SHARED * NT:
                    shared_transposes(n - 1)
                if n >= 2:
                    shared_down(n - 2)
                if n == 2:
                    pe.wait_ge(choice_ready, 1)
                    nc.tensor.matmul(ps[:, 6, P:2 * P], all_ones, chosen_any, start=True, stop=True)
                    nc.tensor.matmul(ps[:, 6, 2 * P:3 * P], earlier, chosen_any, start=True, stop=True).then_inc(rank_ready, 1)

            def slot_tile(n, turn, b):
                if has_tile(n):
                    pe.wait_ge(slot_loaded[b], turn * DMA + DMA)
                    if counts(n - 1):
                        pe.wait_ge(slot_xf_ready, n - 1)
                    for k in range(KD):
                        mm = nc.tensor.transpose(ps[:, 6 + b % 2, k * P:(k + 1) * P], slot_x[:, b, k * P:(k + 1) * P], ident[:, :])
                    mm.then_inc(slot_xT_ready, 1)
                if has_tile(n - 1):
                    expert = pe.value_load(slot_expert[0:1, bass.ds(n - 1, 1)], min_val=0, max_val=E - 1)
                    pe.wait_ge(slot_xf_ready, n)
                    if counts(n - 2):
                        pe.wait_ge(slot_h_ready, n - 2)
                    for k in range(KD):
                        mm = nc.tensor.matmul(ps[:, (b + 1) % 2, 0:2 * EI], slot_xf[:, (b + 1) % 2, k, :],
                                              w_gu[:, bass.ds(expert, 1), k, :], start=(k == 0), stop=(k == KD - 1))
                    mm.then_inc(slot_gu_ready, 1)
                if has_tile(n - 2):
                    pe.wait_ge(slot_h_ready, n - 1)
                    if counts(n - 3):
                        pe.wait_ge(slot_hf_ready, n - 3)
                    for c in range(2):
                        mm = nc.tensor.transpose(ps[0:EH, 2 + b % 2, c * P:(c + 1) * P], e_h[:, b % 2, c * EH:(c + 1) * EH], ident[:, :])
                    mm.then_inc(slot_hT_ready, 1)
                if has_tile(n - 3):
                    expert = pe.value_load(slot_expert[0:1, bass.ds(n - 3, 1)], min_val=0, max_val=E - 1)
                    pe.wait_ge(slot_hf_ready, n - 2)
                    if counts(n - 4):
                        pe.wait_ge(slot_y_ready, n - 4)
                    for c in range(2):
                        mm = nc.tensor.matmul(ps[:, 4 + (b + 1) % 2, 0:D], e_f[0:EH, (b + 1) % 2, c, :],
                                              w_dn[0:EH, bass.ds(expert, 1), c, :], start=(c == 0), stop=(c == 1))
                    mm.then_inc(slot_down_ready, 1)

            pe.wait_ge(ld_experts, 8 * DMA)
            pe.wait_ge(slot_expert_ready, 1)
            pe.wait_ge(shared_added, NT)
            in_steps(pe, slot_tile, SLOTS + 3)

        @block.scalar
        def _(act):
            act.wait_ge(ld_small, 4 * DMA)
            act.wait_ge(bias_ready, 1)
            for i, (m, h) in enumerate(QK_ORDER):
                act.wait_ge(qk_ready, i + 1)
                bias = b_q4[:, m:m + 1] if m < KD else cols[:, m:m + 1]
                scale = HD ** -0.5 if m < KD else 1.0
                nc.scalar.activation(qk_full[:, i, :], ps[:, i, :], ACT.Identity, bias=bias, scale=scale)
                nc.scalar.activation(qk_part[:, 0, m, h * TH:(h + 1) * TH], ps[:, i, :], ACT.Identity,
                                     bias=bias, scale=scale).then_inc(qk_taken, 1)

            def evacuate(phase):
                h, g = PHASES[phase]
                act.wait_ge(pv_done, first_round(phase + 1))
                nc.scalar.activation(o_feat[:, g, h * TH:(h + 1) * TH], ps[:, 6 + phase % 2, :], ACT.Copy).then_inc(o_taken, 1)

            for n, (phase, st, w, js) in enumerate(SCORES):
                r = first_round(phase) + st
                act.wait_ge(scores_ready, n + 1)
                if r >= 3:
                    act.wait_ge(pv_done, r - 2)
                elif n == 0:
                    for sent in parts_out:
                        act.wait_ge(sent, DMA)
                nc.scalar.activation(probs[:, r % 3, js[0]:js[-1] + 1, 0:w],
                                     ps[:, RB + n % RB, 0:w * len(js)].rearrange("p (j t) -> p j t", t=w), ACT.Exp).then_inc(probs_ready, 1)
                if phase and st == 2 and SCORES[n + 1][1] != 2:
                    evacuate(phase - 1)
            evacuate(len(PHASES) - 1)

            for tt in range(NT):
                act.wait_ge(oN_ready, tt + 1)
                if tt >= 2:
                    act.wait_ge(wo_ready, tt - 1)
                nc.scalar.activation(o_nf[:, tt % 2, :, :], ps[:, 2 + tt % 2, 0:D].rearrange("p (k t) -> p k t", k=KD),
                                     ACT.Copy).then_inc(onf_ready, 1)

            def features(layer, h):
                act.wait_ge(xT_ready, layer * NH + h + 1)
                nc.scalar.activation(x_feat[:, :, h * TH:(h + 1) * TH], ps[:, 6:8, :], ACT.Copy).then_inc(feat_ready, 1)

            def magnitude(n):
                h, b = divmod(n, FB)
                q = n // GS % 2
                act.wait_ge(ffh_ready, n + 1)
                if n >= 2 * GS:
                    act.wait_ge(kept_ready, (n // GS - 1) * GS)
                nc.scalar.activation(ff_a[:, q, b % GS, :], ff_h[:, q, b % GS, :], ACT.Abs).then_inc(abs_ready, 1)

            for h in range(NH):
                features(0, h)
                for b in range(FB):
                    n = h * FB + b
                    act.wait_ge(gu_ready, n + 1)
                    if n >= 2:
                        act.wait_ge(ffh_ready, n - 1)
                    nc.scalar.activation(ff_s[:, n % 2, :], ps[:, 2 * (n % 2), :], ACT.Silu).then_inc(silu_ready, 1)
                    if n:
                        magnitude(n - 1)
            magnitude(NH * FB - 1)

            act.wait_ge(ld_small, 4 * DMA)
            features(1, 0)
            act.wait_ge(down_ready, NT)
            act.wait_ge(zero_ready, 1)
            cw = lambda k, tap: cols[:, COLS["conv_w"][0] + k * TAPS + tap:COLS["conv_w"][0] + k * TAPS + tap + 1]
            cc = lambda name, k: cols[:, COLS[name][0] + k:COLS[name][0] + k + 1]

            def act_x(h):
                t = slice(h * TH, (h + 1) * TH)
                for k in range(KI):
                    act.wait_ge(conv_done, h * KI + k + 1)
                    nc.scalar.activation(xa[:, k, t], xa[:, k, t], ACT.Silu).then_inc(xa_ready, 1)

            for h in range(NH):
                t = slice(h * TH, (h + 1) * TH)
                if h:
                    features(1, h)
                for k in range(KI):
                    act.wait_ge(inx_ready, h * 2 * KI + k + 1)
                    nc.scalar.activation(xa[:, k, t], ps[:, k, :], ACT.Identity, bias=cc("conv_b", k), scale=cw(k, TAPS - 1))
                    nc.scalar.activation(x_in[:, k, TAPS - 1 + h * TH:TAPS - 1 + (h + 1) * TH], ps[:, k, :],
                                         ACT.Copy).then_inc(xin_ready, 1)
                for k in range(KI):
                    act.wait_ge(inx_ready, h * 2 * KI + KI + k + 1)
                    nc.scalar.activation(sz[:, k, t], ps[:, k, :], ACT.Silu).then_inc(z_ready, 1)
                act_x(h)
            nc.scalar.activation(a_neg[:, :, :], cols[:, COLS["a_log"][0]:COLS["a_log"][1]].rearrange("p (k n) -> p k n", k=KI),
                                 ACT.Exp).then_inc(a_exp, 1)
            for i in range(NH * KI):
                h, k = divmod(i, KI)
                act.wait_ge(sp_abs, i + 1)
                if h:
                    act.wait_ge(dt_done, i - KI + 1)
                nc.scalar.activation(sp_e[:, k, :], ps[:, k, :], ACT.Abs, bias=cc("dt_b", k)).then_inc(act_own, 1)
                act.wait_ge(act_own, i + 1)
                nc.scalar.activation(sp_e[:, k, :], sp_e[:, k, :], ACT.Exp, scale=-1.0).then_inc(sp_exp, 1)
                act.wait_ge(sp_w_ready, i + 1)
                nc.scalar.activation(sp_w[:, k, :], sp_w[:, k, :], ACT.Ln).then_inc(sp_ln, 1)
            act.wait_ge(a_ready, 1)

            def copy_b(i):
                act.wait_ge(b_ready, i + 1)
                if i >= 2:
                    act.wait_ge(dBx_ready, i - 1)
                nc.scalar.activation(b_sb[:, i % 2, :], ps[:, 0, :], ACT.Copy).then_inc(b_copied, 1)

            act.wait_ge(u_done, NH * KI)
            copy_b(0)
            for i in range(NH * NS):
                h, n = divmod(i, NS)
                if i + 1 < NH * NS:
                    copy_b(i + 1)
                if i >= 2:
                    act.wait_ge(scanned, KI * (i - 1))
                for k in range(KI):
                    nc.scalar.activation(dA[:, i % 2, k, :], dt_[:, k, h * TH:(h + 1) * TH], ACT.Exp,
                                         scale=a_neg[:, k, n:n + 1]).then_inc(dA_ready, 1)
            for h in range(NH):
                features(2, h)
            act.wait_ge(r_sub, 1)
            nc.scalar.activation(r_p[:, :, :], r_p[:, :, :], ACT.Exp).then_inc(r_exp, 1)
            for n in range(SHARED * NT + 1):
                if n < SHARED * NT:
                    act.wait_ge(egu_ready, n + 1)
                    if n >= 2:
                        act.wait_ge(eh_ready, n - 1)
                    nc.scalar.activation(e_s[:, n % 2, :], ps[:, n % 2, 0:EI], ACT.Silu).then_inc(es_ready, 1)
                if n:
                    act.wait_ge(eT_ready, n)
                    if n >= 3:
                        act.wait_ge(edn_ready, n - 2)
                    nc.scalar.activation(e_f[0:EH, (n - 1) % 2, :, :], ps[0:EH, 2 + (n - 1) % 2, 0:2 * P].rearrange("p (c t) -> p c t", c=2),
                                         ACT.Copy).then_inc(ef_ready, 1)

            def slot_tile(n, turn, b):
                if has_tile(n):
                    act.wait_ge(slot_xT_ready, n + 1)
                    if counts(n - 1):
                        act.wait_ge(slot_gu_ready, n - 1)
                    nc.scalar.activation(slot_xf[:, b % 2, :, :], ps[:, 6 + b % 2, 0:D].rearrange("p (k t) -> p k t", k=KD),
                                         ACT.Copy).then_inc(slot_xf_ready, 1)
                if has_tile(n - 1):
                    act.wait_ge(slot_gu_ready, n)
                    if counts(n - 2):
                        act.wait_ge(slot_h_ready, n - 2)
                    nc.scalar.activation(e_s[:, (b + 1) % 2, :], ps[:, (b + 1) % 2, 0:EI], ACT.Silu).then_inc(slot_silu_ready, 1)
                if has_tile(n - 2):
                    act.wait_ge(slot_hT_ready, n - 1)
                    if counts(n - 3):
                        act.wait_ge(slot_down_ready, n - 3)
                    nc.scalar.activation(e_f[0:EH, b % 2, :, :], ps[0:EH, 2 + b % 2, 0:2 * P].rearrange("p (c t) -> p c t", c=2),
                                         ACT.Copy).then_inc(slot_hf_ready, 1)

            act.wait_ge(y_acc, NH * NS)
            act.wait_ge(ym_ready, NH * KI)
            act.wait_ge(eh_ready, SHARED * NT)
            act.wait_ge(edn_ready, SHARED * NT)
            in_steps(act, slot_tile, SLOTS + 2)

        @block.vector
        def _(dve):
            done = [0]

            def link(ins):
                done[0] += 1
                ins.then_inc(vec_own, 1)
                dve.wait_ge(vec_own, done[0])

            dve.wait_ge(ld_small, 4 * DMA)
            nc.vector.tensor_scalar(b_q4[:, :], cols[:, 0:KD], HD ** -0.5, None, ALU.mult).then_inc(bias_ready, 1)
            for i, (m, h) in enumerate(QK_ORDER):
                t = slice(h * TH, (h + 1) * TH)
                dve.wait_ge(qk_taken, i + 1)
                link(nc.vector.tensor_tensor(qk_full[:, i, :], qk_full[:, i, :], qk_part[:, 0, m, t], ALU.subtract))
                link(nc.vector.tensor_copy(qk_part[:, 1, m, t], qk_full[:, i, :]))
                nc.vector.tensor_tensor(qk_part[:, 2, m, t], qk_full[:, i, :], qk_part[:, 1, m, t],
                                        ALU.subtract).then_inc(parts_ready, 1)
            for tt in range(NT):
                dve.wait_ge(v_ready, tt + 1)
                nc.vector.tensor_tensor(v_aug[:, tt, :, 0:HD], ps[:, tt, 0:D].rearrange("p (h d) -> p h d", h=HEADS),
                                        bias_vo[:, 0, :].rearrange("p (h d) -> p h d", h=HEADS),
                                        ALU.add).then_inc(v_taken, 1)
            taken = [0, 0]
            for n, entry in enumerate(MAX):
                phase = entry[0]
                h, g = PHASES[phase]
                if len(entry) == 1:
                    dve.wait_ge(nmaxT_ready, phase + 1)
                    if phase >= 2:
                        dve.wait_ge(nmax_loaded[phase - 2], SPLIT * DMA)
                    nc.vector.tensor_copy(nmax_f[0:SPLIT * G, phase % 2, :], psb[0:SPLIT * G, n % RB, 0:TH]).then_inc(nmax_feat, 1)
                    continue
                _, tt, half, w, js = entry
                taken[0] += 1
                dve.wait_ge(max_ready, taken[0])
                nc.vector.tensor_reduce(nmax[:, half, tt, js[0]:js[-1] + 1],
                                        ps[:, n % RB, 0:w * len(js)].rearrange("p (j t) -> p j t", t=w), AX.X, ALU.max,
                                        negate=True).then_inc(max_taken, 1)
                if taken[0] == sum(len(max_jobs(q)) for q in range(phase + 1)):
                    dve.wait_ge(max_taken, taken[0])
                    tts = slice(h * TPH, (h + 1) * TPH)
                    if h:
                        link(nc.vector.tensor_tensor(nmax[:, 0, tts, :], nmax[:, 0, tts, :], nmax[:, 1, tts, :], ALU.min))
                    if phase >= 2:
                        dve.wait_ge(nmaxT_ready, phase - 1)
                    parts = nmax_p[:, phase % 2, :, :, :]
                    link(nc.vector.tensor_copy(parts[:, :, 0, :], nmax[:, 0, tts, :]))
                    link(nc.vector.tensor_tensor(nmax_r[:, :, :], nmax[:, 0, tts, :], parts[:, :, 0, :], ALU.subtract))
                    link(nc.vector.tensor_copy(parts[:, :, 1, :], nmax_r[:, :, :]))
                    nc.vector.tensor_tensor(parts[:, :, 2, :], nmax_r[:, :, :], parts[:, :, 1, :],
                                            ALU.subtract).then_inc(nmax_parts, 1)
                    dve.wait_ge(nmax_parts, phase + 1)

            def add_residual(source, tt):
                nc.vector.tensor_tensor(y_tok[:, tt, :], source, x_tok[:, tt, :], ALU.add).then_inc(y_ready, 1)

            def statistics(layer, h):
                tts = range(h * TPH, (h + 1) * TPH)
                dve.wait_ge(y_ready, layer * NT + (h + 1) * TPH)
                for tt in tts:
                    last = nc.vector.bn_stats(stats[:, tt, :], y_tok[:, tt, :])
                link(last)
                for tt in tts:
                    last = nc.vector.bn_aggr(mv[:, tt, :], stats[:, tt, :])
                link(last)
                nc.vector.tensor_scalar(mv[:, h * TPH:(h + 1) * TPH, 1], mv[:, h * TPH:(h + 1) * TPH, 1], EPS, None,
                                        ALU.add).then_inc(stats_ready, 1)

            def normalise(layer, h):
                dve.wait_ge(rstd_ready, layer * NH + h + 1)
                for tt in range(h * TPH, (h + 1) * TPH):
                    nc.vector.tensor_scalar(x_tok[:, tt, :], y_tok[:, tt, :], mv[:, tt, 0:1], rstd[:, tt:tt + 1],
                                            ALU.subtract, ALU.mult).then_inc(norm_ready, 1)

            dve.wait_ge(xb_ready, 1)

            def divide(tt):
                heads = ps[:, tt % 2, :].rearrange("p (h c) -> p h c", h=HEADS)
                dve.wait_ge(oT_ready, tt + 1)
                link(nc.vector.reciprocal(rden[:, tt % 2, :], heads[:, :, HD]))
                if tt >= 2:
                    dve.wait_ge(oN_ready, tt - 1)
                nc.vector.tensor_tensor(o_tok[:, tt % 2, :].rearrange("p (h c) -> p h c", h=HEADS), heads[:, :, 0:HD],
                                        rden[:, tt % 2, :].unsqueeze(2).broadcast_to([P, HEADS, HD]), ALU.mult).then_inc(o_norm, 1)

            for i in range(NT + 2):
                if i < NT:
                    divide(i)
                if i >= 2:
                    tt = i - 2
                    dve.wait_ge(wo_ready, tt + 1)
                    add_residual(ps[:, 4 + tt % 2, 0:D], tt)
                    if tt == TPH - 1:
                        statistics(0, 0)
                        normalise(0, 0)
            statistics(0, 1)
            normalise(0, 1)

            def keep_two(q):
                hb, ab = ff_h[:, q % 2, :, :], ff_a[:, q % 2, :, :]
                dve.wait_ge(abs_ready, GS * (q + 1))
                nc.vector.tensor_tensor(ff_c[:, 0:3, :], ab[:, 0, :].unsqueeze(1).broadcast_to([P, 3, TH]), ab[:, 1:4, :], ALU.is_ge)
                nc.vector.tensor_tensor(ff_c[:, 3:5, :], ab[:, 1, :].unsqueeze(1).broadcast_to([P, 2, TH]), ab[:, 2:4, :], ALU.is_ge)
                link(nc.vector.tensor_tensor(ff_c[:, 5, :], ab[:, 2, :], ab[:, 3, :], ALU.is_ge))
                for j, (x, y) in enumerate(((0, 1), (3, 4), (1, 3), (2, 4))):
                    last = nc.vector.tensor_tensor(ff_w[:, j, :], ff_c[:, x, :], ff_c[:, y, :], ALU.add)
                link(last)
                nc.vector.tensor_tensor(ff_w[:, 0, :], ff_w[:, 0, :], ff_c[:, 2, :], ALU.add)
                nc.vector.tensor_tensor(ff_w[:, 1, :], ff_w[:, 1, :], ff_c[:, 0, :], ALU.subtract)
                nc.vector.tensor_tensor(ff_w[:, 2, :], ff_c[:, 5, :], ff_w[:, 2, :], ALU.subtract)
                link(nc.vector.tensor_tensor(ff_w[:, 3, :], ff_w[:, 3, :], ff_c[:, 5, :], ALU.add))
                h, gb = divmod(q, 2)
                for j, (bound, op) in enumerate(((1.5, ALU.is_ge), (0.5, ALU.is_ge), (-0.5, ALU.is_ge), (1.5, ALU.is_le))):
                    nc.vector.scalar_tensor_tensor(out=ff_k[:, gb * GS + j, h * TH:(h + 1) * TH], in0=ff_w[:, j, :], scalar=bound,
                                                   in1=hb[:, j, :], op0=op, op1=ALU.mult).then_inc(kept_ready, 1)

            for n in range(NH * FB):
                dve.wait_ge(silu_ready, n + 1)
                if n >= 2 * GS:
                    dve.wait_ge(kept_ready, (n // GS - 1) * GS)
                nc.vector.tensor_tensor(ff_h[:, n // GS % 2, n % GS, :], ff_s[:, n % 2, :], ps[:, 2 * (n % 2) + 1, :],
                                        ALU.mult).then_inc(ffh_ready, 1)
                if n % GS == GS - 2 and n > GS:
                    keep_two(n // GS - 1)
            keep_two(NH * FB // GS - 1)
            for h in range(NH):
                for tt in range(h * TPH, (h + 1) * TPH):
                    dve.wait_ge(down_ready, tt + 1)
                    add_residual(ps[:, 4 + tt % 2, 0:D], tt)
                statistics(1, h)
                normalise(1, h)

            cw = lambda k, tap: cols[:, COLS["conv_w"][0] + k * TAPS + tap:COLS["conv_w"][0] + k * TAPS + tap + 1]
            cc = lambda name, k: cols[:, COLS[name][0] + k:COLS[name][0] + k + 1]
            for h in range(NH):
                t = slice(h * TH, (h + 1) * TH)
                for k in range(KI):
                    dve.wait_ge(xin_ready, h * KI + k + 1)
                    for tap in range(TAPS - 1):
                        ins = nc.vector.scalar_tensor_tensor(out=xa[:, k, t], in0=x_in[:, k, h * TH + tap:h * TH + tap + TH],
                                                             scalar=cw(k, tap), in1=xa[:, k, t], op0=ALU.mult, op1=ALU.add)
                        if tap < TAPS - 2:
                            link(ins)
                    ins.then_inc(conv_done, 1)
            dve.wait_ge(a_exp, 1)
            nc.vector.tensor_scalar(a_neg[:, :, :], a_neg[:, :, :], -1.0, None, ALU.mult).then_inc(a_ready, 1)
            for h in range(NH):
                t = slice(h * TH, (h + 1) * TH)
                xd = ps[:, 4 + h, :]
                dve.wait_ge(xd_ready, h + 1)
                nc.vector.tensor_copy(dt_lo[3 * BC:XD, t], xd[3 * BC:XD, :]).then_inc(dt_ready, 1)
                link(nc.vector.tensor_copy(bc_p[0:3 * BC, 0, :], xd[0:3 * BC, :]))
                link(nc.vector.tensor_tensor(bc_r[0:3 * BC, :], xd[0:3 * BC, :], bc_p[0:3 * BC, 0, :], ALU.subtract))
                link(nc.vector.tensor_copy(bc_p[0:3 * BC, 1, :], bc_r[0:3 * BC, :]))
                link(nc.vector.tensor_tensor(bc3[0:3 * BC, t], bc_r[0:3 * BC, :], bc_p[0:3 * BC, 1, :], ALU.subtract))
                nc.vector.tensor_copy(bc3[0:BC, t], bc_p[0:BC, 0, :])
                last = nc.vector.tensor_copy(bc3[BC:2 * BC, t], bc_p[BC:2 * BC, 1, :])
                last.then_inc(bc_ready, 1)
                dve.wait_ge(bc_ready, h + 1)
            for i in range(NH * KI):
                h, k = divmod(i, KI)
                t = slice(h * TH, (h + 1) * TH)
                dve.wait_ge(sp_exp, i + 1)
                link(nc.vector.tensor_scalar(sp_d[:, k, :], sp_e[:, k, :], 1.0, None, ALU.add))
                nc.vector.tensor_copy(sp_w[:, k, :], sp_d[:, k, :]).then_inc(sp_w_ready, 1)
                link(nc.vector.scalar_tensor_tensor(out=sp_d[:, k, :], in0=sp_d[:, k, :], scalar=-1.0, in1=sp_e[:, k, :],
                                                    op0=ALU.add, op1=ALU.subtract))
                nc.vector.tensor_scalar(dt_[:, k, t], ps[:, k, :], cc("dt_b", k), 0.0, ALU.add, ALU.max).then_inc(sp_d_ready, 1)
                dve.wait_ge(sp_d_ready, i + 1)
                link(nc.vector.tensor_tensor(dt_[:, k, t], dt_[:, k, t], sp_d[:, k, :], ALU.subtract))
                dve.wait_ge(sp_ln, i + 1)
                nc.vector.tensor_tensor(dt_[:, k, t], dt_[:, k, t], sp_w[:, k, :], ALU.add).then_inc(dt_done, 1)
            for i in range(NH * NS):
                h, n = divmod(i, NS)
                dve.wait_ge(dBx_ready, i + 1)
                for k in range(KI):
                    dve.wait_ge(dA_ready, KI * i + k + 1)
                    nc.vector.tensor_tensor_scan(hs[:, i % 2, k, :], dA[:, i % 2, k, :], dBx[:, i % 2, k, :],
                                                 h_last[:, k, n:n + 1] if h else 0.0, ALU.mult, ALU.add).then_inc(scanned, 1)
                dve.wait_ge(scanned, KI * (i + 1))
                if h < NH - 1:
                    nc.vector.tensor_copy(h_last[:, :, n], hs[:, i % 2, :, TH - 1])
                dve.wait_ge(c_ready, i + 1)
                if i >= 2:
                    dve.wait_ge(y_acc, i - 1)
                nc.vector.tensor_tensor(hc[:, i % 2, :, :], hs[:, i % 2, :, :],
                                        ps[:, 1 + i % 2, :].unsqueeze(1).broadcast_to([P, KI, TH]), ALU.mult).then_inc(cmul_done, 1)
                if n == NS - 1:
                    t = slice(h * TH, (h + 1) * TH)
                    dve.wait_ge(y_acc, i + 1)
                    for k in range(KI):
                        ins = nc.vector.scalar_tensor_tensor(out=dtx[:, k, t], in0=xa[:, k, t], scalar=cc("skip", k),
                                                             in1=ps[:, 4 + k, :], op0=ALU.mult, op1=ALU.add)
                    ins.then_inc(y_half, 1)
                    dve.wait_ge(y_half, h + 1)
                    for k in range(KI):
                        nc.vector.tensor_tensor(dtx[:, k, t], dtx[:, k, t], sz[:, k, t], ALU.mult).then_inc(ym_ready, 1)
                if i >= NS + 1 and i < NS + 1 + TPH:
                    tt = i - NS - 1
                    dve.wait_ge(mout_ready, tt + 1)
                    add_residual(ps[:, out_bank(tt), 0:D], tt)
                if i == NS + 5:
                    statistics(2, 0)
                if i == NS + 8:
                    normalise(2, 0)
            for tt in range(TPH, NT):
                dve.wait_ge(mout_ready, tt + 1)
                add_residual(ps[:, out_bank(tt), 0:D], tt)
            statistics(2, 1)
            normalise(2, 1)

            logits = ps[:, 6, 0:NT * E].rearrange("p (t e) -> p t e", t=NT)
            wide = lambda x: x.broadcast_to([P, NT, E])

            def subtract_maximum():
                dve.wait_ge(logit_ready, 1)
                link(nc.vector.tensor_reduce(r_max[:, :], logits, AX.X, ALU.max))
                nc.vector.tensor_tensor(r_p[:, :, :], logits, wide(r_max[:, :].unsqueeze(2)), ALU.subtract).then_inc(r_sub, 1)

            def choose():
                dve.wait_ge(r_exp, 1)
                link(nc.vector.tensor_reduce(r_max[:, :], r_p[:, :, :], AX.X, ALU.add))
                link(nc.vector.reciprocal(r_max[:, :], r_max[:, :]))
                link(nc.vector.tensor_tensor(r_p[:, :, :], r_p[:, :, :], wide(r_max[:, :].unsqueeze(2)), ALU.mult))
                for tt in range(NT):
                    last = nc.vector.max(r_8[:, tt, :], r_p[:, tt, :])
                link(last)
                for tt in range(NT):
                    last = nc.vector.max_index(r_i[:, tt, :].bitcast(U32), r_8[:, tt, :], r_p[:, tt, :])
                link(last)
                link(nc.vector.tensor_copy(r_if[:, :, :], r_i[:, :, :].bitcast(U32)))
                dve.wait_ge(ld_router, 2 * DMA)
                experts = iota_e.unsqueeze(1).broadcast_to([P, NT, E])
                nc.vector.tensor_tensor(chosen[:, 0, :, :], experts, wide(r_if[:, :, 0:1]), ALU.is_equal)
                link(nc.vector.tensor_tensor(chosen[:, 1, :, :], experts, wide(r_if[:, :, 1:2]), ALU.is_equal))
                nc.vector.tensor_tensor(chosen_any.rearrange("p (t e) -> p t e", t=NT), chosen[:, 0, :, :], chosen[:, 1, :, :],
                                        ALU.add).then_inc(choice_ready, 1)

            def count_tokens():
                dve.wait_ge(rank_ready, 1)
                dve.wait_ge(zero_ready, 2)
                link(nc.vector.tensor_copy(per_tile.rearrange("p (e t) -> p e t", e=E),
                                           ps[:, 6, P:2 * P].rearrange("p (t e) -> p e t", t=NT)))
                link(nc.vector.tensor_tensor_scan(upto, ones_r, per_tile, 0.0, ALU.mult, ALU.add))
                link(nc.vector.tensor_tensor(before[:, :, :].rearrange("p e t -> p (e t)"), upto, per_tile, ALU.subtract))
                link(nc.vector.tensor_tensor(count, upto.rearrange("p (e t) -> p e t", e=E)[:, :, NT - 1], before[:, :, 0], ALU.subtract))
                link(nc.vector.tensor_tensor(per_tile.rearrange("p (e t) -> p e t", e=E), count.unsqueeze(2).broadcast_to([P, E, NT]),
                                             fill_steps.unsqueeze(1).broadcast_to([P, E, NT]), ALU.is_gt))
                link(nc.vector.tensor_reduce(tiles_of, per_tile.rearrange("p (e t) -> p e t", e=E), AX.X, ALU.add))

            def place_experts():
                link(nc.vector.tensor_tensor_scan(end_tile, ones_r[:, 0:E], tiles_of, 0.0, ALU.mult, ALU.add))
                link(nc.vector.tensor_tensor(base, end_tile, tiles_of, ALU.subtract))
                link(nc.vector.scalar_tensor_tensor(out=base, in0=base, scalar=float(P), in1=before[:, :, 0],
                                                    op0=ALU.mult, op1=ALU.subtract))
                link(nc.vector.tensor_tensor(before[:, :, :], before[:, :, :], base.unsqueeze(2).broadcast_to([P, E, NT]), ALU.add))
                link(nc.vector.tensor_tensor(place[:, :, :], before[:, :, :].rearrange("p e t -> p t e"),
                                             ps[:, 6, 2 * P:3 * P].rearrange("p (t e) -> p t e", t=NT), ALU.add))

            def place_tokens():
                link(nc.vector.tensor_tensor(r_q[:, :, :, :], chosen[:, :, :, :],
                                             place[:, :, :].unsqueeze(1).broadcast_to([P, TOP, NT, E]), ALU.mult))
                link(nc.vector.tensor_reduce(position_f[:, :, :], r_q[:, :, :, :], AX.X, ALU.add))
                nc.vector.tensor_copy(position[:, :, :], position_f[:, :, :]).then_inc(position_ready, 1)

            def name_experts():
                ended = picked_flat[0:1, 0:SLOTS * E].rearrange("p (s e) -> p s e", s=SLOTS)
                link(nc.vector.tensor_tensor(ended, iota_slot[0:1, :].unsqueeze(2).broadcast_to([1, SLOTS, E]),
                                             end_tile[0:1, :].unsqueeze(1).broadcast_to([1, SLOTS, E]), ALU.is_ge))
                link(nc.vector.tensor_reduce(slot_f[0:1, :], ended, AX.X, ALU.add))
                nc.vector.tensor_scalar(slot_expert[0:1, :], slot_f[0:1, :], float(E - 1), None, ALU.min).then_inc(slot_expert_ready, 1)

            routing = {0: choose, 1: count_tokens, 2: place_experts, 3: place_tokens, 4: name_experts}
            subtract_maximum()
            for n in range(SHARED * NT + 3):
                if n < SHARED * NT:
                    dve.wait_ge(es_ready, n + 1)
                    if n >= 2:
                        dve.wait_ge(eT_ready, n - 1)
                    nc.vector.tensor_tensor(e_h[:, n % 2, :], e_s[:, n % 2, :], ps[:, n % 2, EI:2 * EI], ALU.mult).then_inc(eh_ready, 1)
                if n >= 4 and n % SHARED == 0:
                    tt = n // SHARED - 2
                    dve.wait_ge(edn_ready, (tt + 1) * SHARED)
                    nc.vector.tensor_tensor(y_tok[:, tt, :], ps[:, 4 + tt % 2, 0:D], x_tok[:, tt, :], ALU.add).then_inc(shared_added, 1)
                if n in routing:
                    routing[n]()

            def slot_tile(n, turn, b):
                if has_tile(n - 1):
                    dve.wait_ge(slot_silu_ready, n)
                    if counts(n - 2):
                        dve.wait_ge(slot_hT_ready, n - 2)
                    nc.vector.tensor_tensor(e_h[:, (b + 1) % 2, :], e_s[:, (b + 1) % 2, :], ps[:, (b + 1) % 2, EI:2 * EI],
                                            ALU.mult).then_inc(slot_h_ready, 1)
                if has_tile(n - 3):
                    dve.wait_ge(slot_down_ready, n - 2)
                    if counts(n - 3 - RING + 1):
                        dve.wait_ge(slot_stored[(b + 1) % RING], stores(turn, b))
                    nc.vector.tensor_copy(slot_y[:, (b + 1) % RING, :], ps[:, 4 + (b + 1) % 2, 0:D]).then_inc(slot_y_ready, 1)

            def stores(turn, b):
                return (turn - 1 + (b + 1) // RING) * DMA

            dve.wait_ge(eT_ready, SHARED * NT)
            in_steps(dve, slot_tile, SLOTS + 3)
            for h in range(NH):
                for tt in range(h * TPH, (h + 1) * TPH):
                    dve.wait_ge(picked_ready[tt], TOP * DMA)
                    dve.wait_ge(shared_added, NT)
                    link(nc.vector.scalar_tensor_tensor(out=y_tok[:, tt, :], in0=picked[:, 0, tt, :], scalar=r_8[:, tt, 0:1],
                                                        in1=y_tok[:, tt, :], op0=ALU.mult, op1=ALU.add))
                    nc.vector.scalar_tensor_tensor(out=y_tok[:, tt, :], in0=picked[:, 1, tt, :], scalar=r_8[:, tt, 1:2],
                                                   in1=y_tok[:, tt, :], op0=ALU.mult, op1=ALU.add).then_inc(y_ready, 1)
                statistics(3, h)
            for h in range(NH):
                normalise(3, h)


def host_arrays(v):
    bits = lambda w: (w.astype(np.float32).view(np.uint32) >> 16).astype(np.uint16)
    f = lambda x: np.asarray(x)
    c = np.ascontiguousarray
    tiles = lambda w: c(w.reshape(-1, P, w.shape[1]).transpose(1, 0, 2))
    x = f(v["L0_attn_x"])[0]
    order = np.arange(D).reshape(KD, HPT, HD).transpose(0, 2, 1).ravel()
    order = np.concatenate([order, D + order, 2 * D + np.arange(D)])
    wqkv, bqkv = f(v["L0_attn_Wqkv"])[:, order], f(v["L0_attn_bqkv"])[order]
    key, query = np.arange(P)[:, None], np.arange(P)[None, :]
    cols = np.zeros((P, NCOLS), np.float32)
    put = lambda n, w: cols.__setitem__((slice(None), slice(*COLS[n])), w)
    put("b_qk", bqkv[:2 * D].reshape(4, P).T)
    colt = lambda w: w.reshape(KI, P, -1).transpose(1, 0, 2).reshape(P, -1)
    put("conv_w", colt(f(v["L1_attn_conv_w"])))
    put("conv_b", colt(f(v["L1_attn_conv_b"])))
    put("dt_b", colt(f(v["L1_attn_dt_proj_b"])))
    put("skip", colt(f(v["L1_attn_D"])))
    put("a_log", colt(f(v["L1_attn_A_log"])))
    bias_vo = np.broadcast_to(np.stack([bqkv[2 * D:], f(v["L0_attn_bo"])])[None], (P, 2, D))
    ffc = np.arange(FF).reshape(2, P, GS).transpose(0, 2, 1).ravel()
    blocks = lambda w: c(w[:, ffc].reshape(KD, P, FB, P).transpose(1, 0, 2, 3))
    xp = f(v["L1_attn_x_proj_w"]).T
    xp = np.concatenate([xp[:, RANK:]] * 3 + [xp[:, :RANK]], 1)
    pick = np.zeros((3, BC, BC, P), np.float32)
    pick[:, np.arange(BC), np.arange(BC)] = 1.0
    sgu, sdn = f(v["L1_ffn_shared_gate_up"]), f(v["L1_ffn_shared_down"])
    half = lambda w, s: w[:, s * EI:(s + 1) * EI]
    ws_gu = np.stack([np.concatenate([half(sgu, s), half(sgu, SHARED + s)], 1) for s in range(SHARED)])
    up = lambda w: c(w.reshape(-1, KD, P, 2 * EI).transpose(2, 0, 1, 3))
    down = lambda w: c(w.reshape(-1, 2, EH, D).transpose(2, 0, 1, 3))
    fills, place = np.arange(NT) * P, np.arange(SLOTS)
    return {
        "w_g": blocks(f(v["L0_ffn_w_gate"])), "w_u": blocks(f(v["L0_ffn_w_up"])), "w_d": tiles(f(v["L0_ffn_w_down"])[ffc]),
        "w_in": tiles(c(f(v["L1_attn_in_proj_w"]).T)), "w_xp": tiles(xp), "w_dt": c(f(v["L1_attn_dt_proj_w"]).T),
        "pick": bits(pick.reshape(3 * BC, BC, P)), "w_out": tiles(c(f(v["L1_attn_out_proj_w"]).T)),
        "w_r": tiles(c(f(v["L1_ffn_gate_w"]).T)), "iota": np.broadcast_to(np.concatenate([np.arange(E), fills, place]).astype(np.float32), (P, E + NT + SLOTS)).copy(),
        "w_gu": up(f(v["L1_ffn_w_gate_up"])), "w_dn": down(f(v["L1_ffn_w_down"])), "ws_gu": up(ws_gu), "ws_dn": down(sdn),
        "x_feat": tiles(c(x.T)), "x_tok": tiles(x), "w_qkv": tiles(wqkv), "cols": cols,
        "bias_vo": c(bias_vo), "w_o": tiles(f(v["L0_attn_Wo"])),
        "masks": bits(np.stack([np.eye(P), np.where(query < key, -30000.0, 0.0),
                                key < query, np.ones((P, P))], 1)),
        "ident": np.eye(P, dtype=np.float32),
    }


def launch_body(nc, args, out):
    scratch = nc.dram_tensor("scratch", [len(QK_ORDER), SPLIT, P, TH], mybir.dt.bfloat16).ap()
    slots = nc.dram_tensor("slots", [SLOTS, P, D], mybir.dt.float32).ap()
    results = nc.dram_tensor("results", [SLOTS, P, D], mybir.dt.float32).ap()
    build(nc, args, out.rearrange("a (t p) d -> p (a t) d", p=P), scratch, slots, results)


def kernel(**inputs):
    import concourse.bacc as _bacc
    from concourse import mybir as _mybir
    from concourse.bass_utils import run_bass_kernel_spmd as _run

    nc = _bacc.Bacc("TRN2", target_bir_lowering=False, num_devices=1)
    arrays, args = {}, {}
    for name, array in host_arrays(inputs).items():
        arrays["in_" + name] = array
        args[name] = nc.dram_tensor("in_" + name, array.shape, _mybir.dt.from_np(array.dtype), kind="ExternalInput").ap()
    out = nc.dram_tensor("out", (1, T, D), _mybir.dt.float32, kind="ExternalOutput").ap()
    launch_body(nc, args, out)
    r = _run(nc, [arrays], core_ids=[0])
    return r.results[0]["out"]
```

```python
from contextlib import ExitStack

import numpy as np

import concourse.bass as bass
from concourse import mybir

F32 = mybir.dt.float32
BF16 = mybir.dt.bfloat16
U32 = mybir.dt.uint32
I32 = mybir.dt.int32
ALU = mybir.AluOpType
ACT = mybir.ActivationFunctionType
AX = mybir.AxisListType

P = 128
T = 1024
NT = T // P
TH = 512
NH = T // TH
TPH = TH // P
D = 256
KD = D // P
HEADS = 16
HD = D // HEADS
HPT = HEADS // KD
G = 4
NG = HEADS // G
VC = 32
SPLIT = 3
KROWS = 6 * HD
KX = KROWS + SPLIT
EPS = 1e-5
FF = 1024
FB = FF // P
GS = 4
DI = 512
KI = DI // P
NS = 16
RANK = 16
BC = 2 * NS
XD = 3 * BC + RANK
TAPS = 4
E = 16
EI = 176
EH = EI // 2
SHARED = 2
TOP = 2
SLOTS = (TOP * T - E) // P + E
RING = 4
AHEAD = 5
EARLY = 6
DMA = 16

QK_ORDER = [(0, 0), (2, 0), (1, 0), (3, 0), (0, 1), (2, 1), (1, 1), (3, 1)]
PHASES = [(h, g) for h in range(NH) for g in range(NG)]
PACE = 3
LAG = 3
RB = 3


def heads_of(w):
    n = {P: 4, 2 * P: 2}.get(w, 1)
    return [list(range(j, j + n)) for j in range(0, G, n)]


def max_jobs(phase):
    h, g = PHASES[phase]
    tiles = [(h * TPH + i, half, TH if half < h else (i + 1) * P) for i in range(TPH) for half in range(h + 1)]
    return [(phase, tt, half, w, js) for tt, half, w in tiles for js in heads_of(w)]


def score_jobs(phase):
    h, g = PHASES[phase]
    tiles = [(st, min(TH, (h + 1) * TH - st * P)) for st in range((h + 1) * TPH)]
    return [(phase, st, w, js) for st, w in tiles for js in heads_of(w)]


def first_round(phase):
    return sum((h + 1) * TPH for h, _ in PHASES[:phase])


MAX = []
for _phase in range(len(PHASES)):
    MAX += max_jobs(_phase)
_late = 4
for _phase in range(len(PHASES)):
    _last = max(i for i, m in enumerate(MAX) if m[0] == _phase and len(m) > 1)
    MAX.insert(min(_last + _late, len(MAX)) if _phase < len(PHASES) - 1 else len(MAX), (_phase,))
SCORES = [job for phase in range(len(PHASES)) for job in score_jobs(phase)]
columns = lambda job: job[-2] * len(job[-1]) if len(job) > 1 else 0


def max_jobs_before(score):
    done = sum(columns(m) for m in SCORES[:score])
    block = G * P
    target = min(16 * block + done * 3 // 2, done + 34 * block)
    n, seen = 0, 0
    while n < len(MAX) and (seen < target or len(MAX[n]) == 1):
        seen += columns(MAX[n])
        n += 1
    need = 1 + next(i for i, m in enumerate(MAX) if m == (SCORES[score][0],))
    return max(n, need)


COLS = {"b_qk": (0, 4), "conv_w": (4, 20), "conv_b": (20, 24), "dt_b": (24, 28), "skip": (28, 32),
        "a_log": (32, 32 + KI * NS)}
NCOLS = 32 + KI * NS


def out_bank(tt):
    return 3 if tt < TPH else 2 + tt % 2


def in_steps(engine, step, steps):
    peeled = 2 * RING
    turns = (SLOTS - peeled) // RING
    for n in range(peeled):
        step(n, n // RING, n % RING)
    with engine.Fori(0, turns) as j:
        for b in range(RING):
            step(j * RING + (peeled + b), j + peeled // RING, b)
    for n in range(peeled + turns * RING, steps):
        step(n, n // RING, n % RING)


def tile_of(rows, n):
    return rows[bass.ds(n, 1), :, :].rearrange("s p d -> p (s d)")


def has_tile(n):
    return not isinstance(n, int) or 0 <= n < SLOTS


def counts(n):
    return not isinstance(n, int) or n > 0


LAST = SCORES.index(score_jobs(len(PHASES) - 1)[0])


def o_stages(step):
    return [i if 0 <= i < TPH else None for i in (step, step - 1, step - 2)]


def build(nc, a, out, scratch, slots, results):
    ctx = ExitStack()
    with ctx:
        def sb(name, shape, dt=F32):
            return ctx.enter_context(nc.sbuf_tensor(name, shape, dt))

        def sem(name):
            return ctx.enter_context(nc.semaphore(name))

        ps = ctx.enter_context(nc.psum_tensor("ps", [P, 8, TH], F32))
        psb = ps[:, :, :].rearrange("p b n -> p (b n)").bitcast(BF16).rearrange("p (b n) -> p b n", b=8)

        ident = sb("ident", [P, P])
        masks = sb("masks", [P, 4, P], BF16)
        identb, causal, earlier, all_ones = (masks[:, i, :] for i in range(4))
        zero_row = sb("zero_row", [P, D])
        cols = sb("cols", [P, NCOLS])
        x_tok = sb("x_tok", [P, NT, D])
        y_tok = sb("y_tok", [P, NT, D])
        x_feat = sb("x_feat", [P, KD, T])
        stats = sb("stats", [P, NT, 6])
        mv = sb("mv", [P, NT, 2])
        rstd = sb("rstd", [P, NT])
        minus_half = sb("minus_half", [P, NT])

        ARENA = 46240
        arena = sb("arena", [P, ARENA])
        at = [0]

        def take(words):
            lo = at[0]
            at[0] += words
            assert at[0] <= ARENA, at[0]
            return arena[:, lo:lo + words]

        def take_b(n):
            return take(n // 2).bitcast(BF16)

        w_g = take(KD * FF).rearrange("p (k b n) -> p k b n", k=KD, b=FB)
        w_u = take(KD * FF).rearrange("p (k b n) -> p k b n", k=KD, b=FB)
        w_d = take(FB * D).rearrange("p (b n) -> p b n", b=FB)
        w_o = take(KD * D).rearrange("p (k n) -> p k n", k=KD)
        o_feat = take(NG * T).rearrange("p (g t) -> p g t", g=NG)
        rden = take(2 * HEADS).rearrange("p (b h) -> p b h", b=2)
        o_tok = take(2 * D).rearrange("p (b d) -> p b d", b=2)
        o_nf = take(2 * D).rearrange("p (b k t) -> p b k t", b=2, k=KD)
        after_attention = at[0]
        w_qkv = take(KD * 3 * D).rearrange("p (k n) -> p k n", k=KD)
        bias_vo = take(2 * D).rearrange("p (b n) -> p b n", b=2)
        b_q4 = take(KD)
        nmax = take(NH * NT * G).rearrange("p (h t j) -> p h t j", h=NH, t=NT)
        nmax_r = take(TPH * G).rearrange("p (t j) -> p t j", t=TPH)
        nmax_p = take_b(2 * TPH * SPLIT * G).rearrange("p (b t c j) -> p b t c j", b=2, t=TPH, c=SPLIT)
        nmax_f = take_b(2 * TH).rearrange("p (b t) -> p b t", b=2)
        v_aug = take(NT * HEADS * VC).rearrange("p (s h c) -> p s h c", s=NT, h=HEADS)
        q_st = take_b(NH * HEADS * TH).rearrange("p (a h t) -> p a h t", a=NH, h=HEADS)
        k_st = take_b(NH * HEADS * TH).rearrange("p (a h t) -> p a h t", a=NH, h=HEADS)
        overlay = at[0]
        qk_full = take(8 * TH).rearrange("p (i t) -> p i t", i=8)
        qk_part = take_b(SPLIT * 4 * T).rearrange("p (c m t) -> p c m t", c=SPLIT, m=4)
        at[0] = overlay
        probs = take(3 * G * TH).rearrange("p (b j t) -> p b j t", b=3, j=G)

        assert at[0] <= ARENA
        at[0] = after_attention
        ff_s = take(2 * TH).rearrange("p (b t) -> p b t", b=2)
        ff_h = take(2 * GS * TH).rearrange("p (b j t) -> p b j t", b=2, j=GS)
        ff_a = take(2 * GS * TH).rearrange("p (b j t) -> p b j t", b=2, j=GS)
        ff_c = take_b(6 * TH).rearrange("p (c t) -> p c t", c=6)
        ff_w = take_b(GS * TH).rearrange("p (j t) -> p j t", j=GS)
        ff_k = take(FB * T).rearrange("p (b t) -> p b t", b=FB)
        after_ffn = at[0]
        sz = take(KI * T).rearrange("p (k t) -> p k t", k=KI)
        x_in_flat = take(KI * (T + TAPS))
        x_in = x_in_flat[:, 0:KI * (T + TAPS - 1)].rearrange("p (k t) -> p k t", k=KI)
        states_top = at[0]
        at[0] = ARENA - (KD * 2 * DI + KI * D + KI * XD + DI + BC * P // 2)
        assert at[0] >= states_top, (at[0], states_top)
        mamba_top = at[0]
        w_in = take(KD * 2 * DI).rearrange("p (k n) -> p k n", k=KD)
        late_w = w_in[:, :, :].rearrange("p k n -> p (k n)").rearrange("p (k t) -> p k t", k=KI)
        w_out = take(KI * D).rearrange("p (k n) -> p k n", k=KI)
        w_xp = take(KI * XD).rearrange("p (k n) -> p k n", k=KI)
        w_dt = take(DI)
        pick = take_b(BC * P).rearrange("p (r n) -> p r n", r=BC)
        at[0] = 0
        bc_p_flat = take(TH)
        bc_p = bc_p_flat.bitcast(BF16).rearrange("p (c t) -> p c t", c=2)
        bc_r = take(TH)
        dt_lo = take(T)
        late_e = [bc_r, bc_p_flat]
        assert at[0] <= SHARED * (KD * 2 * EI + 2 * D)
        at[0] = 0
        ws_gu = take(SHARED * KD * 2 * EI).rearrange("p (b k n) -> p b k n", b=SHARED, k=KD)
        ws_dn = take(SHARED * 2 * D).rearrange("p (b k n) -> p b k n", b=SHARED, k=2)
        w_r = take(KD * E).rearrange("p (k e) -> p k e", k=KD)
        e_s = take(2 * EI).rearrange("p (b n) -> p b n", b=2)
        e_h = take(2 * EI).rearrange("p (b n) -> p b n", b=2)
        e_f = take(2 * 2 * P).rearrange("p (b c t) -> p b c t", b=2, c=2)
        r_p = take(NT * E).rearrange("p (t e) -> p t e", t=NT)
        chosen = take(TOP * NT * E).rearrange("p (c t e) -> p c t e", c=TOP, t=NT)
        chosen_any = take_b(NT * E)
        r_q = take(TOP * NT * E).rearrange("p (c t e) -> p c t e", c=TOP, t=NT)
        r_max = take(NT)
        r_8 = take(NT * 8).rearrange("p (t e) -> p t e", t=NT)
        r_i = take(NT * 8).rearrange("p (t e) -> p t e", t=NT)
        r_if = take(NT * 8).rearrange("p (t e) -> p t e", t=NT)
        iota = take(E + NT + SLOTS)
        iota_e, fill_steps, iota_slot = iota[:, 0:E], iota[:, E:E + NT], iota[:, E + NT:]
        per_tile = take(E * NT)
        ones_r = take(E * NT)
        upto = take(E * NT)
        before = take(E * NT).rearrange("p (e t) -> p e t", e=E)
        place = take(NT * E).rearrange("p (t e) -> p t e", t=NT)
        count = take(E)
        tiles_of = take(E)
        end_tile = take(E)
        base = take(E)
        position_f = take(TOP * NT).rearrange("p (c t) -> p c t", c=TOP)
        position = take(TOP * NT).bitcast(U32).rearrange("p (c t) -> p c t", c=TOP)
        slot_f = take(SLOTS)
        slot_expert = take(SLOTS).bitcast(I32)
        bc3 = take_b(T)
        a_neg = take(KI * NS).rearrange("p (k n) -> p k n", k=KI)
        h_last = take(KI * NS).rearrange("p (k n) -> p k n", k=KI)
        assert at[0] <= KD * FF * 2 + FB * D, at[0]
        at[0] = KD * FF * 2 + FB * D
        xa_at = at[0]
        xa = take(KI * T).rearrange("p (k t) -> p k t", k=KI)
        dtx = take(KI * T).rearrange("p (k t) -> p k t", k=KI)
        dt_at = at[0]
        dt_ = take(KI * T).rearrange("p (k t) -> p k t", k=KI)
        scan_at = at[0]
        dBx = take(2 * KI * TH).rearrange("p (b k t) -> p b k t", b=2, k=KI)
        hs = take(2 * KI * TH).rearrange("p (b k t) -> p b k t", b=2, k=KI)
        hc = take(2 * KI * TH).rearrange("p (b k t) -> p b k t", b=2, k=KI)
        b_sb = take(2 * TH).rearrange("p (b t) -> p b t", b=2)
        assert at[0] <= after_ffn, (at[0], after_ffn)
        dA = x_in_flat[:, 0:2 * KI * TH].rearrange("p (b k t) -> p b k t", b=2, k=KI)
        at[0] = scan_at
        sp_e = take(KI * TH).rearrange("p (k t) -> p k t", k=KI)
        sp_l = take(KI * TH).rearrange("p (k t) -> p k t", k=KI)
        sp_w = take(KI * TH).rearrange("p (k t) -> p k t", k=KI)
        assert at[0] <= after_ffn
        at[0] = xa_at
        slot_x = take(RING * D).rearrange("p (b d) -> p b d", b=RING)
        slot_y = take(RING * D).rearrange("p (b d) -> p b d", b=RING)
        slot_xf = take(2 * D).rearrange("p (b k t) -> p b k t", b=2, k=KD)
        assert at[0] <= xa_at + KI * T
        at[0] = dt_at
        w_gu = take(E * KD * 2 * EI).rearrange("p (e k n) -> p e k n", e=E, k=KD)
        w_dn = take(E * 2 * D).rearrange("p (e k n) -> p e k n", e=E, k=2)
        picked_flat = take(TOP * NT * D)
        picked = picked_flat.rearrange("p (c t d) -> p c t d", c=TOP, t=NT)
        assert at[0] <= mamba_top

        ld_x = sem("ld_x")
        ld_wqkv = sem("ld_wqkv")
        ld_small = sem("ld_small")
        ld_tok = sem("ld_tok")
        ld_wo = sem("ld_wo")
        parts_out = [sem(f"parts_out{i}") for i in range(len(QK_ORDER))]
        st_loaded = [sem(f"st_loaded{i}") for i in range(NH * KD)]
        nmax_loaded = [sem(f"nmax_loaded{i}") for i in range(len(PHASES))]
        stored = sem("stored")
        bias_ready = sem("bias_ready")
        qk_ready = sem("qk_ready")
        qk_taken = sem("qk_taken")
        qk_rest = sem("qk_rest")
        qk_mid = sem("qk_mid")
        parts_ready = sem("parts_ready")
        v_ready = sem("v_ready")
        v_taken = sem("v_taken")
        ones_ready = sem("ones_ready")
        max_ready = sem("max_ready")
        max_taken = sem("max_taken")
        nmax_parts = sem("nmax_parts")
        nmaxT_ready = sem("nmaxT_ready")
        nmax_feat = sem("nmax_feat")
        scores_ready = sem("scores_ready")
        probs_ready = sem("probs_ready")
        pv_done = sem("pv_done")
        o_taken = sem("o_taken")
        vec_own = sem("vec_own")
        ld_ffw = sem("ld_ffw")
        ld_mamba = sem("ld_mamba")
        ld_router = sem("ld_router")
        xb_ready = sem("xb_ready")
        oT_ready = sem("oT_ready")
        o_norm = sem("o_norm")
        oN_ready = sem("oN_ready")
        onf_ready = sem("onf_ready")
        wo_ready = sem("wo_ready")
        y_ready = sem("y_ready")
        tile_stats = sem("tile_stats")
        stats_ready = sem("stats_ready")
        rstd_ready = sem("rstd_ready")
        norm_ready = sem("norm_ready")
        xT_ready = sem("xT_ready")
        feat_ready = sem("feat_ready")
        gu_ready = sem("gu_ready")
        silu_ready = sem("silu_ready")
        ffh_ready = sem("ffh_ready")
        abs_ready = sem("abs_ready")
        kept_ready = sem("kept_ready")
        down_ready = sem("down_ready")
        inx_ready = sem("inx_ready")
        xin_ready = sem("xin_ready")
        xacc_ready = sem("xacc_ready")
        conv_done = sem("conv_done")
        xa_ready = sem("xa_ready")
        z_ready = sem("z_ready")
        xd_ready = sem("xd_ready")
        bc_ready = sem("bc_ready")
        dt_ready = sem("dt_ready")
        dtp_ready = sem("dtp_ready")
        dt_positive = sem("dt_positive")
        sp_exp = sem("sp_exp")
        sp_w_ready = sem("sp_w_ready")
        sp_ln = sem("sp_ln")
        sp_d_used = sem("sp_d_used")
        dt_done = sem("dt_done")
        u_done = sem("u_done")
        a_exp = sem("a_exp")
        a_ready = sem("a_ready")
        b_ready = sem("b_ready")
        c_ready = sem("c_ready")
        b_copied = sem("b_copied")
        dA_ready = sem("dA_ready")
        dBx_ready = sem("dBx_ready")
        scanned = sem("scanned")
        cmul_done = sem("cmul_done")
        y_acc = sem("y_acc")
        y_part = sem("y_part")
        ym_ready = sem("ym_ready")
        mout_ready = sem("mout_ready")
        logit_ready = sem("logit_ready")
        r_sub = sem("r_sub")
        r_exp = sem("r_exp")
        choice_ready = sem("choice_ready")
        rank_ready = sem("rank_ready")
        position_ready = sem("position_ready")
        slot_expert_ready = sem("slot_expert_ready")
        slots_zeroed = sem("slots_zeroed")
        scattered = sem("scattered")
        shared_added = sem("shared_added")
        slot_xT_ready = sem("slot_xT_ready")
        slot_xf_ready = sem("slot_xf_ready")
        slot_gu_ready = sem("slot_gu_ready")
        slot_silu_ready = sem("slot_silu_ready")
        slot_h_ready = sem("slot_h_ready")
        slot_hT_ready = sem("slot_hT_ready")
        slot_hf_ready = sem("slot_hf_ready")
        slot_down_ready = sem("slot_down_ready")
        slot_y_ready = sem("slot_y_ready")
        slot_loaded = [sem(f"slot_loaded{i}") for i in range(RING)]
        slot_stored = [sem(f"slot_stored{i}") for i in range(RING)]
        picked_ready = [sem(f"picked_ready{i}") for i in range(NT)]
        zero_ready = sem("zero_ready")
        egu_ready = sem("egu_ready")
        es_ready = sem("es_ready")
        eh_ready = sem("eh_ready")
        eT_ready = sem("eT_ready")
        ef_ready = sem("ef_ready")
        edn_ready = sem("edn_ready")
        act_own = sem("act_own")
        ld_shared = sem("ld_shared")
        ld_experts = sem("ld_experts")
        block = ctx.enter_context(nc.Block())

        @block.sync
        def _(sp):
            for k in range(KD):
                sp.dma_start(w_qkv[:, k, :], a["w_qkv"][:, k, :]).then_inc(ld_wqkv, DMA)
                sp.dma_start(x_feat[:, k, :], a["x_feat"][:, k, :]).then_inc(ld_x, DMA)
            sp.dma_start(cols[:, :], a["cols"]).then_inc(ld_small, DMA)
            sp.dma_start(bias_vo[:, :, :], a["bias_vo"]).then_inc(ld_small, DMA)
            sp.dma_start(masks[:, :, :], a["masks"].bitcast(BF16)).then_inc(ld_small, DMA)
            sp.dma_start(ident[:, :], a["ident"]).then_inc(ld_small, DMA)
            for chunk in range(NH * KD):
                h, pair = divmod(chunk, KD)
                for qk in range(2):
                    i = 2 * chunk + qk
                    m = QK_ORDER[i][0]
                    sp.wait_ge(parts_ready, i + 1)
                    sp.dma_start(scratch[i].rearrange("c p t -> p c t"), qk_part[:, :, m, h * TH:(h + 1) * TH]).then_inc(parts_out[i], DMA)
                heads = slice(pair * HPT, (pair + 1) * HPT)
                for qk, st in ((0, q_st), (1, k_st)):
                    i = 2 * chunk + qk
                    sp.wait_ge(parts_out[i], DMA)
                    for slot, n in ((0, 3), (3, 2), (5, 1)):
                        if qk == 0:
                            src = scratch[i, 0:n].rearrange("c (r h) t -> (c r) (h t)", h=HPT)
                        else:
                            part = {0: 0, 3: 1, 5: 2}[slot]
                            src = scratch[i, part:part + 1].rearrange("c (r h) t -> c r (h t)", h=HPT).broadcast_to([n, HD, HPT * TH])
                        dst = st[slot * HD:(slot + n) * HD, h, heads, :]
                        sp.dma_start(dst, src).then_inc(st_loaded[chunk], DMA)
            sp.dma_start(x_tok[:, :, :], a["x_tok"]).then_inc(ld_tok, DMA)
            sp.dma_start(w_o[:, :, :], a["w_o"]).then_inc(ld_wo, DMA)
            for phase, (h, g) in enumerate(PHASES):
                sp.wait_ge(nmax_feat, phase + 1)
                for c in range(SPLIT):
                    sp.dma_start(q_st[KROWS + c:KROWS + c + 1, h, G * g:G * g + G, :],
                                 nmax_f[c * G:(c + 1) * G, phase % 2, :]).then_inc(nmax_loaded[phase], DMA)
                if phase == NG - 1:
                    sp.dma_start(w_g[:, :, :, :], a["w_g"]).then_inc(ld_ffw, DMA)
                    sp.dma_start(w_u[:, :, :, :], a["w_u"]).then_inc(ld_ffw, DMA)
                    sp.dma_start(w_d[:, :, :], a["w_d"]).then_inc(ld_ffw, DMA)
            sp.wait_ge(ones_ready, 4)
            sp.dma_start(slots.rearrange("s p d -> p s d"),
                         zero_row[:, :].unsqueeze(1).broadcast_to([P, SLOTS, D])).then_inc(slots_zeroed, DMA)
            sp.wait_ge(pv_done, first_round(len(PHASES)))
            sp.dma_start(w_in[:, :, :], a["w_in"]).then_inc(ld_mamba, DMA)
            sp.dma_start(w_xp[:, :, :], a["w_xp"]).then_inc(ld_mamba, DMA)
            sp.dma_start(w_dt[3 * BC:XD, :], a["w_dt"]).then_inc(ld_mamba, DMA)
            sp.dma_start(pick[0:3 * BC, :, :], a["pick"].bitcast(BF16)).then_inc(ld_mamba, DMA)
            sp.dma_start(w_out[:, :, :], a["w_out"]).then_inc(ld_mamba, DMA)
            sp.wait_ge(down_ready, NT)
            sp.dma_start(w_r[:, :, :], a["w_r"]).then_inc(ld_router, DMA)
            sp.dma_start(iota[:, :], a["iota"]).then_inc(ld_router, DMA)
            sp.wait_ge(dt_done, NH * KI)
            sp.dma_start(ws_gu[:, :, :, :], a["ws_gu"]).then_inc(ld_shared, DMA)
            sp.dma_start(ws_dn[0:EH, :, :, :], a["ws_dn"]).then_inc(ld_shared, DMA)
            sp.wait_ge(y_acc, NH * NS)
            sp.wait_ge(ym_ready, NH * KI)
            for e in range(0, E, E // 4):
                es = slice(e, e + E // 4)
                sp.dma_start(w_gu[:, es, :, :], a["w_gu"][:, es]).then_inc(ld_experts, DMA)
                sp.dma_start(w_dn[0:EH, es, :, :], a["w_dn"][:, es]).then_inc(ld_experts, DMA)

            def exchange(n, turn, b):
                if has_tile(n):
                    if counts(n - RING + 1):
                        sp.wait_ge(slot_xT_ready, n - RING + 1)
                    sp.dma_start(slot_x[:, b, :], tile_of(slots, n)).then_inc(slot_loaded[b], DMA)
                if has_tile(n - 2 * RING):
                    sp.wait_ge(slot_y_ready, n - 2 * RING + 1)
                    sp.dma_start(tile_of(results, n - 2 * RING), slot_y[:, b, :]).then_inc(slot_stored[b], DMA)

            sp.wait_ge(slots_zeroed, DMA)
            sp.wait_ge(scattered, TOP * NT * DMA)
            in_steps(sp, exchange, SLOTS + 2 * RING)
            for h in range(NH):
                sp.wait_ge(norm_ready, 3 * NT + (h + 1) * TPH)
                sp.dma_start(out[:, h * TPH:(h + 1) * TPH, :], x_tok[:, h * TPH:(h + 1) * TPH, :]).then_inc(stored, DMA)
            sp.wait_ge(stored, NH * DMA)

        @block.gpsimd
        def _(pool):
            nc.gpsimd.memset(v_aug[:, :, :, HD:VC], 1.0).then_inc(ones_ready, 1)
            pool.wait_ge(ones_ready, 1)
            nc.gpsimd.memset(k_st[KROWS:KX, :, :, :], 1.0).then_inc(ones_ready, 1)
            pool.wait_ge(ones_ready, 2)
            nc.gpsimd.memset(minus_half[:, :], -0.5).then_inc(ones_ready, 1)
            nc.gpsimd.memset(zero_row[:, :], 0.0).then_inc(ones_ready, 1)

            pool.wait_ge(ld_tok, DMA)
            pool.wait_ge(ld_small, 4 * DMA)
            nc.gpsimd.tensor_tensor(x_tok[:, :, :], x_tok[:, :, :],
                                    bias_vo[:, 1, :].unsqueeze(1).broadcast_to([P, NT, D]), ALU.add).then_inc(xb_ready, 1)

            def inverse_deviation(layer, h):
                n = layer * NH + h + 1
                tts = slice(h * TPH, (h + 1) * TPH)
                pool.wait_ge(stats_ready, n)
                nc.gpsimd.tensor_tensor(rstd[:, tts], mv[:, tts, 1], minus_half[:, tts], ALU.pow).then_inc(rstd_ready, 1)

            for h in range(NH):
                inverse_deviation(0, h)
            nc.gpsimd.memset(x_in[:, :, 0:TAPS - 1], 0.0).then_inc(zero_ready, 1)
            for h in range(NH):
                inverse_deviation(1, h)
            pool.wait_ge(down_ready, NT)
            nc.gpsimd.memset(ones_r, 1.0).then_inc(zero_ready, 1)
            def times_x(h):
                for k in range(KI):
                    pool.wait_ge(dt_done, h * KI + k + 1)
                    nc.gpsimd.tensor_tensor(dtx[:, k, h * TH:(h + 1) * TH], dt_[:, k, h * TH:(h + 1) * TH],
                                            xa[:, k, h * TH:(h + 1) * TH], ALU.mult).then_inc(u_done, 1)
                pool.wait_ge(u_done, (h + 1) * KI)

            times_x(0)
            for i in range(NH * NS):
                h, n = divmod(i, NS)
                pool.wait_ge(b_copied, i + 1)
                if i >= 2:
                    pool.wait_ge(scanned, KI * (i - 1))
                nc.gpsimd.tensor_tensor(dBx[:, i % 2, :, :], dtx[:, :, h * TH:(h + 1) * TH],
                                        b_sb[:, i % 2, :].unsqueeze(1).broadcast_to([P, KI, TH]),
                                        ALU.mult).then_inc(dBx_ready, 1)
                if i == 11:
                    times_x(1)
                if i == NS + 6:
                    inverse_deviation(2, 0)
            inverse_deviation(2, 1)
            pool.wait_ge(slots_zeroed, DMA)
            pool.wait_ge(norm_ready, 3 * NT)
            pool.wait_ge(position_ready, 1)
            for tt in range(NT):
                for c in range(TOP):
                    to = bass.IndirectOffsetOnAxis(ap=position[:, c, tt:tt + 1], axis=0)
                    nc.gpsimd.indirect_dma_start(slots.rearrange("s p d -> (s p) d"), to, x_tok[:, tt, :], None).then_inc(scattered, DMA)
            for b in range(RING):
                pool.wait_ge(slot_stored[b], len(range(b, SLOTS, RING)) * DMA)
            for tt in range(NT):
                for c in range(TOP):
                    where = bass.IndirectOffsetOnAxis(ap=position[:, c, tt:tt + 1], axis=0)
                    nc.gpsimd.indirect_dma_start(picked[:, c, tt, :], None, results.rearrange("s p d -> (s p) d"), where).then_inc(picked_ready[tt], DMA)
            for h in range(NH):
                inverse_deviation(3, h)

        @block.tensor
        def _(pe):
            pe.wait_ge(ld_wqkv, KD * DMA)
            pe.wait_ge(ld_x, KD * DMA)
            for h in range(NH):
                for i in range(h * 2 * KD, (h + 1) * 2 * KD):
                    m = QK_ORDER[i][0]
                    for k in range(KD):
                        mm = nc.tensor.matmul(ps[:, i, :], w_qkv[:, k, m * P:(m + 1) * P],
                                              x_feat[:, k, h * TH:(h + 1) * TH], start=(k == 0), stop=(k == KD - 1))
                    mm.then_inc(qk_ready, 1)
                for tt in range(h * TPH, (h + 1) * TPH):
                    pe.wait_ge(qk_taken, tt + 1)
                    for k in range(KD):
                        mm = nc.tensor.matmul(ps[:, tt, 0:D], x_feat[:, k, tt * P:(tt + 1) * P],
                                              w_qkv[:, k, 2 * D:3 * D], start=(k == 0), stop=(k == KD - 1))
                    mm.then_inc(v_ready, 1)

            def max_entry(n):
                if n >= RB:
                    before = MAX[:n - RB + 1]
                    if len(before[-1]) == 1:
                        pe.wait_ge(nmax_feat, sum(len(m) == 1 for m in before))
                    else:
                        pe.wait_ge(max_taken, sum(len(m) > 1 for m in before))
                bank = n % RB
                if len(MAX[n]) == 1:
                    phase = MAX[n][0]
                    pe.wait_ge(nmax_parts, phase + 1)
                    for i in range(TPH):
                        mm = nc.tensor.transpose(psb[0:SPLIT * G, bank, i * P:(i + 1) * P],
                                                 nmax_p[:, phase % 2, i, :, :].rearrange("p c j -> p (c j)"), identb)
                    mm.then_inc(nmaxT_ready, 1)
                    return
                phase, tt, half, w, js = MAX[n]
                h, g = PHASES[phase]
                if n == 0 or MAX[n - 1][0] != phase:
                    pe.wait_ge(st_loaded[h * KD + g // 2], 6 * DMA)
                for a_, j in enumerate(js):
                    c = a_ * w
                    head = G * g + j
                    diagonal = half == h
                    mm = nc.tensor.matmul(ps[:, bank, c:c + w], q_st[0:KROWS, h, head, (tt % TPH) * P:(tt % TPH + 1) * P],
                                          k_st[0:KROWS, half, head, 0:w], start=True, stop=not diagonal)
                    if diagonal:
                        mm = nc.tensor.matmul(ps[:, bank, c + w - P:c + w], causal, identb, start=False, stop=True)
                mm.then_inc(max_ready, 1)

            def score(n):
                phase, st, w, js = SCORES[n]
                h, g = PHASES[phase]
                if n >= RB:
                    pe.wait_ge(probs_ready, n - RB + 1)
                if n == 0 or SCORES[n - 1][0] != phase:
                    pe.wait_ge(nmax_loaded[phase], SPLIT * DMA)
                for a_, j in enumerate(js):
                    c = a_ * w
                    head = G * g + j
                    diagonal = st // TPH == h
                    mm = nc.tensor.matmul(ps[:, RB + n % RB, c:c + w], k_st[0:KX, st // TPH, head, (st % TPH) * P:(st % TPH + 1) * P],
                                          q_st[0:KX, h, head, TH - w:TH], start=True, stop=not diagonal)
                    if diagonal:
                        mm = nc.tensor.matmul(ps[:, RB + n % RB, c:c + P], identb, causal, start=False, stop=True)
                mm.then_inc(scores_ready, 1)

            def values(phase, st):
                h, g = PHASES[phase]
                r = first_round(phase) + st
                pe.wait_ge(probs_ready, 1 + max(i for i, s in enumerate(SCORES) if s[:2] == (phase, st)))
                if st == 0 and phase >= 2:
                    pe.wait_ge(o_taken, phase - 1)
                w = min(TH, (h + 1) * TH - st * P)
                for j in range(G):
                    mm = nc.tensor.matmul(ps[VC * j:VC * (j + 1), 6 + phase % 2, TH - w:TH], v_aug[:, st, G * g + j, :],
                                          probs[:, r % 3, j, 0:w], start=(st == 0), stop=(st == (h + 1) * TPH - 1))
                mm.then_inc(pv_done, 1)

            def o_transposes(tt):
                if tt:
                    pe.wait_ge(o_norm, tt)
                for g in range(NG):
                    mm = nc.tensor.transpose(ps[:, 4 * (tt // TPH), g * P:(g + 1) * P], o_feat[:, g, tt * P:(tt + 1) * P], ident[:, :])
                mm.then_inc(oT_ready, 1)

            def o_back(tt):
                pe.wait_ge(o_norm, tt + 1)
                if tt:
                    pe.wait_ge(onf_ready, tt)
                for k in range(KD):
                    mm = nc.tensor.transpose(ps[:, 4 * (tt // TPH) + 1, k * P:(k + 1) * P], o_tok[:, tt % 2, k * P:(k + 1) * P], ident[:, :])
                mm.then_inc(oN_ready, 1)

            def o_project(tt):
                pe.wait_ge(onf_ready, tt + 1)
                if tt:
                    pe.wait_ge(y_ready, tt)
                for k in range(KD):
                    mm = nc.tensor.matmul(ps[:, 4 * (tt // TPH) + 2, 0:D], o_nf[:, tt % 2, k, :], w_o[:, k, :],
                                          start=(k == 0), stop=(k == KD - 1))
                mm.then_inc(wo_ready, 1)

            def o_step(h, step):
                for stage, i in zip((o_transposes, o_back, o_project), o_stages(step)):
                    if i is not None:
                        stage(h * TPH + i)

            def to_features(layer, h):
                bank = 6 if layer or h else 0
                if layer or h:
                    pe.wait_ge(feat_ready, layer * NH + h)
                for tt in range(h * TPH, (h + 1) * TPH):
                    pe.wait_ge(norm_ready, layer * NT + tt + 1)
                    for k in range(KD):
                        c = (tt - h * TPH) * P
                        mm = nc.tensor.transpose(ps[:, bank + k, c:c + P], x_tok[:, tt, k * P:(k + 1) * P], ident[:, :])
                mm.then_inc(xT_ready, 1)

            pe.wait_ge(ones_ready, 3)
            pe.wait_ge(ld_small, 4 * DMA)
            pe.wait_ge(v_taken, NT)
            issued = 0
            for n, job in enumerate(SCORES):
                while issued < max_jobs_before(n):
                    max_entry(issued)
                    issued += 1
                if n == LAST:
                    pe.wait_ge(ld_wo, DMA)
                    pe.wait_ge(o_taken, NG)
                    pe.wait_ge(nmax_feat, len(PHASES))
                score(n)
                if n >= LAST and (n - LAST) % PACE == 0 and (n - LAST) // PACE < TPH + 2:
                    o_step(0, (n - LAST) // PACE)
                if n >= LAG and SCORES[n - LAG][:2] != SCORES[n - LAG + 1][:2]:
                    values(*SCORES[n - LAG][:2])
            to_features(0, 0)
            for n in range(len(SCORES) - LAG, len(SCORES) - 1):
                if SCORES[n][:2] != SCORES[n + 1][:2]:
                    values(*SCORES[n][:2])
            values(*SCORES[-1][:2])

            def gate_up(n):
                h, b = divmod(n, FB)
                pe.wait_ge(feat_ready, h + 1)
                if n >= 2:
                    pe.wait_ge(ffh_ready, n - 1)
                for w, bank in ((w_g, 2 * (n % 2)), (w_u, 2 * (n % 2) + 1)):
                    for k in range(KD):
                        mm = nc.tensor.matmul(ps[:, bank, :], w[:, k, b, :], x_feat[:, k, h * TH:(h + 1) * TH],
                                              start=(k == 0), stop=(k == KD - 1))
                mm.then_inc(gu_ready, 1)

            def down(h):
                for tt in range(h * TPH, (h + 1) * TPH):
                    pe.wait_ge(y_ready, NT + tt - 1)
                    for b in range(FB):
                        if tt % TPH == 0:
                            pe.wait_ge(kept_ready, tt // TPH * FB + b + 1)
                        mm = nc.tensor.matmul(ps[:, 4 + tt % 2, 0:D], ff_k[:, b, tt * P:(tt + 1) * P], w_d[:, b, :],
                                              start=(b == 0), stop=(b == FB - 1))
                    mm.then_inc(down_ready, 1)

            def in_projection(h):
                pe.wait_ge(feat_ready, NH + h + 1)
                for m in range(2 * KI):
                    if m >= KI:
                        pe.wait_ge(xin_ready, h * KI + m - KI + 1)
                    elif h == 0 and m == 2:
                        pe.wait_ge(ffh_ready, NH * FB)
                    elif h:
                        pe.wait_ge(dt_positive, (h - 1) * KI + m + 1)
                    for k in range(KD):
                        mm = nc.tensor.matmul(ps[:, m % 4, :], w_in[:, k, m * P:(m + 1) * P], x_feat[:, k, h * TH:(h + 1) * TH],
                                              start=(k == 0), stop=(k == KD - 1))
                    mm.then_inc(inx_ready, 1)

            def x_projection(h):
                for k in range(KI):
                    pe.wait_ge(xa_ready, h * KI + k + 1)
                    mm = nc.tensor.matmul(ps[0:XD, 4 - h, :], w_xp[:, k, :], xa[:, k, h * TH:(h + 1) * TH],
                                          start=(k == 0), stop=(k == KI - 1))
                mm.then_inc(xd_ready, 1)

            def dt_projection(h, k):
                if k == 0:
                    pe.wait_ge(dt_ready, h + 1)
                if h == 0:
                    pe.wait_ge(z_ready, k + 1)
                elif k == 0:
                    pe.wait_ge(bc_ready, h + 1)
                else:
                    pe.wait_ge(dt_positive, KI + k)
                nc.tensor.matmul(ps[:, 3 if h else k, :], w_dt[3 * BC:XD, k * P:(k + 1) * P], dt_lo[3 * BC:XD, h * TH:(h + 1) * TH],
                                 start=True, stop=True).then_inc(dtp_ready, 1)

            pe.wait_ge(ld_ffw, 3 * DMA)
            pe.wait_ge(o_taken, len(PHASES))
            for n in range(FB):
                o_step(1, n)
                gate_up(n)
            to_features(0, 1)
            for n in range(FB, FB + AHEAD):
                gate_up(n)
            down(0)
            for n in range(FB + AHEAD, NH * FB):
                gate_up(n)
            to_features(1, 0)
            pe.wait_ge(ld_mamba, 5 * DMA)
            pe.wait_ge(ffh_ready, NH * FB - 1)
            in_projection(0)
            down(1)
            pe.wait_ge(y_ready, 2 * NT)
            x_projection(0)
            to_features(1, 1)
            for k in range(KI):
                dt_projection(0, k)
            in_projection(1)

            def broadcast_b(i):
                h, n = divmod(i, NS)
                pe.wait_ge(bc_ready, h + 1)
                if i:
                    pe.wait_ge(b_copied, i)
                nc.tensor.matmul(ps[:, 0, :], pick[0:3 * BC, n, :], bc3[0:3 * BC, h * TH:(h + 1) * TH],
                                 start=True, stop=True).then_inc(b_ready, 1)

            def broadcast_c(i):
                h, n = divmod(i, NS)
                if i >= 2:
                    pe.wait_ge(cmul_done, i - 1)
                nc.tensor.matmul(ps[:, 1 + i % 2, :], pick[0:3 * BC, NS + n, :], bc3[0:3 * BC, h * TH:(h + 1) * TH],
                                 start=True, stop=True).then_inc(c_ready, 1)

            def accumulate(i):
                h, n = divmod(i, NS)
                last = i == NH * NS - 1
                if not last:
                    pe.wait_ge(cmul_done, i + 1)
                if h and n == 0:
                    pe.wait_ge(y_part, h * KI)
                for k in range(KI):
                    if last:
                        pe.wait_ge(cmul_done, i + k + 1)
                    mm = nc.tensor.matmul(ps[:, 4 + k, :], ident[:, :], hc[:, i % 2, k, :], start=(n == 0), stop=(n == NS - 1))
                    if last or k == KI - 1:
                        mm.then_inc(y_acc, 1)

            def mamba_out(tt):
                pe.wait_ge(y_ready, 2 * NT + (tt if tt < TPH else tt - 1))
                for k in range(KI):
                    pe.wait_ge(ym_ready, tt // TPH * KI + k + 1)
                    mm = nc.tensor.matmul(ps[:, out_bank(tt), 0:D], dtx[:, k, tt * P:(tt + 1) * P], w_out[:, k, :],
                                          start=(k == 0), stop=(k == KI - 1))
                mm.then_inc(mout_ready, 1)

            pe.wait_ge(z_ready, NH * KI)
            pe.wait_ge(feat_ready, 2 * NH)
            broadcast_b(0)
            broadcast_c(0)
            broadcast_b(1)
            for i in range(NH * NS):
                if i + 2 < NH * NS:
                    broadcast_b(i + 2)
                if i + 1 < NH * NS:
                    broadcast_c(i + 1)
                if i == 0:
                    x_projection(1)
                if 0 <= i - 3 < KI:
                    dt_projection(1, i - 3)
                if i:
                    accumulate(i - 1)
                if NS + 1 <= i <= NS + TPH:
                    mamba_out(i - NS - 1)
            accumulate(NH * NS - 1)
            for tt in range(TPH, NT):
                mamba_out(tt)

            pe.wait_ge(ld_router, 2 * DMA)
            pe.wait_ge(y_part, NH * KI)
            for h in range(NH):
                to_features(2, h)
                pe.wait_ge(feat_ready, 2 * NH + h + 1)
                for tt in range(h * TPH, (h + 1) * TPH):
                    for k in range(KD):
                        mm = nc.tensor.matmul(ps[:, 5 + h, tt * E:(tt + 1) * E], x_feat[:, k, tt * P:(tt + 1) * P], w_r[:, k, :],
                                              start=(k == 0), stop=(k == KD - 1))
                mm.then_inc(logit_ready, 1)

            def shared_up(n):
                tt, s = divmod(n, SHARED)
                if n >= 2:
                    pe.wait_ge(eh_ready, n - 1)
                for k in range(KD):
                    mm = nc.tensor.matmul(ps[:, n % 2, 0:2 * EI], x_feat[:, k, tt * P:(tt + 1) * P], ws_gu[:, s, k, :],
                                          start=(k == 0), stop=(k == KD - 1))
                mm.then_inc(egu_ready, 1)

            def shared_transposes(n):
                pe.wait_ge(eh_ready, n + 1)
                if n >= 2:
                    pe.wait_ge(ef_ready, n - 1)
                for c in range(2):
                    mm = nc.tensor.transpose(ps[0:EH, 2 + n % 2, c * P:(c + 1) * P], e_h[:, n % 2, c * EH:(c + 1) * EH], ident[:, :])
                mm.then_inc(eT_ready, 1)

            def shared_down(n):
                tt, s = divmod(n, SHARED)
                pe.wait_ge(ef_ready, n + 1)
                if s == 0 and tt >= 2:
                    pe.wait_ge(shared_added, tt - 1)
                for c in range(2):
                    mm = nc.tensor.matmul(ps[:, 4 + tt % 2, 0:D], e_f[0:EH, n % 2, c, :], ws_dn[0:EH, s, c, :],
                                          start=(s == 0 and c == 0), stop=(s == SHARED - 1 and c == 1))
                mm.then_inc(edn_ready, 1)

            pe.wait_ge(ld_shared, 2 * DMA)
            pe.wait_ge(y_ready, 3 * NT)
            def shared_expert(first, end):
                for n in range(first, end + 2):
                    if n < end:
                        shared_up(n)
                    if first < n <= end:
                        shared_transposes(n - 1)
                    if n >= first + 2:
                        shared_down(n - 2)
                    if n == 2:
                        count_choices()

            def count_choices():
                pe.wait_ge(choice_ready, 1)
                nc.tensor.matmul(ps[:, 6, P:2 * P], all_ones, chosen_any, start=True, stop=True)
                nc.tensor.matmul(ps[:, 6, 2 * P:3 * P], earlier, chosen_any, start=True, stop=True).then_inc(rank_ready, 1)

            shared_expert(0, SHARED * EARLY)

            def slot_tile(n, turn, b):
                if has_tile(n):
                    pe.wait_ge(slot_loaded[b], turn * DMA + DMA)
                    if counts(n - 1):
                        pe.wait_ge(slot_xf_ready, n - 1)
                    for k in range(KD):
                        mm = nc.tensor.transpose(ps[:, 6 + b % 2, k * P:(k + 1) * P], slot_x[:, b, k * P:(k + 1) * P], ident[:, :])
                    mm.then_inc(slot_xT_ready, 1)
                if has_tile(n - 1):
                    expert = pe.value_load(slot_expert[0:1, bass.ds(n - 1, 1)], min_val=0, max_val=E - 1)
                    pe.wait_ge(slot_xf_ready, n)
                    if counts(n - 2):
                        pe.wait_ge(slot_h_ready, n - 2)
                    for k in range(KD):
                        mm = nc.tensor.matmul(ps[:, (b + 1) % 2, 0:2 * EI], slot_xf[:, (b + 1) % 2, k, :],
                                              w_gu[:, bass.ds(expert, 1), k, :], start=(k == 0), stop=(k == KD - 1))
                    mm.then_inc(slot_gu_ready, 1)
                if has_tile(n - 2):
                    pe.wait_ge(slot_h_ready, n - 1)
                    if counts(n - 3):
                        pe.wait_ge(slot_hf_ready, n - 3)
                    for c in range(2):
                        mm = nc.tensor.transpose(ps[0:EH, 2 + b % 2, c * P:(c + 1) * P], e_h[:, b % 2, c * EH:(c + 1) * EH], ident[:, :])
                    mm.then_inc(slot_hT_ready, 1)
                if has_tile(n - 3):
                    expert = pe.value_load(slot_expert[0:1, bass.ds(n - 3, 1)], min_val=0, max_val=E - 1)
                    pe.wait_ge(slot_hf_ready, n - 2)
                    if counts(n - 4):
                        pe.wait_ge(slot_y_ready, n - 4)
                    for c in range(2):
                        mm = nc.tensor.matmul(ps[:, 4 + (b + 1) % 2, 0:D], e_f[0:EH, (b + 1) % 2, c, :],
                                              w_dn[0:EH, bass.ds(expert, 1), c, :], start=(c == 0), stop=(c == 1))
                    mm.then_inc(slot_down_ready, 1)

            pe.wait_ge(ld_experts, 8 * DMA)
            pe.wait_ge(slot_expert_ready, 1)
            pe.wait_ge(shared_added, EARLY)
            in_steps(pe, slot_tile, SLOTS + 3)
            pe.wait_ge(slot_y_ready, SLOTS)
            shared_expert(SHARED * EARLY, SHARED * NT)

        @block.scalar
        def _(act):
            act.wait_ge(ld_small, 4 * DMA)
            act.wait_ge(bias_ready, 1)
            for i, (m, h) in enumerate(QK_ORDER):
                act.wait_ge(qk_ready, i + 1)
                bias = b_q4[:, m:m + 1] if m < KD else cols[:, m:m + 1]
                scale = HD ** -0.5 if m < KD else 1.0
                nc.scalar.activation(qk_full[:, i, :], ps[:, i, :], ACT.Identity, bias=bias, scale=scale)
                nc.scalar.activation(qk_part[:, 0, m, h * TH:(h + 1) * TH], ps[:, i, :], ACT.Identity,
                                     bias=bias, scale=scale).then_inc(qk_taken, 1)

            def evacuate(phase):
                h, g = PHASES[phase]
                act.wait_ge(pv_done, first_round(phase + 1))
                nc.scalar.activation(o_feat[:, g, h * TH:(h + 1) * TH], ps[:, 6 + phase % 2, :], ACT.Copy).then_inc(o_taken, 1)

            for n, (phase, st, w, js) in enumerate(SCORES):
                r = first_round(phase) + st
                act.wait_ge(scores_ready, n + 1)
                if r >= 3:
                    act.wait_ge(pv_done, r - 2)
                elif n == 0:
                    for sent in parts_out:
                        act.wait_ge(sent, DMA)
                nc.scalar.activation(probs[:, r % 3, js[0]:js[-1] + 1, 0:w],
                                     ps[:, RB + n % RB, 0:w * len(js)].rearrange("p (j t) -> p j t", t=w), ACT.Exp).then_inc(probs_ready, 1)
                if phase and st == 2 and SCORES[n + 1][1] != 2:
                    evacuate(phase - 1)
            evacuate(len(PHASES) - 1)

            def features(layer, h):
                act.wait_ge(xT_ready, layer * NH + h + 1)
                nc.scalar.activation(x_feat[:, :, h * TH:(h + 1) * TH], ps[:, 6:8, :], ACT.Copy).then_inc(feat_ready, 1)

            def magnitude(n):
                h, b = divmod(n, FB)
                q = n // GS % 2
                act.wait_ge(ffh_ready, n + 1)
                if n >= 2 * GS:
                    act.wait_ge(kept_ready, (n // GS - 1) * GS)
                nc.scalar.activation(ff_a[:, q, b % GS, :], ff_h[:, q, b % GS, :], ACT.Abs).then_inc(abs_ready, 1)

            for h in range(NH):
                if h:
                    features(0, h)
                for b in range(FB):
                    n = h * FB + b
                    act.wait_ge(gu_ready, n + 1)
                    if n >= 2:
                        act.wait_ge(ffh_ready, n - 1)
                    nc.scalar.activation(ff_s[:, n % 2, :], ps[:, 2 * (n % 2), :], ACT.Silu).then_inc(silu_ready, 1)
                    if n:
                        magnitude(n - 1)
            cw = lambda k, tap: cols[:, COLS["conv_w"][0] + k * TAPS + tap:COLS["conv_w"][0] + k * TAPS + tap + 1]
            cc = lambda name, k: cols[:, COLS[name][0] + k:COLS[name][0] + k + 1]

            def take_x(h, ks):
                t = slice(h * TH, (h + 1) * TH)
                for k in ks:
                    act.wait_ge(inx_ready, h * 2 * KI + k + 1)
                    nc.scalar.activation(xa[:, k, t], ps[:, k, :], ACT.Identity, bias=cc("conv_b", k), scale=cw(k, TAPS - 1))
                    nc.scalar.activation(x_in[:, k, TAPS - 1 + h * TH:TAPS - 1 + (h + 1) * TH], ps[:, k, :],
                                         ACT.Copy).then_inc(xin_ready, 1)

            def act_z(h):
                t = slice(h * TH, (h + 1) * TH)
                for k in range(KI):
                    act.wait_ge(inx_ready, h * 2 * KI + KI + k + 1)
                    nc.scalar.activation(sz[:, k, t], ps[:, k, :], ACT.Silu).then_inc(z_ready, 1)

            def act_x(h):
                t = slice(h * TH, (h + 1) * TH)
                for k in range(KI):
                    act.wait_ge(conv_done, h * KI + k + 1)
                    nc.scalar.activation(xa[:, k, t], xa[:, k, t], ACT.Silu).then_inc(xa_ready, 1)

            def softplus_exp(h, k, bank, e):
                act.wait_ge(dtp_ready, h * KI + k + 1)
                nc.scalar.activation(e, ps[:, bank, :], ACT.Abs, bias=cc("dt_b", k)).then_inc(act_own, 1)
                nc.scalar.activation(dt_[:, k, h * TH:(h + 1) * TH], ps[:, bank, :], ACT.Relu,
                                     bias=cc("dt_b", k)).then_inc(dt_positive, 1)
                act.wait_ge(act_own, h * KI + k + 1)
                nc.scalar.activation(e, e, ACT.Exp, scale=-1.0).then_inc(sp_exp, 1)

            def softplus_ln(h, l, w):
                for k in range(KI):
                    act.wait_ge(sp_w_ready, h * KI + k + 1)
                    if h:
                        act.wait_ge(sp_d_used, k + 1)
                    nc.scalar.activation(l[:, k, :], w[:, k, :], ACT.Ln).then_inc(sp_ln, 1)

            def copy_b(i):
                act.wait_ge(b_ready, i + 1)
                if i >= 2:
                    act.wait_ge(dBx_ready, i - 1)
                nc.scalar.activation(b_sb[:, i % 2, :], ps[:, 0, :], ACT.Copy).then_inc(b_copied, 1)

            act.wait_ge(zero_ready, 1)
            features(1, 0)
            take_x(0, range(2))
            magnitude(NH * FB - 1)
            take_x(0, range(2, KI))
            act_z(0)
            act_x(0)
            features(1, 1)
            for k in range(KI):
                softplus_exp(0, k, k, sp_e[:, k, :])
            nc.scalar.activation(a_neg[:, :, :], cols[:, COLS["a_log"][0]:COLS["a_log"][1]].rearrange("p (k n) -> p k n", k=KI),
                                 ACT.Exp).then_inc(a_exp, 1)
            take_x(1, range(2))
            softplus_ln(0, sp_l, sp_w)
            take_x(1, range(2, KI))
            act_z(1)
            copy_b(0)
            copy_b(1)
            act_x(1)
            act.wait_ge(a_ready, 1)

            for i in range(NH * NS):
                h, n = divmod(i, NS)
                if 1 < i + 1 < NH * NS:
                    copy_b(i + 1)
                if i >= 2:
                    act.wait_ge(scanned, KI * (i - 1))
                if n == 0:
                    act.wait_ge(dt_done, (h + 1) * KI)
                for k in range(KI):
                    nc.scalar.activation(dA[:, i % 2, k, :], dt_[:, k, h * TH:(h + 1) * TH], ACT.Exp,
                                         scale=a_neg[:, k, n:n + 1]).then_inc(dA_ready, 1)
                if 0 <= i - 4 < KI:
                    k = i - 4
                    if k == 0:
                        act.wait_ge(bc_ready, NH)
                    elif k >= 2:
                        act.wait_ge(sp_d_used, k - 1)
                    softplus_exp(1, k, 3, late_e[k % 2])
                if i == 9:
                    softplus_ln(1, late_w, late_w)
            for h in range(NH):
                features(2, h)
            act.wait_ge(r_sub, NH)
            nc.scalar.activation(r_p[:, :, :], r_p[:, :, :], ACT.Exp).then_inc(r_exp, 1)
            def shared_expert(first, end):
              for n in range(first, end + 1):
                if n < end:
                    act.wait_ge(egu_ready, n + 1)
                    if n >= 2:
                        act.wait_ge(eh_ready, n - 1)
                    nc.scalar.activation(e_s[:, n % 2, :], ps[:, n % 2, 0:EI], ACT.Silu).then_inc(es_ready, 1)
                if n > first:
                    act.wait_ge(eT_ready, n)
                    if n >= 3:
                        act.wait_ge(edn_ready, n - 2)
                    nc.scalar.activation(e_f[0:EH, (n - 1) % 2, :, :], ps[0:EH, 2 + (n - 1) % 2, 0:2 * P].rearrange("p (c t) -> p c t", c=2),
                                         ACT.Copy).then_inc(ef_ready, 1)

            shared_expert(0, SHARED * EARLY)

            def slot_tile(n, turn, b):
                if has_tile(n):
                    act.wait_ge(slot_xT_ready, n + 1)
                    if counts(n - 1):
                        act.wait_ge(slot_gu_ready, n - 1)
                    nc.scalar.activation(slot_xf[:, b % 2, :, :], ps[:, 6 + b % 2, 0:D].rearrange("p (k t) -> p k t", k=KD),
                                         ACT.Copy).then_inc(slot_xf_ready, 1)
                if has_tile(n - 1):
                    act.wait_ge(slot_gu_ready, n)
                    if counts(n - 2):
                        act.wait_ge(slot_h_ready, n - 2)
                    nc.scalar.activation(e_s[:, (b + 1) % 2, :], ps[:, (b + 1) % 2, 0:EI], ACT.Silu).then_inc(slot_silu_ready, 1)
                if has_tile(n - 2):
                    act.wait_ge(slot_hT_ready, n - 1)
                    if counts(n - 3):
                        act.wait_ge(slot_down_ready, n - 3)
                    nc.scalar.activation(e_f[0:EH, b % 2, :, :], ps[0:EH, 2 + b % 2, 0:2 * P].rearrange("p (c t) -> p c t", c=2),
                                         ACT.Copy).then_inc(slot_hf_ready, 1)

            act.wait_ge(y_acc, NH * NS)
            act.wait_ge(ym_ready, NH * KI)
            act.wait_ge(eh_ready, SHARED * EARLY)
            act.wait_ge(edn_ready, SHARED * EARLY)
            in_steps(act, slot_tile, SLOTS + 2)
            act.wait_ge(slot_h_ready, SLOTS)
            act.wait_ge(slot_down_ready, SLOTS)
            shared_expert(SHARED * EARLY, SHARED * NT)

        @block.vector
        def _(dve):
            done = [0]

            def link(ins):
                done[0] += 1
                ins.then_inc(vec_own, 1)
                dve.wait_ge(vec_own, done[0])

            dve.wait_ge(ld_small, 4 * DMA)
            nc.vector.tensor_scalar(b_q4[:, :], cols[:, 0:KD], HD ** -0.5, None, ALU.mult).then_inc(bias_ready, 1)
            for i, (m, h) in enumerate(QK_ORDER):
                t = slice(h * TH, (h + 1) * TH)
                dve.wait_ge(qk_taken, i + 1)
                link(nc.vector.tensor_tensor(qk_full[:, i, :], qk_full[:, i, :], qk_part[:, 0, m, t], ALU.subtract))
                link(nc.vector.tensor_copy(qk_part[:, 1, m, t], qk_full[:, i, :]))
                nc.vector.tensor_tensor(qk_part[:, 2, m, t], qk_full[:, i, :], qk_part[:, 1, m, t],
                                        ALU.subtract).then_inc(parts_ready, 1)
            for tt in range(NT):
                dve.wait_ge(v_ready, tt + 1)
                nc.vector.tensor_tensor(v_aug[:, tt, :, 0:HD], ps[:, tt, 0:D].rearrange("p (h d) -> p h d", h=HEADS),
                                        bias_vo[:, 0, :].rearrange("p (h d) -> p h d", h=HEADS),
                                        ALU.add).then_inc(v_taken, 1)
            taken = [0, 0]
            for n, entry in enumerate(MAX):
                phase = entry[0]
                h, g = PHASES[phase]
                if len(entry) == 1:
                    dve.wait_ge(nmaxT_ready, phase + 1)
                    if phase >= 2:
                        dve.wait_ge(nmax_loaded[phase - 2], SPLIT * DMA)
                    nc.vector.tensor_copy(nmax_f[0:SPLIT * G, phase % 2, :], psb[0:SPLIT * G, n % RB, 0:TH]).then_inc(nmax_feat, 1)
                    continue
                _, tt, half, w, js = entry
                taken[0] += 1
                dve.wait_ge(max_ready, taken[0])
                nc.vector.tensor_reduce(nmax[:, half, tt, js[0]:js[-1] + 1],
                                        ps[:, n % RB, 0:w * len(js)].rearrange("p (j t) -> p j t", t=w), AX.X, ALU.max,
                                        negate=True).then_inc(max_taken, 1)
                if taken[0] == sum(len(max_jobs(q)) for q in range(phase + 1)):
                    dve.wait_ge(max_taken, taken[0])
                    tts = slice(h * TPH, (h + 1) * TPH)
                    if h:
                        link(nc.vector.tensor_tensor(nmax[:, 0, tts, :], nmax[:, 0, tts, :], nmax[:, 1, tts, :], ALU.min))
                    if phase >= 2:
                        dve.wait_ge(nmaxT_ready, phase - 1)
                    parts = nmax_p[:, phase % 2, :, :, :]
                    link(nc.vector.tensor_copy(parts[:, :, 0, :], nmax[:, 0, tts, :]))
                    link(nc.vector.tensor_tensor(nmax_r[:, :, :], nmax[:, 0, tts, :], parts[:, :, 0, :], ALU.subtract))
                    link(nc.vector.tensor_copy(parts[:, :, 1, :], nmax_r[:, :, :]))
                    nc.vector.tensor_tensor(parts[:, :, 2, :], nmax_r[:, :, :], parts[:, :, 1, :],
                                            ALU.subtract).then_inc(nmax_parts, 1)
                    dve.wait_ge(nmax_parts, phase + 1)

            def tile_statistics(layer, tt):
                dve.wait_ge(y_ready, layer * NT + tt + 1)
                nc.vector.bn_stats(stats[:, tt, :], y_tok[:, tt, :]).then_inc(tile_stats, 1)

            def add_residual(source, layer, tt):
                nc.vector.tensor_tensor(y_tok[:, tt, :], source, x_tok[:, tt, :], ALU.add).then_inc(y_ready, 1)
                tile_statistics(layer, tt)

            def statistics(layer, h):
                dve.wait_ge(tile_stats, layer * NT + (h + 1) * TPH)
                for tt in range(h * TPH, (h + 1) * TPH):
                    last = nc.vector.bn_aggr(mv[:, tt, :], stats[:, tt, :])
                link(last)
                nc.vector.tensor_scalar(mv[:, h * TPH:(h + 1) * TPH, 1], mv[:, h * TPH:(h + 1) * TPH, 1], EPS, None,
                                        ALU.add).then_inc(stats_ready, 1)

            def normalise(layer, h):
                dve.wait_ge(rstd_ready, layer * NH + h + 1)
                for tt in range(h * TPH, (h + 1) * TPH):
                    nc.vector.tensor_scalar(x_tok[:, tt, :], y_tok[:, tt, :], mv[:, tt, 0:1], rstd[:, tt:tt + 1],
                                            ALU.subtract, ALU.mult).then_inc(norm_ready, 1)

            dve.wait_ge(xb_ready, 1)

            def divide(tt):
                heads = ps[:, 4 * (tt // TPH), :].rearrange("p (h c) -> p h c", h=HEADS)
                dve.wait_ge(oT_ready, tt + 1)
                link(nc.vector.reciprocal(rden[:, tt % 2, :], heads[:, :, HD]))
                if tt >= 2:
                    dve.wait_ge(oN_ready, tt - 1)
                nc.vector.tensor_tensor(o_tok[:, tt % 2, :].rearrange("p (h c) -> p h c", h=HEADS), heads[:, :, 0:HD],
                                        rden[:, tt % 2, :].unsqueeze(2).broadcast_to([P, HEADS, HD]), ALU.mult).then_inc(o_norm, 1)

            def take_back(tt):
                dve.wait_ge(oN_ready, tt + 1)
                if tt >= 2:
                    dve.wait_ge(wo_ready, tt - 1)
                nc.vector.tensor_copy(o_nf[:, tt % 2, :, :], ps[:, 4 * (tt // TPH) + 1, 0:D].rearrange("p (k t) -> p k t", k=KD)).then_inc(onf_ready, 1)

            def wo_residual(tt):
                dve.wait_ge(wo_ready, tt + 1)
                add_residual(ps[:, 4 * (tt // TPH) + 2, 0:D], 0, tt)

            def o_step(h, step):
                for stage, i in zip((divide, take_back, wo_residual), o_stages(step)):
                    if i is not None:
                        stage(h * TPH + i)

            for step in range(TPH + 2):
                o_step(0, step)
            statistics(0, 0)
            normalise(0, 0)
            dve.wait_ge(xT_ready, 1)
            nc.vector.tensor_copy(x_feat[:, :, 0:TH], ps[:, 0:2, :]).then_inc(feat_ready, 1)

            def keep_two(q):
                hb, ab = ff_h[:, q % 2, :, :], ff_a[:, q % 2, :, :]
                dve.wait_ge(abs_ready, GS * (q + 1))
                nc.vector.tensor_tensor(ff_c[:, 0:3, :], ab[:, 0, :].unsqueeze(1).broadcast_to([P, 3, TH]), ab[:, 1:4, :], ALU.is_ge)
                nc.vector.tensor_tensor(ff_c[:, 3:5, :], ab[:, 1, :].unsqueeze(1).broadcast_to([P, 2, TH]), ab[:, 2:4, :], ALU.is_ge)
                link(nc.vector.tensor_tensor(ff_c[:, 5, :], ab[:, 2, :], ab[:, 3, :], ALU.is_ge))
                for j, (x, y) in enumerate(((0, 1), (3, 4), (1, 3), (2, 4))):
                    last = nc.vector.tensor_tensor(ff_w[:, j, :], ff_c[:, x, :], ff_c[:, y, :], ALU.add)
                link(last)
                nc.vector.tensor_tensor(ff_w[:, 0, :], ff_w[:, 0, :], ff_c[:, 2, :], ALU.add)
                nc.vector.tensor_tensor(ff_w[:, 1, :], ff_w[:, 1, :], ff_c[:, 0, :], ALU.subtract)
                nc.vector.tensor_tensor(ff_w[:, 2, :], ff_c[:, 5, :], ff_w[:, 2, :], ALU.subtract)
                link(nc.vector.tensor_tensor(ff_w[:, 3, :], ff_w[:, 3, :], ff_c[:, 5, :], ALU.add))
                h, gb = divmod(q, 2)
                for j, (bound, op) in enumerate(((1.5, ALU.is_ge), (0.5, ALU.is_ge), (-0.5, ALU.is_ge), (1.5, ALU.is_le))):
                    nc.vector.scalar_tensor_tensor(out=ff_k[:, gb * GS + j, h * TH:(h + 1) * TH], in0=ff_w[:, j, :], scalar=bound,
                                                   in1=hb[:, j, :], op0=op, op1=ALU.mult).then_inc(kept_ready, 1)

            def gated(n):
                dve.wait_ge(silu_ready, n + 1)
                if n >= 2 * GS:
                    dve.wait_ge(kept_ready, (n // GS - 1) * GS)
                nc.vector.tensor_tensor(ff_h[:, n // GS % 2, n % GS, :], ff_s[:, n % 2, :], ps[:, 2 * (n % 2) + 1, :],
                                        ALU.mult).then_inc(ffh_ready, 1)
                if n in (2 * GS - 1, 2 * GS + 2, 3 * GS + 2):
                    keep_two((n - 2) // GS - 1 if n > 2 * GS else 0)

            def down_residual(h):
                for tt in range(h * TPH, (h + 1) * TPH):
                    dve.wait_ge(down_ready, tt + 1)
                    add_residual(ps[:, 4 + tt % 2, 0:D], 1, tt)
                statistics(1, h)

            cw = lambda k, tap: cols[:, COLS["conv_w"][0] + k * TAPS + tap:COLS["conv_w"][0] + k * TAPS + tap + 1]
            cc = lambda name, k: cols[:, COLS[name][0] + k:COLS[name][0] + k + 1]

            def convolve(h):
                t = slice(h * TH, (h + 1) * TH)
                for k in range(KI):
                    dve.wait_ge(xin_ready, h * KI + k + 1)
                    for tap in range(TAPS - 1):
                        ins = nc.vector.scalar_tensor_tensor(out=xa[:, k, t], in0=x_in[:, k, h * TH + tap:h * TH + tap + TH],
                                                             scalar=cw(k, tap), in1=xa[:, k, t], op0=ALU.mult, op1=ALU.add)
                        if tap < TAPS - 2:
                            link(ins)
                    ins.then_inc(conv_done, 1)

            def split_bc(h):
                t = slice(h * TH, (h + 1) * TH)
                xd = ps[:, 4 - h, :]
                dve.wait_ge(xd_ready, h + 1)
                nc.vector.tensor_copy(dt_lo[3 * BC:XD, t], xd[3 * BC:XD, :]).then_inc(dt_ready, 1)
                link(nc.vector.tensor_copy(bc_p[0:3 * BC, 0, :], xd[0:3 * BC, :]))
                link(nc.vector.tensor_tensor(bc_r[0:3 * BC, :], xd[0:3 * BC, :], bc_p[0:3 * BC, 0, :], ALU.subtract))
                link(nc.vector.tensor_copy(bc_p[0:3 * BC, 1, :], bc_r[0:3 * BC, :]))
                link(nc.vector.tensor_tensor(bc3[0:3 * BC, t], bc_r[0:3 * BC, :], bc_p[0:3 * BC, 1, :], ALU.subtract))
                nc.vector.tensor_copy(bc3[0:BC, t], bc_p[0:BC, 0, :])
                last = nc.vector.tensor_copy(bc3[BC:2 * BC, t], bc_p[BC:2 * BC, 1, :])
                last.then_inc(bc_ready, 1)
                dve.wait_ge(bc_ready, h + 1)

            def softplus(h):
                t = slice(h * TH, (h + 1) * TH)
                for k in range(KI):
                    dve.wait_ge(sp_exp, h * KI + k + 1)
                    nc.vector.tensor_scalar(sp_w[:, k, :], sp_e[:, k, :], 1.0, None, ALU.add).then_inc(sp_w_ready, 1)
                for k in range(KI):
                    dve.wait_ge(sp_w_ready, h * KI + k + 1)
                    last = nc.vector.scalar_tensor_tensor(out=sp_e[:, k, :], in0=sp_w[:, k, :], scalar=-1.0, in1=sp_e[:, k, :],
                                                          op0=ALU.add, op1=ALU.subtract)
                link(last)
                for k in range(KI):
                    last = nc.vector.tensor_tensor(dt_[:, k, t], dt_[:, k, t], sp_e[:, k, :], ALU.subtract)
                link(last)
                for k in range(KI):
                    dve.wait_ge(sp_ln, h * KI + k + 1)
                    nc.vector.tensor_tensor(dt_[:, k, t], dt_[:, k, t], sp_l[:, k, :], ALU.add).then_inc(dt_done, 1)

            def late_softplus(k):
                t = slice(TH, T)
                dve.wait_ge(sp_exp, KI + k + 1)
                nc.vector.tensor_scalar(late_w[:, k, :], late_e[k % 2], 1.0, None, ALU.add).then_inc(sp_w_ready, 1)
                dve.wait_ge(sp_w_ready, KI + k + 1)
                link(nc.vector.scalar_tensor_tensor(out=late_e[k % 2], in0=late_w[:, k, :], scalar=-1.0, in1=late_e[k % 2],
                                                    op0=ALU.add, op1=ALU.subtract))
                nc.vector.tensor_tensor(dt_[:, k, t], dt_[:, k, t], late_e[k % 2], ALU.subtract).then_inc(sp_d_used, 1)

            def late_dt():
                for k in range(KI):
                    dve.wait_ge(sp_ln, KI + k + 1)
                    nc.vector.tensor_tensor(dt_[:, k, TH:T], dt_[:, k, TH:T], late_w[:, k, :], ALU.add).then_inc(dt_done, 1)

            for n in range(FB + AHEAD):
                if n < FB:
                    o_step(1, n)
                if n == TPH + 2:
                    statistics(0, 1)
                if n == TPH + 3:
                    normalise(0, 1)
                gated(n)
            down_residual(0)
            gated(FB + AHEAD)
            normalise(1, 0)
            for n in range(FB + AHEAD + 1, NH * FB):
                gated(n)
            keep_two(NH * FB // GS - 1)
            convolve(0)
            down_residual(1)
            normalise(1, 1)
            split_bc(0)
            softplus(0)
            convolve(1)
            dve.wait_ge(a_exp, 1)
            nc.vector.tensor_scalar(a_neg[:, :, :], a_neg[:, :, :], -1.0, None, ALU.mult).then_inc(a_ready, 1)
            def gate_y(h):
                t = slice(h * TH, (h + 1) * TH)
                dve.wait_ge(dBx_ready, (h + 1) * NS)
                for k in range(KI + 1):
                    if k < KI:
                        dve.wait_ge(y_acc, NH * NS + k if h else NS)
                        nc.vector.scalar_tensor_tensor(out=dtx[:, k, t], in0=xa[:, k, t], scalar=cc("skip", k),
                                                       in1=ps[:, 4 + k, :], op0=ALU.mult, op1=ALU.add).then_inc(y_part, 1)
                    if k:
                        dve.wait_ge(y_part, h * KI + k)
                        nc.vector.tensor_tensor(dtx[:, k - 1, t], dtx[:, k - 1, t], sz[:, k - 1, t], ALU.mult).then_inc(ym_ready, 1)

            for i in range(NH * NS):
                h, n = divmod(i, NS)
                dve.wait_ge(dBx_ready, i + 1)
                for k in range(KI):
                    dve.wait_ge(dA_ready, KI * i + k + 1)
                    nc.vector.tensor_tensor_scan(hs[:, i % 2, k, :], dA[:, i % 2, k, :], dBx[:, i % 2, k, :],
                                                 h_last[:, k, n:n + 1] if h else 0.0, ALU.mult, ALU.add).then_inc(scanned, 1)
                dve.wait_ge(scanned, KI * (i + 1))
                if h < NH - 1:
                    nc.vector.tensor_copy(h_last[:, :, n], hs[:, i % 2, :, TH - 1])
                dve.wait_ge(c_ready, i + 1)
                if i >= 2:
                    dve.wait_ge(y_acc, i - 1)
                if i < NH * NS - 1:
                    nc.vector.tensor_tensor(hc[:, i % 2, :, :], hs[:, i % 2, :, :],
                                            ps[:, 1 + i % 2, :].unsqueeze(1).broadcast_to([P, KI, TH]), ALU.mult).then_inc(cmul_done, 1)
                else:
                    for k in range(KI):
                        nc.vector.tensor_tensor(hc[:, i % 2, k, :], hs[:, i % 2, k, :], ps[:, 1 + i % 2, :], ALU.mult).then_inc(cmul_done, 1)
                if i == 1:
                    split_bc(1)
                if 0 <= i - 5 < KI:
                    late_softplus(i - 5)
                if i == 10:
                    dve.wait_ge(sp_d_used, KI)
                    late_dt()
                if i == NS:
                    gate_y(0)
                if i >= NS + 1 and i < NS + 1 + TPH:
                    tt = i - NS - 1
                    dve.wait_ge(mout_ready, tt + 1)
                    add_residual(ps[:, out_bank(tt), 0:D], 2, tt)
                if i == NS + 5:
                    statistics(2, 0)
                if i == NS + 8:
                    normalise(2, 0)
            gate_y(NH - 1)
            for tt in range(TPH, NT):
                dve.wait_ge(mout_ready, tt + 1)
                add_residual(ps[:, out_bank(tt), 0:D], 2, tt)
            statistics(2, 1)
            normalise(2, 1)

            wide = lambda x: x.broadcast_to([P, NT, E])

            def subtract_maximum(h):
                tts = slice(h * TPH, (h + 1) * TPH)
                logits = ps[:, 5 + h, 0:NT * E].rearrange("p (t e) -> p t e", t=NT)[:, tts, :]
                dve.wait_ge(logit_ready, h + 1)
                link(nc.vector.tensor_reduce(r_max[:, tts], logits, AX.X, ALU.max))
                nc.vector.tensor_tensor(r_p[:, tts, :], logits, r_max[:, tts].unsqueeze(2).broadcast_to([P, TPH, E]),
                                        ALU.subtract).then_inc(r_sub, 1)

            def choose():
                dve.wait_ge(r_exp, 1)
                link(nc.vector.tensor_reduce(r_max[:, :], r_p[:, :, :], AX.X, ALU.add))
                link(nc.vector.reciprocal(r_max[:, :], r_max[:, :]))
                link(nc.vector.tensor_tensor(r_p[:, :, :], r_p[:, :, :], wide(r_max[:, :].unsqueeze(2)), ALU.mult))
                for tt in range(NT):
                    last = nc.vector.max(r_8[:, tt, :], r_p[:, tt, :])
                link(last)
                for tt in range(NT):
                    last = nc.vector.max_index(r_i[:, tt, :].bitcast(U32), r_8[:, tt, :], r_p[:, tt, :])
                link(last)
                link(nc.vector.tensor_copy(r_if[:, :, :], r_i[:, :, :].bitcast(U32)))
                dve.wait_ge(ld_router, 2 * DMA)
                experts = iota_e.unsqueeze(1).broadcast_to([P, NT, E])
                nc.vector.tensor_tensor(chosen[:, 0, :, :], experts, wide(r_if[:, :, 0:1]), ALU.is_equal)
                link(nc.vector.tensor_tensor(chosen[:, 1, :, :], experts, wide(r_if[:, :, 1:2]), ALU.is_equal))
                nc.vector.tensor_tensor(chosen_any.rearrange("p (t e) -> p t e", t=NT), chosen[:, 0, :, :], chosen[:, 1, :, :],
                                        ALU.add).then_inc(choice_ready, 1)

            def count_tokens():
                dve.wait_ge(rank_ready, 1)
                dve.wait_ge(zero_ready, 2)
                link(nc.vector.tensor_copy(per_tile.rearrange("p (e t) -> p e t", e=E),
                                           ps[:, 6, P:2 * P].rearrange("p (t e) -> p e t", t=NT)))
                link(nc.vector.tensor_tensor_scan(upto, ones_r, per_tile, 0.0, ALU.mult, ALU.add))
                link(nc.vector.tensor_tensor(before[:, :, :].rearrange("p e t -> p (e t)"), upto, per_tile, ALU.subtract))
                link(nc.vector.tensor_tensor(count, upto.rearrange("p (e t) -> p e t", e=E)[:, :, NT - 1], before[:, :, 0], ALU.subtract))
                link(nc.vector.tensor_tensor(per_tile.rearrange("p (e t) -> p e t", e=E), count.unsqueeze(2).broadcast_to([P, E, NT]),
                                             fill_steps.unsqueeze(1).broadcast_to([P, E, NT]), ALU.is_gt))
                link(nc.vector.tensor_reduce(tiles_of, per_tile.rearrange("p (e t) -> p e t", e=E), AX.X, ALU.add))

            def place_experts():
                link(nc.vector.tensor_tensor_scan(end_tile, ones_r[:, 0:E], tiles_of, 0.0, ALU.mult, ALU.add))
                link(nc.vector.tensor_tensor(base, end_tile, tiles_of, ALU.subtract))
                link(nc.vector.scalar_tensor_tensor(out=base, in0=base, scalar=float(P), in1=before[:, :, 0],
                                                    op0=ALU.mult, op1=ALU.subtract))
                link(nc.vector.tensor_tensor(before[:, :, :], before[:, :, :], base.unsqueeze(2).broadcast_to([P, E, NT]), ALU.add))
                link(nc.vector.tensor_tensor(place[:, :, :], before[:, :, :].rearrange("p e t -> p t e"),
                                             ps[:, 6, 2 * P:3 * P].rearrange("p (t e) -> p t e", t=NT), ALU.add))

            def place_tokens():
                link(nc.vector.tensor_tensor(r_q[:, :, :, :], chosen[:, :, :, :],
                                             place[:, :, :].unsqueeze(1).broadcast_to([P, TOP, NT, E]), ALU.mult))
                link(nc.vector.tensor_reduce(position_f[:, :, :], r_q[:, :, :, :], AX.X, ALU.add))
                nc.vector.tensor_copy(position[:, :, :], position_f[:, :, :]).then_inc(position_ready, 1)

            def name_experts():
                ended = picked_flat[0:1, 0:SLOTS * E].rearrange("p (s e) -> p s e", s=SLOTS)
                link(nc.vector.tensor_tensor(ended, iota_slot[0:1, :].unsqueeze(2).broadcast_to([1, SLOTS, E]),
                                             end_tile[0:1, :].unsqueeze(1).broadcast_to([1, SLOTS, E]), ALU.is_ge))
                link(nc.vector.tensor_reduce(slot_f[0:1, :], ended, AX.X, ALU.add))
                nc.vector.tensor_scalar(slot_expert[0:1, :], slot_f[0:1, :], float(E - 1), None, ALU.min).then_inc(slot_expert_ready, 1)

            routing = {0: choose, 1: count_tokens, 2: place_experts, 3: place_tokens, 4: name_experts}
            for h in range(NH):
                subtract_maximum(h)
            def shared_expert(first, end):
              for n in range(first, end + 3):
                if n < end:
                    dve.wait_ge(es_ready, n + 1)
                    if n >= 2:
                        dve.wait_ge(eT_ready, n - 1)
                    nc.vector.tensor_tensor(e_h[:, n % 2, :], e_s[:, n % 2, :], ps[:, n % 2, EI:2 * EI], ALU.mult).then_inc(eh_ready, 1)
                if n >= first + 4 and n % SHARED == 0:
                    tt = n // SHARED - 2
                    dve.wait_ge(edn_ready, (tt + 1) * SHARED)
                    nc.vector.tensor_tensor(y_tok[:, tt, :], ps[:, 4 + tt % 2, 0:D], x_tok[:, tt, :], ALU.add).then_inc(shared_added, 1)
                if n in routing:
                    routing[n]()

            shared_expert(0, SHARED * EARLY)

            def slot_tile(n, turn, b):
                if has_tile(n - 1):
                    dve.wait_ge(slot_silu_ready, n)
                    if counts(n - 2):
                        dve.wait_ge(slot_hT_ready, n - 2)
                    nc.vector.tensor_tensor(e_h[:, (b + 1) % 2, :], e_s[:, (b + 1) % 2, :], ps[:, (b + 1) % 2, EI:2 * EI],
                                            ALU.mult).then_inc(slot_h_ready, 1)
                if has_tile(n - 3):
                    dve.wait_ge(slot_down_ready, n - 2)
                    if counts(n - 3 - RING + 1):
                        dve.wait_ge(slot_stored[(b + 1) % RING], stores(turn, b))
                    nc.vector.tensor_copy(slot_y[:, (b + 1) % RING, :], ps[:, 4 + (b + 1) % 2, 0:D]).then_inc(slot_y_ready, 1)

            def stores(turn, b):
                return (turn - 1 + (b + 1) // RING) * DMA

            dve.wait_ge(eT_ready, SHARED * EARLY)
            in_steps(dve, slot_tile, SLOTS + 3)
            dve.wait_ge(slot_hT_ready, SLOTS)
            shared_expert(SHARED * EARLY, SHARED * NT)
            for h in range(NH):
                for tt in range(h * TPH, (h + 1) * TPH):
                    dve.wait_ge(picked_ready[tt], TOP * DMA)
                    dve.wait_ge(shared_added, NT)
                    link(nc.vector.scalar_tensor_tensor(out=y_tok[:, tt, :], in0=picked[:, 0, tt, :], scalar=r_8[:, tt, 0:1],
                                                        in1=y_tok[:, tt, :], op0=ALU.mult, op1=ALU.add))
                    nc.vector.scalar_tensor_tensor(out=y_tok[:, tt, :], in0=picked[:, 1, tt, :], scalar=r_8[:, tt, 1:2],
                                                   in1=y_tok[:, tt, :], op0=ALU.mult, op1=ALU.add).then_inc(y_ready, 1)
                    tile_statistics(3, tt)
                statistics(3, h)
            for h in range(NH):
                normalise(3, h)


def host_arrays(v):
    bits = lambda w: (w.astype(np.float32).view(np.uint32) >> 16).astype(np.uint16)
    f = lambda x: np.asarray(x)
    c = np.ascontiguousarray
    tiles = lambda w: c(w.reshape(-1, P, w.shape[1]).transpose(1, 0, 2))
    x = f(v["L0_attn_x"])[0]
    order = np.arange(D).reshape(KD, HPT, HD).transpose(0, 2, 1).ravel()
    order = np.concatenate([order, D + order, 2 * D + np.arange(D)])
    wqkv, bqkv = f(v["L0_attn_Wqkv"])[:, order], f(v["L0_attn_bqkv"])[order]
    key, query = np.arange(P)[:, None], np.arange(P)[None, :]
    cols = np.zeros((P, NCOLS), np.float32)
    put = lambda n, w: cols.__setitem__((slice(None), slice(*COLS[n])), w)
    put("b_qk", bqkv[:2 * D].reshape(4, P).T)
    colt = lambda w: w.reshape(KI, P, -1).transpose(1, 0, 2).reshape(P, -1)
    put("conv_w", colt(f(v["L1_attn_conv_w"])))
    put("conv_b", colt(f(v["L1_attn_conv_b"])))
    put("dt_b", colt(f(v["L1_attn_dt_proj_b"])))
    put("skip", colt(f(v["L1_attn_D"])))
    put("a_log", colt(f(v["L1_attn_A_log"])))
    bias_vo = np.broadcast_to(np.stack([bqkv[2 * D:], f(v["L0_attn_bo"])])[None], (P, 2, D))
    ffc = np.arange(FF).reshape(2, P, GS).transpose(0, 2, 1).ravel()
    blocks = lambda w: c(w[:, ffc].reshape(KD, P, FB, P).transpose(1, 0, 2, 3))
    xp = f(v["L1_attn_x_proj_w"]).T
    xp = np.concatenate([xp[:, RANK:]] * 3 + [xp[:, :RANK]], 1)
    pick = np.zeros((3, BC, BC, P), np.float32)
    pick[:, np.arange(BC), np.arange(BC)] = 1.0
    sgu, sdn = f(v["L1_ffn_shared_gate_up"]), f(v["L1_ffn_shared_down"])
    half = lambda w, s: w[:, s * EI:(s + 1) * EI]
    ws_gu = np.stack([np.concatenate([half(sgu, s), half(sgu, SHARED + s)], 1) for s in range(SHARED)])
    up = lambda w: c(w.reshape(-1, KD, P, 2 * EI).transpose(2, 0, 1, 3))
    down = lambda w: c(w.reshape(-1, 2, EH, D).transpose(2, 0, 1, 3))
    fills, place = np.arange(NT) * P, np.arange(SLOTS)
    return {
        "w_g": blocks(f(v["L0_ffn_w_gate"])), "w_u": blocks(f(v["L0_ffn_w_up"])), "w_d": tiles(f(v["L0_ffn_w_down"])[ffc]),
        "w_in": tiles(c(f(v["L1_attn_in_proj_w"]).T)), "w_xp": tiles(xp), "w_dt": c(f(v["L1_attn_dt_proj_w"]).T),
        "pick": bits(pick.reshape(3 * BC, BC, P)), "w_out": tiles(c(f(v["L1_attn_out_proj_w"]).T)),
        "w_r": tiles(c(f(v["L1_ffn_gate_w"]).T)), "iota": np.broadcast_to(np.concatenate([np.arange(E), fills, place]).astype(np.float32), (P, E + NT + SLOTS)).copy(),
        "w_gu": up(f(v["L1_ffn_w_gate_up"])), "w_dn": down(f(v["L1_ffn_w_down"])), "ws_gu": up(ws_gu), "ws_dn": down(sdn),
        "x_feat": tiles(c(x.T)), "x_tok": tiles(x), "w_qkv": tiles(wqkv), "cols": cols,
        "bias_vo": c(bias_vo), "w_o": tiles(f(v["L0_attn_Wo"])),
        "masks": bits(np.stack([np.eye(P), np.where(query < key, -30000.0, 0.0),
                                key < query, np.ones((P, P))], 1)),
        "ident": np.eye(P, dtype=np.float32),
    }


def launch_body(nc, args, out):
    scratch = nc.dram_tensor("scratch", [len(QK_ORDER), SPLIT, P, TH], mybir.dt.bfloat16).ap()
    slots = nc.dram_tensor("slots", [SLOTS, P, D], mybir.dt.float32).ap()
    results = nc.dram_tensor("results", [SLOTS, P, D], mybir.dt.float32).ap()
    build(nc, args, out.rearrange("a (t p) d -> p (a t) d", p=P), scratch, slots, results)


def kernel(**inputs):
    import concourse.bacc as _bacc
    from concourse import mybir as _mybir
    from concourse.bass_utils import run_bass_kernel_spmd as _run

    nc = _bacc.Bacc("TRN2", target_bir_lowering=False, num_devices=1)
    arrays, args = {}, {}
    for name, array in host_arrays(inputs).items():
        arrays["in_" + name] = array
        args[name] = nc.dram_tensor("in_" + name, array.shape, _mybir.dt.from_np(array.dtype), kind="ExternalInput").ap()
    out = nc.dram_tensor("out", (1, T, D), _mybir.dt.float32, kind="ExternalOutput").ap()
    launch_body(nc, args, out)
    r = _run(nc, [arrays], core_ids=[0])
    return r.results[0]["out"]
```
